# Optimizing a Trainium2 kernel written in Bass

```python
import numpy as np
import jax
import jax.numpy as jnp

def _softmax(x, axis=-1):
    return jax.nn.softmax(x, axis=axis)

def _gelu(x):
    return jax.nn.gelu(x, approximate=True)

def _silu(x):
    return jax.nn.silu(x)

def _sigmoid(x):
    return jax.nn.sigmoid(x)

def _layernorm(x, axis=-1, eps=1e-05):
    m = jnp.mean(x, axis=axis, keepdims=True)
    v = jnp.var(x, axis=axis, keepdims=True)
    return (x - m) / jnp.sqrt(v + eps)

def _scatter_add(tgt, idx, src, axis=0):
    return tgt.at[idx].add(src)

def _segment_sum(src, seg, n):
    return jax.ops.segment_sum(src, seg, n)
kernel_name = 'mk_sandwich_d2_jaxref_r8_0720e9'

def setup_inputs(seed: int=0):
    np.random.seed(seed)
    _w = jnp.asarray

    def _L0_attn_setup():
        import jax, jax.numpy as jnp
        import numpy as np
        D_MODEL = 256
        N_HEADS = 16
        D_K = 128
        EPS = 1e-05
        ROPE_BASE = 10000.0

        def rope(x):
            b, s, h, d = x.shape
            d2 = d // 2
            theta = 1.0 / ROPE_BASE ** (jnp.arange(0, d, 2, dtype=jnp.float32) / d)
            pos = jnp.arange(s, dtype=jnp.float32)
            freqs = pos[:, None] * theta[None, :]
            freqs = jnp.concatenate([freqs, freqs], axis=-1)
            cos = jnp.cos(freqs)[None, :, None, :]
            sin = jnp.sin(freqs)[None, :, None, :]
            x_rot = jnp.concatenate([-x[..., d2:], x[..., :d2]], axis=-1)
            return x * cos + x_rot * sin
        key = jax.random.key(seed)
        ks = jax.random.split(key, 10)
        hd = N_HEADS * D_K

        def xavier(k, shape):
            fan_in, fan_out = (shape[1], shape[0])
            lim = np.sqrt(6.0 / (fan_in + fan_out))
            return jax.random.uniform(k, shape, jnp.float32, -lim, lim)
        return {'h': jax.random.normal(ks[0], (2, 256, D_MODEL), jnp.float32), 'wq': xavier(ks[1], (hd, D_MODEL)), 'bq': jnp.zeros((hd,), jnp.float32), 'wk': xavier(ks[2], (hd, D_MODEL)), 'bk': jnp.zeros((hd,), jnp.float32), 'wv': xavier(ks[3], (hd, D_MODEL)), 'bv': jnp.zeros((hd,), jnp.float32), 'wo': xavier(ks[4], (D_MODEL, hd)), 'bo': jnp.zeros((D_MODEL,), jnp.float32), 'ln_g': jnp.ones((D_MODEL,), jnp.float32), 'ln_b': jnp.zeros((D_MODEL,), jnp.float32)}
    _L0_attn_in = _L0_attn_setup()

    def _L0_ffn_setup():
        import jax, jax.numpy as jnp
        import numpy as np
        BLOCK_SIZE = 32
        HIDDEN_SIZE = 256
        MLP_DIM = 2048
        NVFP4_LUT = jnp.array([0.0, 0.5, 1.0, 1.5, 2.0, 3.0, 4.0, 6.0, 0.0, -0.5, -1.0, -1.5, -2.0, -3.0, -4.0, -6.0], dtype=jnp.float32)

        def dequant_nvfp4(W_packed, scales, block=BLOCK_SIZE):
            N = W_packed.shape[0]
            low = W_packed & 15
            high = W_packed >> 4 & 15
            idx = jnp.stack([low, high], axis=-1).reshape(N, -1)
            vals = NVFP4_LUT[idx]
            K = vals.shape[1]
            vals = vals.reshape(N, K // block, block) * scales[:, :, None]
            return vals.reshape(N, K)
        key = jax.random.key(seed)
        ks = jax.random.split(key, 7)
        x = jax.random.normal(ks[0], (4, 32, HIDDEN_SIZE), dtype=jnp.float32)
        gate_W_packed = jax.random.randint(ks[1], (MLP_DIM, HIDDEN_SIZE // 2), 0, 32, dtype=jnp.int32)
        gate_scales = jax.random.uniform(ks[2], (MLP_DIM, HIDDEN_SIZE // BLOCK_SIZE), dtype=jnp.float32) * 0.1 + 0.001
        up_W_packed = jax.random.randint(ks[3], (MLP_DIM, HIDDEN_SIZE // 2), 0, 32, dtype=jnp.int32)
        up_scales = jax.random.uniform(ks[4], (MLP_DIM, HIDDEN_SIZE // BLOCK_SIZE), dtype=jnp.float32) * 0.1 + 0.001
        down_W_packed = jax.random.randint(ks[5], (HIDDEN_SIZE, MLP_DIM // 2), 0, 32, dtype=jnp.int32)
        down_scales = jax.random.uniform(ks[6], (HIDDEN_SIZE, MLP_DIM // BLOCK_SIZE), dtype=jnp.float32) * 0.1 + 0.001
        return {'x': x, 'gate_W_packed': gate_W_packed, 'gate_scales': gate_scales, 'up_W_packed': up_W_packed, 'up_scales': up_scales, 'down_W_packed': down_W_packed, 'down_scales': down_scales}
    _L0_ffn_in = _L0_ffn_setup()

    def _L1_attn_setup():
        import jax, jax.numpy as jnp
        import numpy as np
        B, L, D, H = (4, 512, 256, 16)
        HD = D // H
        EPS = 1e-09

        def phi(x):
            return jax.nn.elu(x) + 1.0
        key = jax.random.key(seed)
        k1, k2, k3 = jax.random.split(key, 3)
        x = jax.random.normal(k1, (B, L, D), dtype=jnp.float32)
        W_qkv = jax.random.normal(k2, (3 * D, D), dtype=jnp.float32) * D ** (-0.5)
        W_out = jax.random.normal(k3, (D, D), dtype=jnp.float32) * D ** (-0.5)
        return {'x': x, 'W_qkv': W_qkv, 'W_out': W_out}
    _L1_attn_in = _L1_attn_setup()

    def _L1_ffn_setup():
        import jax, jax.numpy as jnp
        import numpy as np
        HIDDEN = 256
        INTER = 688
        LUT_SIZE = 16

        def _ghost_linear(x, idx, lut):
            w = lut[idx]
            return jnp.einsum('bsh,oh->bso', x, w)
        key = jax.random.key(seed)
        k_x, k_lut, k_g, k_u, k_d = jax.random.split(key, 5)
        x = jax.random.normal(k_x, (2, 512, HIDDEN), dtype=jnp.float32)
        lut = jax.random.normal(k_lut, (LUT_SIZE,), dtype=jnp.float32) * 0.02
        gate_idx = jax.random.randint(k_g, (INTER, HIDDEN), 0, LUT_SIZE, dtype=jnp.int32)
        up_idx = jax.random.randint(k_u, (INTER, HIDDEN), 0, LUT_SIZE, dtype=jnp.int32)
        down_idx = jax.random.randint(k_d, (HIDDEN, INTER), 0, LUT_SIZE, dtype=jnp.int32)
        return {'x': x, 'lut': lut, 'gate_idx': gate_idx, 'up_idx': up_idx, 'down_idx': down_idx}
    _L1_ffn_in = _L1_ffn_setup()
    _d = {'L0_attn_h': _L0_attn_in['h'], 'L0_attn_wq': _L0_attn_in['wq'], 'L0_attn_bq': _L0_attn_in['bq'], 'L0_attn_wk': _L0_attn_in['wk'], 'L0_attn_bk': _L0_attn_in['bk'], 'L0_attn_wv': _L0_attn_in['wv'], 'L0_attn_bv': _L0_attn_in['bv'], 'L0_attn_wo': _L0_attn_in['wo'], 'L0_attn_bo': _L0_attn_in['bo'], 'L0_attn_ln_g': _L0_attn_in['ln_g'], 'L0_attn_ln_b': _L0_attn_in['ln_b'], 'L0_ffn_gate_W_packed': _L0_ffn_in['gate_W_packed'], 'L0_ffn_gate_scales': _L0_ffn_in['gate_scales'], 'L0_ffn_up_W_packed': _L0_ffn_in['up_W_packed'], 'L0_ffn_up_scales': _L0_ffn_in['up_scales'], 'L0_ffn_down_W_packed': _L0_ffn_in['down_W_packed'], 'L0_ffn_down_scales': _L0_ffn_in['down_scales'], 'L1_attn_W_qkv': _L1_attn_in['W_qkv'], 'L1_attn_W_out': _L1_attn_in['W_out'], 'L1_ffn_lut': _L1_ffn_in['lut'], 'L1_ffn_gate_idx': _L1_ffn_in['gate_idx'], 'L1_ffn_up_idx': _L1_ffn_in['up_idx'], 'L1_ffn_down_idx': _L1_ffn_in['down_idx']}
    _x0 = _d['L0_attn_h']
    _d['L0_attn_h'] = jax.random.normal(jax.random.fold_in(jax.random.key(seed), 1), (2, 512, 256), dtype=_x0.dtype)
    del _x0
    return _d

def reference(L0_attn_h, L0_attn_wq, L0_attn_bq, L0_attn_wk, L0_attn_bk, L0_attn_wv, L0_attn_bv, L0_attn_wo, L0_attn_bo, L0_attn_ln_g, L0_attn_ln_b, L0_ffn_gate_W_packed, L0_ffn_gate_scales, L0_ffn_up_W_packed, L0_ffn_up_scales, L0_ffn_down_W_packed, L0_ffn_down_scales, L1_attn_W_qkv, L1_attn_W_out, L1_ffn_lut, L1_ffn_gate_idx, L1_ffn_up_idx, L1_ffn_down_idx):

    def _L0_attn_ref(h, wq, bq, wk, bk, wv, bv, wo, bo, ln_g, ln_b):
        import jax, jax.numpy as jnp
        import numpy as np
        D_MODEL = 256
        N_HEADS = 16
        D_K = 128
        EPS = 1e-05
        ROPE_BASE = 10000.0

        def rope(x):
            b, s, h, d = x.shape
            d2 = d // 2
            theta = 1.0 / ROPE_BASE ** (jnp.arange(0, d, 2, dtype=jnp.float32) / d)
            pos = jnp.arange(s, dtype=jnp.float32)
            freqs = pos[:, None] * theta[None, :]
            freqs = jnp.concatenate([freqs, freqs], axis=-1)
            cos = jnp.cos(freqs)[None, :, None, :]
            sin = jnp.sin(freqs)[None, :, None, :]
            x_rot = jnp.concatenate([-x[..., d2:], x[..., :d2]], axis=-1)
            return x * cos + x_rot * sin
        residual = h
        mu = jnp.mean(h, axis=-1, keepdims=True)
        var = jnp.mean(jnp.square(h - mu), axis=-1, keepdims=True)
        x = (h - mu) * jax.lax.rsqrt(var + EPS) * ln_g + ln_b
        b, s, _ = x.shape
        q = (x @ wq.T + bq).reshape(b, s, N_HEADS, D_K)
        k = (x @ wk.T + bk).reshape(b, s, N_HEADS, D_K)
        v = (x @ wv.T + bv).reshape(b, s, N_HEADS, D_K)
        q = rope(q)
        k = rope(k)
        scale = 1.0 / np.sqrt(D_K)
        attn = jnp.einsum('bihd,bjhd->bhij', q, k) * scale
        causal = jnp.triu(jnp.ones((s, s), dtype=bool), k=1)
        attn = jnp.where(causal[None, None], -jnp.inf, attn)
        attn = jax.nn.softmax(attn, axis=-1)
        o = jnp.einsum('bhij,bjhd->bihd', attn, v).reshape(b, s, N_HEADS * D_K)
        return o @ wo.T + bo + residual

    def _L0_ffn_ref(x, gate_W_packed, gate_scales, up_W_packed, up_scales, down_W_packed, down_scales):
        import jax, jax.numpy as jnp
        import numpy as np
        BLOCK_SIZE = 32
        HIDDEN_SIZE = 256
        MLP_DIM = 2048
        NVFP4_LUT = jnp.array([0.0, 0.5, 1.0, 1.5, 2.0, 3.0, 4.0, 6.0, 0.0, -0.5, -1.0, -1.5, -2.0, -3.0, -4.0, -6.0], dtype=jnp.float32)

        def dequant_nvfp4(W_packed, scales, block=BLOCK_SIZE):
            N = W_packed.shape[0]
            low = W_packed & 15
            high = W_packed >> 4 & 15
            idx = jnp.stack([low, high], axis=-1).reshape(N, -1)
            vals = NVFP4_LUT[idx]
            K = vals.shape[1]
            vals = vals.reshape(N, K // block, block) * scales[:, :, None]
            return vals.reshape(N, K)
        B, S, H = x.shape
        xt = x.reshape(B * S, H)
        Wg = dequant_nvfp4(gate_W_packed, gate_scales)
        Wu = dequant_nvfp4(up_W_packed, up_scales)
        Wd = dequant_nvfp4(down_W_packed, down_scales)
        gate = jnp.einsum('th,nh->tn', xt, Wg)
        up = jnp.einsum('th,nh->tn', xt, Wu)
        gelu = jnp.tanh(0.7978845608028654 * (gate + 0.044715 * gate ** 3)) * gate * 0.5 + gate * 0.5
        inter = gelu * up
        out = jnp.einsum('tn,hn->th', inter, Wd)
        return out.reshape(B, S, H)

    def _L1_attn_ref(x, W_qkv, W_out):
        import jax, jax.numpy as jnp
        import numpy as np
        B, L, D, H = (4, 512, 256, 16)
        HD = D // H
        EPS = 1e-09

        def phi(x):
            return jax.nn.elu(x) + 1.0
        b, l, d = x.shape
        qkv = x @ W_qkv.T
        q, k, v = jnp.split(qkv, 3, axis=-1)
        q = q.reshape(b, l, H, HD).transpose(0, 2, 1, 3)
        k = k.reshape(b, l, H, HD).transpose(0, 2, 1, 3)
        v = v.reshape(b, l, H, HD).transpose(0, 2, 1, 3)
        q = phi(q)
        k = phi(k)
        kv_cumsum = jnp.cumsum(k * v, axis=2)
        k_cumsum = jnp.cumsum(k, axis=2)
        out = q * kv_cumsum / (q * k_cumsum + EPS)
        out = out.transpose(0, 2, 1, 3).reshape(b, l, d)
        return out @ W_out.T * HD ** (-0.5)

    def _L1_ffn_ref(x, lut, gate_idx, up_idx, down_idx):
        import jax, jax.numpy as jnp
        import numpy as np
        HIDDEN = 256
        INTER = 688
        LUT_SIZE = 16

        def _ghost_linear(x, idx, lut):
            w = lut[idx]
            return jnp.einsum('bsh,oh->bso', x, w)
        gate = _ghost_linear(x, gate_idx, lut)
        up = _ghost_linear(x, up_idx, lut)
        h = jax.nn.silu(gate) * up
        return _ghost_linear(h, down_idx, lut)
    x = L0_attn_h
    x = x + _layernorm(_L0_attn_ref(_layernorm(x, axis=-1), L0_attn_wq, L0_attn_bq, L0_attn_wk, L0_attn_bk, L0_attn_wv, L0_attn_bv, L0_attn_wo, L0_attn_bo, L0_attn_ln_g, L0_attn_ln_b), axis=-1)
    x = x + _layernorm(_L0_ffn_ref(_layernorm(x, axis=-1), L0_ffn_gate_W_packed, L0_ffn_gate_scales, L0_ffn_up_W_packed, L0_ffn_up_scales, L0_ffn_down_W_packed, L0_ffn_down_scales), axis=-1)
    x = x + _layernorm(_L1_attn_ref(_layernorm(x, axis=-1), L1_attn_W_qkv, L1_attn_W_out), axis=-1)
    x = x + _layernorm(_L1_ffn_ref(_layernorm(x, axis=-1), L1_ffn_lut, L1_ffn_gate_idx, L1_ffn_up_idx, L1_ffn_down_idx), axis=-1)
    return x

_drawn_inputs = setup_inputs


def setup_inputs(seed=0):
    import zlib

    import numpy as np

    out = dict(_drawn_inputs(seed))
    spreads = {'L0_attn_bq': (0.0, 0.8),
     'L0_attn_bk': (0.0, 0.8),
     'L0_attn_bv': (0.0, 0.1),
     'L0_attn_bo': (0.0, 0.1),
     'L0_attn_ln_g': (1.0, 0.6),
     'L0_attn_ln_b': (0.0, 0.1)}
    factors = {'L0_attn_wq': 4.982, 'L0_attn_wk': 4.585}
    for name, (base, spread) in spreads.items():
        noise = np.random.default_rng([zlib.crc32(name.encode()), seed]).standard_normal(out[name].shape)
        drawn = base * np.exp(spread * noise) if base else spread * noise
        out[name] = jnp.asarray(drawn.astype(out[name].dtype))
    for name, factor in factors.items():
        out[name] = (out[name] * factor).astype(out[name].dtype)
    return out
```

```python
from contextlib import ExitStack

import concourse.bass as bass
from concourse import mybir

ALU = mybir.AluOpType
ACT = mybir.ActivationFunctionType
AX_X = mybir.AxisListType.X
F32 = mybir.dt.float32
F16 = mybir.dt.float16
BF16 = mybir.dt.bfloat16
FP8 = mybir.dt.float8e4
I32 = mybir.dt.int32

P = 128
B, S, D = 2, 512, 256
TPB = S // P
KC = D // P
HEADS, DK = 16, 128
HD = HEADS * DK
LN_EPS = 1e-5
MASKED = -1e30

X_SCALE = 16.0
W_SCALE = 256.0
STAGES = 4
P_SCALE = 64.0
UNITS = B * HEADS
W_COLS = 1024
W_PIECES = 4 * 4096 // W_COLS + 2
MLP = 2048
M_TILES = MLP // P
NIBBLES = 2
Q_BLOCK = 32
Q_ROWS = Q_BLOCK // NIBBLES
Q_COLS = 512
Q_PIECES = 3 * MLP // Q_COLS
FP4_AS_FP8 = 64.0
DW = 1024
FT = D // P
ATT_SCALE = 16.0
CUM_EPS = 1e-9
OUT1_SCALE = (D // 16) ** -0.5
INTER = 688
I_TILES = -(-INTER // P)
LUT = 16
GU_COLS = KC * 2 * INTER
DOWN_COLS = I_TILES * D
GU_PIECES = 4
L_PIECES = GU_PIECES + 2


def sandwich(nc, x_in, wqT, wkT, wvT, woT, bqT, bkT, bvT, bo, gT, bT, ropes, w1T, packed, scales, codes, lut, out):
    with ExitStack() as ctx:
        def sb(name, shape, dt):
            return ctx.enter_context(nc.sbuf_tensor(name, shape, dt))

        def sem(name):
            return ctx.enter_context(nc.semaphore(name))

        bank = [ctx.enter_context(nc.psum_tensor(f"bank{i}", [P, 512], F32)) for i in range(8)]
        acc_bank, S_bank, T_bank, proj_bank, o_bank = bank[0:2], bank[2:4], bank[4:6], bank[6], bank[7]

        x = sb("x", [P, B * TPB, D], F32)
        xa = sb("xa", [P, B * TPB, D], F32)
        nrm = sb("nrm", [P, B * TPB, D], F32)
        y = sb("y", [P, TPB, D], F32)
        stats = sb("stats", [P, TPB, 6], F32)
        mv = sb("mv", [P, TPB, 2], F32)
        std = sb("std", [P, TPB], F32)
        rstd = sb("rstd", [P, TPB], F32)
        eps_ln = sb("eps_ln", [P, 1], F32)
        xTh = sb("xTh", [P, KC, B * S], F16)
        xTl = sb("xTl", [P, KC, B * S], F16)
        identf = sb("identf", [P, P], F32)
        identb = sb("identb", [P, P], BF16)
        maskb = sb("maskb", [P, P], BF16)
        zerob = sb("zerob", [P, 512], BF16)
        wh = [sb(f"w{n}h", [P, 4096], F16) for n in "qkvo"]
        wl = [sb(f"w{n}l", [P, 4096], F16) for n in "qkvo"]
        bias_q = sb("bias_q", [P, HEADS], F32)
        bias_k = sb("bias_k", [P, HEADS], F32)
        bias_v = sb("bias_v", [P, HEADS], F32)
        bo_row = sb("bo_row", [P, D], F32)
        ln_g = sb("ln_g", [P, KC], F32)
        ln_b = sb("ln_b", [P, KC], F32)
        rope = sb("rope", [P, 4, S], F32)
        w1h = sb("w1h", [P, KC, DW], F16)
        w1l = sb("w1l", [P, KC, DW], F16)
        raw = sb("raw", [P, 2, Q_COLS], I32)
        scl = sb("scl", [P, 2, Q_COLS], F32)
        bits = sb("bits", [P, 3, Q_COLS], I32)
        lut_row = sb("lut_row", [P, LUT], F32)
        w2dh = sb("w2dh", [P, DOWN_COLS], F16)
        w2dl = sb("w2dl", [P, DOWN_COLS], F16)
        qf = sb("qf", [P, 2, S], F32)
        xT = qf
        rc = sb("rc", [P, 2, S], F32)
        rs = sb("rs", [P, 2, S], F32)
        rr = sb("rr", [P, 2, S], F32)
        qkh = sb("qkh", [P, 2, 2, S], F16)
        qkl = sb("qkl", [P, 2, 2, S], F16)
        vh = sb("vh", [P, S], F16)
        vl = sb("vl", [P, S], F16)
        prob = sb("prob", [P, 2, TPB, S], F32)
        nmax = sb("nmax", [P, 2, TPB], F32)
        psum_row = sb("psum_row", [P, 2, TPB], F32)
        rinv = sb("rinv", [P, 2, TPB], F32)
        stage = prob[:, :, :, :].rearrange("p a t n -> p (a t n)").rearrange("p (i n) -> p i n", n=W_COLS)
        pTh = sb("pTh", [P, TPB, S], F16)
        pTl = sb("pTl", [P, TPB, S], F16)
        oh = sb("oh", [P, S], F16)
        ol = sb("ol", [P, S], F16)
        gel = qf
        inter = rc
        ih = [qkh[:, i, 0, :] for i in range(2)]
        il = [qkl[:, i, 0, :] for i in range(2)]
        G_bank, U_bank = S_bank, T_bank
        idx = [rope[:, 2 * i:2 * i + 2, :].rearrange("p f s -> p (f s)").bitcast(I32) for i in range(2)]
        hot = [prob[:, 0, 2 * i:2 * i + 2, :].rearrange("p t n -> p (t n)") for i in range(2)]
        val = prob[:, 1, 0:2, :].rearrange("p t n -> p (t n)")
        w32 = rr
        neg = qf
        expo = rc
        pos = rs
        phi = rr
        kv = prob[:, 0, 0, :]
        kv_sum = prob[:, 0, 1, :]
        k_sum = prob[:, 0, 2, :]
        num = prob[:, 0, 3, :]
        den = prob[:, 1, 0, :]
        att = prob[:, 1, 1, :]
        ones = prob[:, 1, 2, :]
        atth = [pTh[:, i, :] for i in range(FT)]
        attl = [pTl[:, i, :] for i in range(FT)]
        fh = [w[:, :].rearrange("p (c n) -> p c n", c=NIBBLES) for w in wh[0:3]]
        fl = [w[:, :].rearrange("p (c n) -> p c n", c=NIBBLES) for w in wl[0:3]]
        qkv_bank = [[bank[2], bank[3], bank[4]], [bank[5], bank[6], bank[7]]]

        s_x = [sem("s_x0"), sem("s_x1")]
        s_small = sem("s_small")
        s_w = [sem(f"s_w{i}") for i in range(4)]
        s_out = sem("s_out")
        s_raw = [sem("s_raw0"), sem("s_raw1")]
        s_idx = [sem("s_idx0"), sem("s_idx1")]
        s_lut = sem("s_lut")
        d_bits = sem("d_bits")
        d_w32 = sem("d_w32")
        a_fh = sem("a_fh")
        d_fl = sem("d_fl")
        d_hot = sem("d_hot")
        g_val = sem("g_val")
        a_w2h = sem("a_w2h")
        g_w2l = sem("g_w2l")
        t_gate = sem("t_gate")
        t_up = sem("t_up")
        t_down = sem("t_down")
        a_gelu = sem("a_gelu")
        d_inter = sem("d_inter")
        a_ih = sem("a_ih")
        g_il = sem("g_il")
        t_qkv = sem("t_qkv")
        d_neg = sem("d_neg")
        a_pos = sem("a_pos")
        a_expo = sem("a_expo")
        g_phi = sem("g_phi")
        d_kv = sem("d_kv")
        d_cum = sem("d_cum")
        g_num = sem("g_num")
        d_den = sem("d_den")
        d_att = sem("d_att")
        a_atth = sem("a_atth")
        g_attl = sem("g_attl")
        t_out1 = sem("t_out1")
        g_const = sem("g_const")
        g_ident = sem("g_ident")
        d_bn = sem("d_bn")
        d_var = sem("d_var")
        a_std = sem("a_std")
        d_rstd = sem("d_rstd")
        d_z = sem("d_z")
        d_nrm = sem("d_nrm")
        d_vec = sem("d_vec")
        g_res = sem("g_res")
        t_xT = sem("t_xT")
        d_xT = sem("d_xT")
        a_xTh = sem("a_xTh")
        d_xTl = sem("d_xTl")
        a_wh = sem("a_wh")
        d_wl = sem("d_wl")
        t_qk = sem("t_qk")
        t_v = sem("t_v")
        t_S = sem("t_S")
        t_T = sem("t_T")
        t_pv = sem("t_pv")
        t_op = sem("t_op")
        a_qk = sem("a_qk")
        a_exp = sem("a_exp")
        a_Th = sem("a_Th")
        a_qkh = sem("a_qkh")
        a_vh = sem("a_vh")
        a_oh = sem("a_oh")
        d_max = sem("d_max")
        d_sin = sem("d_sin")
        d_Tl = sem("d_Tl")
        d_vl = sem("d_vl")
        d_rinv = sem("d_rinv")
        d_ol = sem("d_ol")
        d_acc = sem("d_acc")
        d_y = sem("d_y")
        d_x = sem("d_x")
        d_prob = sem("d_prob")
        g_cos = sem("g_cos")
        g_rot = sem("g_rot")
        g_qkl = sem("g_qkl")

        x_tok = x_in.rearrange("b (t p) d -> p (b t) d", p=P)
        out_tok = out.rearrange("b (t p) d -> p (b t) d", p=P)
        w1_dram = w1T.rearrange("(c p) n -> p c n", p=P)
        w_dram = [w.rearrange("(c p) n -> p c n", p=P) for w in (wqT, wkT, wvT, woT)]

        def w_piece(j):
            return j * W_COLS // 4096, j * W_COLS % 4096

        def w_high(j):
            w, c0 = w_piece(j)
            return wh[w][:, c0:c0 + W_COLS] if w < 4 else w1h[:, c0 // DW, :]

        def w_low(j):
            w, c0 = w_piece(j)
            return wl[w][:, c0:c0 + W_COLS] if w < 4 else w1l[:, c0 // DW, :]

        def q_piece(j):
            c0 = j * Q_COLS % MLP
            return j * Q_COLS // MLP, slice(c0, c0 + Q_COLS)

        def l_piece(j):
            if j < GU_PIECES:
                n = GU_COLS // GU_PIECES
                return j * n, n, wh[3][:, j * n:(j + 1) * n], wl[3][:, j * n:(j + 1) * n]
            n = DOWN_COLS // (L_PIECES - GU_PIECES)
            c = (j - GU_PIECES) * n
            return GU_COLS + c, n, w2dh[:, c:c + n], w2dl[:, c:c + n]

        def i_rows(m):
            return min(P, INTER - m * P)

        def first(n):
            return isinstance(n, int) and n == 0

        block = ctx.enter_context(nc.Block())


        def pipeline(eng, step, finish_batch):
            def unit(n):
                return (n // HEADS, n % HEADS, n, n % 2) if 0 <= n < UNITS else None

            def around(n):
                return unit(n), unit(n + 1), unit(n - 1), unit(n - 2)

            step(*around(-1))
            for b in range(B):
                step(*around(b * HEADS))
                step(*around(b * HEADS + 1))
                if b:
                    finish_batch(b - 1)
                with eng.Fori(2, HEADS - 2, 2) as i:
                    for j in range(2):
                        step(*((b, i + k, i + (b * HEADS + k), k % 2) for k in (j, j + 1, j - 1, j - 2)))
                step(*around((b + 1) * HEADS - 2))
                step(*around((b + 1) * HEADS - 1))
            step(*around(UNITS))
            step(*around(UNITS + 1))
            finish_batch(B - 1)

        @block.sync
        def _(sp):
            for b in range(B):
                sp.dma_start(x[:, b * TPB:(b + 1) * TPB, :], x_tok[:, b * TPB:(b + 1) * TPB, :]).then_inc(s_x[b], 16)
            for dst, src in ((bias_q, bqT), (bias_k, bkT), (bias_v, bvT), (ln_g, gT), (ln_b, bT)):
                sp.dma_start(dst[:, :], src).then_inc(s_small, 16)
            sp.dma_start(bo_row[:, :], bo.partition_broadcast(P)).then_inc(s_small, 16)
            sp.dma_start(rope[:, :, :], ropes.rearrange("f p s -> p f s")).then_inc(s_small, 16)
            for j in range(W_PIECES):
                w, c0 = w_piece(j)
                if j >= 4:
                    sp.wait_ge(d_wl, j - 3)
                if w == 4:
                    src = w1_dram[:, c0 // DW, :]
                    dst = stage[:, j % 4, :]
                elif w < 3:
                    src = w_dram[w][:, c0 // HD, c0 % HD:c0 % HD + W_COLS]
                    dst = stage[:, j % 4, :]
                else:
                    src = w_dram[w][:, c0 // D:(c0 + W_COLS) // D, :]
                    dst = stage[:, j % 4, :].rearrange("p (h n) -> p h n", n=D)
                sp.dma_start(dst, src).then_inc(s_w[j % 4], 16)
            sp.dma_start(lut_row[:, :], lut.partition_broadcast(P)).then_inc(s_lut, 16)
            sp.wait_ge(t_op, UNITS)
            for j in range(L_PIECES):
                if j >= 2:
                    sp.wait_ge(d_hot, LUT * (j - 1))
                c0, n, _, _ = l_piece(j)
                sp.dma_start(idx[j % 2][:, 0:n], codes[:, c0:c0 + n]).then_inc(s_idx[j % 2], 16)
            for j in range(Q_PIECES):
                w, cols = q_piece(j)
                if j >= 2:
                    sp.wait_ge(d_w32, NIBBLES * (j - 1))
                sp.dma_start(raw[:, j % 2, :], packed[w, :, cols]).then_inc(s_raw[j % 2], 16)
                for g in range(P // Q_ROWS):
                    sp.dma_start(scl[g * Q_ROWS:(g + 1) * Q_ROWS, j % 2, :],
                                 scales[w, g, cols].partition_broadcast(Q_ROWS)).then_inc(s_raw[j % 2], 16)
            for b in range(B):
                sp.wait_ge(d_x, STAGES * B - B + b + 1)
                sp.dma_start(out_tok[:, b * TPB:(b + 1) * TPB, :], x[:, b * TPB:(b + 1) * TPB, :]).then_inc(s_out, 16)
            sp.wait_ge(s_out, 16 * B)

        @block.gpsimd
        def _(pool):
            pool.memset(identf[:, :], 0.0).then_inc(g_const, 1)
            pool.memset(identb[:, :], 0.0).then_inc(g_const, 1)
            pool.memset(maskb[:, :], 0.0).then_inc(g_const, 1)
            pool.memset(eps_ln[:, :], LN_EPS).then_inc(g_const, 1)
            pool.memset(zerob[:, :], 0.0).then_inc(g_const, 1)
            pool.wait_ge(g_const, 5)
            for m in (identf, identb):
                pool.affine_select(out=m[:, :], in_=m[:, :], compare_op=ALU.not_equal, fill=1.0, base=0,
                                   pattern=[[-1, P]], channel_multiplier=1).then_inc(g_ident, 1)
            pool.affine_select(out=maskb[:, :], in_=maskb[:, :], compare_op=ALU.is_ge, fill=MASKED, base=0,
                               pattern=[[-1, P]], channel_multiplier=1).then_inc(g_ident, 1)
            pool.wait_ge(s_small, 16 * 7)
            for b in range(B):
                pool.wait_ge(d_nrm, b + 1)
                for t in range(b * TPB, (b + 1) * TPB):
                    last = pool.tensor_tensor(xa[:, t, :], xa[:, t, :], bo_row[:, :], ALU.add)
                last.then_inc(g_res, 1)

            def step(cur, nxt, prev, prev2):
                if nxt:
                    b, h, u, p = nxt
                    for w in range(2):
                        pool.wait_ge(a_qk, 2 * u + (w + 1))
                        pool.tensor_tensor(rc[:, w, :], qf[:, w, :], rope[:, 2 * w, :], ALU.mult).then_inc(g_cos, 1)
                        pool.wait_ge(g_cos, 2 * u + (w + 1))
                        pool.wait_ge(d_sin, 2 * u + (w + 1))
                        pool.tensor_tensor(rr[:, w, :], rc[:, w, :], rs[:, w, :], ALU.add).then_inc(g_rot, 1)
                    for w in range(2):
                        pool.wait_ge(a_qkh, 2 * u + (w + 1))
                        pool.tensor_tensor(qkl[:, p, w, :], rr[:, w, :], qkh[:, p, w, :], ALU.subtract).then_inc(g_qkl, 1)

            pipeline(pool, step, lambda b: None)

            for j in range(L_PIECES):
                _, cols, w_h, w_l = l_piece(j)
                for e in range(LUT):
                    n = j * LUT + e
                    pool.wait_ge(d_hot, n + 1)
                    if e:
                        pool.wait_ge(g_val, n)
                        pool.tensor_tensor(val[:, 0:cols], val[:, 0:cols], hot[n % 2][:, 0:cols], ALU.add).then_inc(g_val, 1)
                    else:
                        if j:
                            pool.wait_ge(g_w2l, j)
                        pool.tensor_copy(val[:, 0:cols], hot[n % 2][:, 0:cols]).then_inc(g_val, 1)
                pool.wait_ge(a_w2h, j + 1)
                pool.tensor_tensor(w_l, val[:, 0:cols], w_h, ALU.subtract).then_inc(g_w2l, 1)

            if STAGES < 2:
                return

            def low_inter(n, rows=P):
                pool.wait_ge(a_ih, n + 1)
                pool.tensor_tensor(il[n % 2][0:rows, :], inter[0:rows, n % 2, :], ih[n % 2][0:rows, :],
                                   ALU.subtract).then_inc(g_il, 1)

            for n in range(B * M_TILES):
                low_inter(n)
            if STAGES < 3:
                return
            for b in range(B):
                for f in range(FT):
                    n = b * FT + f
                    for w in range(2):
                        pool.wait_ge(a_expo, 2 * n + w + 1)
                        pool.tensor_tensor(phi[:, w, :], pos[:, w, :], expo[:, w, :], ALU.add).then_inc(g_phi, 1)
                    pool.wait_ge(d_cum, 2 * n + 2)
                    pool.tensor_tensor(num, phi[:, 0, :], kv_sum, ALU.mult).then_inc(g_num, 1)
                    pool.wait_ge(a_atth, n + 1)
                    pool.tensor_tensor(attl[f], att, atth[f], ALU.subtract).then_inc(g_attl, 1)
            if STAGES < 4:
                return
            for b in range(B):
                for m in range(I_TILES):
                    low_inter(B * M_TILES + b * I_TILES + m, i_rows(m))

        @block.scalar
        def _(act):
            def std_of(event):
                act.wait_ge(d_var, event + 1)
                act.activation(std[:, :], mv[:, :, 1], ACT.Sqrt, bias=eps_ln[:, 0:1]).then_inc(a_std, 1)

            act.wait_ge(g_const, 5)
            for e in range(2 * B):
                std_of(e)
            for n in range(B * KC):
                b, c = n // KC, n % KC
                act.wait_ge(d_xT, n + 1)
                act.activation(xTh[:, c, b * S:(b + 1) * S], xT[:, n % 2, :], ACT.Copy).then_inc(a_xTh, 1)
            for j in range(W_PIECES):
                w, c0 = w_piece(j)
                act.wait_ge(s_w[j % 4], 16 * (j // 4 + 1))
                act.activation(w_high(j), stage[:, j % 4, :], ACT.Copy, scale=W_SCALE).then_inc(a_wh, 1)

            def step(cur, nxt, prev, prev2):
                def take(w):
                    b, h, u, p = nxt
                    act.wait_ge(t_qk, 2 * u + (w + 1))
                    if not first(u):
                        act.wait_ge(g_rot, 2 * u + (w - 1))
                    act.activation(qf[:, w, :], proj_bank[:, :], ACT.Identity, scale=1 / (X_SCALE * W_SCALE),
                                   bias=(bias_q, bias_k)[w][:, bass.ds(h, 1)]).then_inc(a_qk, 1)

                def exp(q):
                    b, h, u, p = cur
                    n = (q + 1) * P
                    act.wait_ge(d_max, 4 * u + (q + 1))
                    act.activation(prob[:, p, q, 0:n], S_bank[q % 2][:, 0:n], ACT.Exp, bias=nmax[:, p, q:q + 1],
                                   accum_out=psum_row[:, p, q:q + 1]).then_inc(a_exp, 1)

                def high_T(q):
                    b, h, u, p = prev
                    act.wait_ge(t_T, 4 * u + (q + 1))
                    act.activation(pTh[:, 0:q + 1, q * P:(q + 1) * P],
                                   T_bank[q % 2][:, 0:(q + 1) * P].rearrange("p (k n) -> p k n", n=P),
                                   ACT.Copy).then_inc(a_Th, 1)

                def high_qk(w):
                    b, h, u, p = nxt
                    act.wait_ge(g_rot, 2 * u + (w + 1))
                    act.activation(qkh[:, p, w, :], rr[:, w, :], ACT.Copy).then_inc(a_qkh, 1)

                if nxt:
                    take(0)
                if cur:
                    exp(0)
                    exp(1)
                if prev2:
                    b, h, u, p = prev2
                    act.wait_ge(t_pv, u + 1)
                    act.activation(oh[:, :], o_bank[:, :], ACT.Identity, bias=bias_v[:, bass.ds(h, 1)]).then_inc(a_oh, 1)
                if nxt:
                    take(1)
                if prev:
                    high_T(0)
                    high_T(1)
                if cur:
                    exp(2)
                if nxt:
                    high_qk(0)
                if prev:
                    high_T(2)
                if cur:
                    exp(3)
                if prev:
                    b, h, u, p = prev
                    act.wait_ge(t_v, u + 1)
                    act.activation(vh[:, :], proj_bank[:, :], ACT.Copy, scale=1 / (X_SCALE * W_SCALE)).then_inc(a_vh, 1)
                    high_T(3)
                if nxt:
                    high_qk(1)

            def finish_batch(b):
                std_of(2 * B + 2 * b)
                std_of(2 * B + 2 * b + 1)

            act.wait_ge(d_vec, 3)
            pipeline(act, step, finish_batch)

            for j in range(L_PIECES):
                _, cols, w_h, w_l = l_piece(j)
                act.wait_ge(g_val, LUT * (j + 1))
                act.activation(w_h, val[:, 0:cols], ACT.Copy).then_inc(a_w2h, 1)
            for j in range(Q_PIECES):
                w, cols = q_piece(j)
                for c in range(NIBBLES):
                    act.wait_ge(d_w32, NIBBLES * j + c + 1)
                    act.activation(fh[w][:, c, cols], w32[:, c, :], ACT.Copy, scale=W_SCALE * FP4_AS_FP8).then_inc(a_fh, 1)
            if STAGES < 2:
                return

            def high_xT(phase, b):
                for c in range(KC):
                    n = (phase * B + b) * KC + c
                    act.wait_ge(t_xT, n + 1)
                    act.activation(xTh[:, c, b * S:(b + 1) * S], T_bank[n % 2][:, :], ACT.Copy, scale=X_SCALE).then_inc(a_xTh, 1)

            def gated(n, func, rows=P):
                act.wait_ge(t_gate, n + 1)
                if n >= 2:
                    act.wait_ge(d_inter, n - 1)
                act.activation(gel[0:rows, n % 2, :], G_bank[n % 2][0:rows, :], func, scale=1 / (X_SCALE * W_SCALE)).then_inc(a_gelu, 1)

            def high_inter(n, rows=P):
                act.wait_ge(d_inter, n + 1)
                if n >= 2:
                    act.wait_ge(t_down, n - 1)
                act.activation(ih[n % 2][0:rows, :], inter[0:rows, n % 2, :], ACT.Copy).then_inc(a_ih, 1)

            for b in range(B):
                high_xT(1, b)
                for m in range(M_TILES):
                    gated(b * M_TILES + m, ACT.Gelu_apprx_tanh)
                    high_inter(b * M_TILES + m)
                std_of(4 * B + 2 * b)
                std_of(4 * B + 2 * b + 1)
            if STAGES < 3:
                return
            for b in range(B):
                high_xT(2, b)
                for f in range(FT):
                    n = b * FT + f
                    for w in range(2):
                        act.wait_ge(t_qkv, 3 * n + w + 1)
                        if n:
                            act.wait_ge(g_phi, 2 * (n - 1) + w + 1)
                        act.activation(pos[:, w, :], qkv_bank[n % 2][w][:, :], ACT.Relu, scale=1 / (X_SCALE * W_SCALE)).then_inc(a_pos, 1)
                        act.wait_ge(d_neg, 2 * n + w + 1)
                        act.activation(expo[:, w, :], neg[:, w, :], ACT.Exp, scale=1 / (X_SCALE * W_SCALE)).then_inc(a_expo, 1)
                    act.wait_ge(d_att, n + 1)
                    if b:
                        act.wait_ge(t_out1, b)
                    act.activation(atth[f], att, ACT.Copy).then_inc(a_atth, 1)
                std_of(6 * B + 2 * b)
                std_of(6 * B + 2 * b + 1)
            if STAGES < 4:
                return
            for b in range(B):
                high_xT(3, b)
                for m in range(I_TILES):
                    n = B * M_TILES + b * I_TILES + m
                    gated(n, ACT.Silu, i_rows(m))
                    high_inter(n, i_rows(m))
                std_of(8 * B + b)

        @block.vector
        def _(dve):
            def norm_of(event, src):
                for t in range(TPB):
                    last = dve.bn_stats(stats[:, t, :], src[:, t, :])
                last.then_inc(d_bn, 1)
                dve.wait_ge(d_bn, event + 1)
                for t in range(TPB):
                    last = dve.bn_aggr(mv[:, t, :], stats[:, t, :])
                last.then_inc(d_var, 1)
                dve.wait_ge(a_std, event + 1)
                dve.reciprocal(rstd[:, :], std[:, :]).then_inc(d_rstd, 1)
                dve.wait_ge(d_rstd, event + 1)

            def normalised(dst, src):
                for t in range(TPB):
                    last = dve.tensor_scalar(dst[:, t, :], src[:, t, :], mv[:, t, 0:1], rstd[:, t:t + 1],
                                             ALU.subtract, ALU.mult)
                return last

            for b in range(B):
                rows = slice(b * TPB, (b + 1) * TPB)
                dve.wait_ge(s_x[b], 16)
                norm_of(2 * b, x[:, rows, :])
                normalised(xa[:, rows, :], x[:, rows, :]).then_inc(d_z, 1)
                dve.wait_ge(d_z, b + 1)
                norm_of(2 * b + 1, xa[:, rows, :])
                normalised(nrm[:, rows, :], xa[:, rows, :]).then_inc(d_nrm, 1)
            dve.wait_ge(s_small, 16 * 7)
            for v, scale in ((ln_g, X_SCALE), (ln_b, X_SCALE), (bias_v, P_SCALE)):
                dve.tensor_scalar(v[:, :], v[:, :], scale, None, ALU.mult).then_inc(d_vec, 1)
            dve.wait_ge(d_vec, 3)
            for n in range(B * KC):
                b, c = n // KC, n % KC
                dve.wait_ge(t_xT, n + 1)
                dve.tensor_scalar(xT[:, n % 2, :], T_bank[n % 2][:, :], ln_g[:, c:c + 1], ln_b[:, c:c + 1],
                                  ALU.mult, ALU.add).then_inc(d_xT, 1)
                dve.wait_ge(a_xTh, n + 1)
                dve.wait_ge(d_xT, n + 1)
                h = xTh[:, c, b * S:(b + 1) * S]
                dve.tensor_tensor(xTl[:, c, b * S:(b + 1) * S], xT[:, n % 2, :], h, ALU.subtract).then_inc(d_xTl, 1)
            for j in range(W_PIECES):
                w, c0 = w_piece(j)
                dve.wait_ge(a_wh, j + 1)
                dve.scalar_tensor_tensor(out=w_low(j), in0=stage[:, j % 4, :], scalar=W_SCALE, in1=w_high(j),
                                         op0=ALU.mult, op1=ALU.subtract).then_inc(d_wl, 1)

            def step(cur, nxt, prev, prev2):
                def top(q):
                    b, h, u, p = cur
                    dve.wait_ge(t_S, 4 * u + (q + 1))
                    dve.tensor_reduce(nmax[:, p, q:q + 1], S_bank[q % 2][:, 0:(q + 1) * P], AX_X, ALU.max,
                                      negate=True).then_inc(d_max, 1)

                def rotate(w):
                    b, h, u, p = nxt
                    dve.wait_ge(a_qk, 2 * u + (w + 1))
                    if not first(u):
                        dve.wait_ge(g_rot, 2 * u + (w - 1))
                    half = DK // 2
                    dve.tensor_tensor(rs[0:half, w, :], qf[half:DK, w, :], rope[half:DK, 2 * w + 1, :], ALU.mult)
                    dve.tensor_tensor(rs[half:DK, w, :], qf[0:half, w, :], rope[0:half, 2 * w + 1, :],
                                      ALU.mult).then_inc(d_sin, 1)

                def low_T(q):
                    b, h, u, p = prev
                    dve.wait_ge(a_Th, 4 * u + (q + 1))
                    dve.tensor_tensor(pTl[:, 0:q + 1, q * P:(q + 1) * P],
                                      T_bank[q % 2][:, 0:(q + 1) * P].rearrange("p (k n) -> p k n", n=P),
                                      pTh[:, 0:q + 1, q * P:(q + 1) * P], ALU.subtract).then_inc(d_Tl, 1)

                if cur:
                    top(0)
                    top(1)
                if nxt:
                    rotate(0)
                if prev2:
                    b, h, u, p = prev2
                    dve.wait_ge(a_oh, u + 1)
                    dve.scalar_tensor_tensor(out=ol[:, :], in0=o_bank[:, :], scalar=bias_v[:, bass.ds(h, 1)],
                                             in1=oh[:, :], op0=ALU.add, op1=ALU.subtract).then_inc(d_ol, 1)
                if prev:
                    low_T(0)
                    low_T(1)
                if cur:
                    top(2)
                if nxt:
                    rotate(1)
                if prev:
                    low_T(2)
                if cur:
                    top(3)
                if prev:
                    b, h, u, p = prev
                    dve.wait_ge(a_vh, u + 1)
                    dve.scalar_tensor_tensor(out=vl[:, :], in0=proj_bank[:, :], scalar=1 / (X_SCALE * W_SCALE),
                                             in1=vh[:, :], op0=ALU.mult, op1=ALU.subtract).then_inc(d_vl, 1)
                    low_T(3)
                if cur:
                    b, h, u, p = cur
                    dve.wait_ge(a_exp, 4 * u + 4)
                    dve.reciprocal(rinv[:, p, :], psum_row[:, p, :]).then_inc(d_rinv, 1)
                    dve.wait_ge(d_rinv, u + 1)
                    for q in range(TPB):
                        row = prob[:, p, q, 0:(q + 1) * P]
                        dve.tensor_scalar(row, row, rinv[:, p, q:q + 1], P_SCALE, ALU.mult, ALU.mult).then_inc(d_prob, 1)

            def add_norm(phase, b, last_phase=False):
                rows = slice(b * TPB, (b + 1) * TPB)
                n = phase * B + b
                dve.wait_ge(d_acc, n + 1)
                norm_of(2 * B + 2 * n if not last_phase else 2 * B + 2 * phase * B + b, y[:, :, :])
                normalised(y[:, :, :], y[:, :, :]).then_inc(d_y, 1)
                dve.wait_ge(d_y, n + 1)
                for t in range(TPB):
                    last = dve.tensor_tensor(x[:, b * TPB + t, :], x[:, b * TPB + t, :], y[:, t, :], ALU.add)
                last.then_inc(d_x, 1)
                if not last_phase:
                    dve.wait_ge(d_x, n + 1)
                    norm_of(2 * B + 2 * n + 1, x[:, rows, :])
                    normalised(nrm[:, rows, :], x[:, rows, :]).then_inc(d_nrm, 1)

            def acc_tile(t):
                return acc_bank[t // 2][:, t % 2 * D:t % 2 * D + D]

            def finish_batch(b):
                dve.wait_ge(t_op, HEADS * (b + 1))
                dve.wait_ge(g_res, b + 1)
                for t in range(TPB):
                    last = dve.scalar_tensor_tensor(out=y[:, t, :], in0=acc_tile(t), scalar=1 / (P_SCALE * W_SCALE),
                                                    in1=xa[:, b * TPB + t, :], op0=ALU.mult, op1=ALU.add)
                last.then_inc(d_acc, 1)
                add_norm(0, b)

            pipeline(dve, step, finish_batch)

            dve.wait_ge(s_lut, 16)
            dve.tensor_scalar(lut_row[:, :], lut_row[:, :], W_SCALE, None, ALU.mult).then_inc(d_vec, 1)
            dve.wait_ge(d_vec, 4)
            for j in range(L_PIECES):
                _, cols, w_h, w_l = l_piece(j)
                dve.wait_ge(s_idx[j % 2], 16 * (j // 2 + 1))
                for e in range(LUT):
                    n = j * LUT + e
                    if n >= 2:
                        dve.wait_ge(g_val, n - 1)
                    dve.tensor_scalar(hot[n % 2][:, 0:cols], idx[j % 2][:, 0:cols], float(e), lut_row[:, e:e + 1],
                                      ALU.is_equal, ALU.mult).then_inc(d_hot, 1)
            for j in range(Q_PIECES):
                w, cols = q_piece(j)
                r = raw[:, j % 2, :]
                dve.wait_ge(s_raw[j % 2], 16 * (1 + P // Q_ROWS) * (j // 2 + 1))
                dve.tensor_scalar(bits[:, 0, :], r, 2, 0x1C, ALU.logical_shift_left, ALU.bitwise_and)
                dve.tensor_scalar(bits[:, 1, :], r, 2, 0x1C, ALU.logical_shift_right, ALU.bitwise_and)
                dve.tensor_scalar(bits[:, 2, :], r, 4, 0x80, ALU.logical_shift_left, ALU.bitwise_and).then_inc(d_bits, 1)
                dve.wait_ge(d_bits, 2 * j + 1)
                dve.tensor_tensor(bits[:, 0, :], bits[:, 0, :], bits[:, 2, :], ALU.bitwise_or)
                dve.scalar_tensor_tensor(out=bits[:, 1, :], in0=r, scalar=0x80, in1=bits[:, 1, :],
                                         op0=ALU.bitwise_and, op1=ALU.bitwise_or).then_inc(d_bits, 1)
                dve.wait_ge(d_bits, 2 * j + 2)
                for c in range(NIBBLES):
                    code = bits[:, c, :].bitcast(FP8).rearrange("p (n e) -> p n e", e=4)[:, :, 0]
                    dve.tensor_tensor(w32[:, c, :], code, scl[:, j % 2, :], ALU.mult).then_inc(d_w32, 1)
                for c in range(NIBBLES):
                    dve.wait_ge(a_fh, NIBBLES * j + c + 1)
                    dve.scalar_tensor_tensor(out=fl[w][:, c, cols], in0=w32[:, c, :], scalar=W_SCALE * FP4_AS_FP8,
                                             in1=fh[w][:, c, cols], op0=ALU.mult, op1=ALU.subtract).then_inc(d_fl, 1)
            if STAGES < 2:
                return

            def low_xT(phase, b):
                for c in range(KC):
                    n = (phase * B + b) * KC + c
                    dve.wait_ge(a_xTh, n + 1)
                    h = xTh[:, c, b * S:(b + 1) * S]
                    dve.scalar_tensor_tensor(out=xTl[:, c, b * S:(b + 1) * S], in0=T_bank[n % 2][:, :], scalar=X_SCALE,
                                             in1=h, op0=ALU.mult, op1=ALU.subtract).then_inc(d_xTl, 1)

            def product_of(n, rows=P):
                dve.wait_ge(a_gelu, n + 1)
                dve.wait_ge(t_up, n + 1)
                if n >= 2:
                    dve.wait_ge(g_il, n - 1)
                dve.scalar_tensor_tensor(out=inter[0:rows, n % 2, :], in0=U_bank[n % 2][0:rows, :],
                                         scalar=1 / (X_SCALE * W_SCALE), in1=gel[0:rows, n % 2, :],
                                         op0=ALU.mult, op1=ALU.mult).then_inc(d_inter, 1)

            def take_sums(scale):
                for t in range(TPB):
                    last = dve.tensor_scalar(y[:, t, :], acc_tile(t), scale, None, ALU.mult)
                last.then_inc(d_acc, 1)

            for b in range(B):
                low_xT(1, b)
                for m in range(M_TILES):
                    product_of(b * M_TILES + m)
                dve.wait_ge(t_down, M_TILES * (b + 1))
                take_sums(1 / W_SCALE)
                add_norm(1, b)
            if STAGES < 3:
                return
            dve.memset(ones, 1.0)
            for b in range(B):
                low_xT(2, b)
                for f in range(FT):
                    n = b * FT + f
                    q, k, v = qkv_bank[n % 2]
                    for w in range(2):
                        dve.wait_ge(a_pos, 2 * n + w + 1)
                        dve.tensor_scalar(neg[:, w, :], (q, k)[w][:, :], 0.0, None, ALU.min).then_inc(d_neg, 1)
                    dve.wait_ge(t_qkv, 3 * n + 3)
                    dve.wait_ge(g_phi, 2 * n + 2)
                    dve.scalar_tensor_tensor(out=kv, in0=v[:, :], scalar=ATT_SCALE / (X_SCALE * W_SCALE), in1=phi[:, 1, :],
                                             op0=ALU.mult, op1=ALU.mult).then_inc(d_kv, 1)
                    dve.wait_ge(d_kv, n + 1)
                    dve.tensor_tensor_scan(kv_sum, ones, kv, 0.0, ALU.mult, ALU.add).then_inc(d_cum, 1)
                    dve.tensor_tensor_scan(k_sum, ones, phi[:, 1, :], 0.0, ALU.mult, ALU.add).then_inc(d_cum, 1)
                    dve.wait_ge(d_cum, 2 * n + 2)
                    dve.tensor_tensor(den, phi[:, 0, :], k_sum, ALU.mult).then_inc(d_den, 1)
                    dve.wait_ge(d_den, 3 * n + 1)
                    dve.tensor_scalar(den, den, CUM_EPS, None, ALU.add).then_inc(d_den, 1)
                    dve.wait_ge(d_den, 3 * n + 2)
                    dve.reciprocal(den, den).then_inc(d_den, 1)
                    dve.wait_ge(d_den, 3 * n + 3)
                    dve.wait_ge(g_num, n + 1)
                    if n:
                        dve.wait_ge(g_attl, n)
                    dve.tensor_tensor(att, num, den, ALU.mult).then_inc(d_att, 1)
                dve.wait_ge(t_out1, b + 1)
                take_sums(OUT1_SCALE / (ATT_SCALE * W_SCALE))
                add_norm(2, b)
            if STAGES < 4:
                return
            for b in range(B):
                low_xT(3, b)
                for m in range(I_TILES):
                    product_of(B * M_TILES + b * I_TILES + m, i_rows(m))
                dve.wait_ge(t_down, B * M_TILES + I_TILES * (b + 1))
                take_sums(1 / W_SCALE)
                add_norm(3, b, last_phase=True)

        @block.tensor
        def _(pe):
            def product(dst, lhs, rhs, start, stop, skip=False):
                terms = ((lhs[0], rhs[0]), (lhs[0], rhs[1]), (lhs[1], rhs[0]))
                for i, (l, r) in enumerate(terms):
                    last = pe.matmul(dst, l, r, start=start and i == 0, stop=stop and i == 2, skip_group_check=skip)
                return last

            pe.wait_ge(g_ident, 3)
            for n in range(B * KC):
                b, c = n // KC, n % KC
                pe.wait_ge(d_nrm, b + 1)
                if n >= 2:
                    pe.wait_ge(d_xT, n - 1)
                for t in range(TPB):
                    last = pe.transpose(T_bank[n % 2][:, t * P:(t + 1) * P], nrm[:, b * TPB + t, c * P:(c + 1) * P],
                                        identf[:, :])
                last.then_inc(t_xT, 1)
            pe.wait_ge(d_xTl, B * KC)
            pe.wait_ge(d_wl, W_PIECES)

            def step(cur, nxt, prev, prev2):
                def scores(q):
                    b, h, u, p = cur
                    if q == 0:
                        pe.wait_ge(a_qkh, 2 * u + 2)
                        pe.wait_ge(g_qkl, 2 * u + 2)
                    if q >= 2 or not first(u):
                        pe.wait_ge(a_exp, 4 * u + (q - 1))
                    n = (q + 1) * P
                    qs = [a[:, p, 0, q * P:(q + 1) * P] for a in (qkh, qkl)]
                    ks = [a[:, p, 1, 0:n] for a in (qkh, qkl)]
                    product(S_bank[q % 2][:, 0:n], qs, ks, True, False)
                    pe.matmul(S_bank[q % 2][:, q * P:n], identb[:, :], maskb[:, :], start=False, stop=True).then_inc(t_S, 1)

                def project(w):
                    b, h, u, p = nxt
                    if w:
                        pe.wait_ge(a_qk, 2 * u + 1)
                    elif not isinstance(u, int) or u >= 3:
                        pe.wait_ge(d_vl, u - 2)
                    elif u:
                        pe.wait_ge(a_qk, 2 * u)
                    for c in range(KC):
                        ws = [a[w][:, bass.ds(h * DK + c * HD, DK)] for a in (wh, wl)]
                        xs = [a[:, c, b * S:(b + 1) * S] for a in (xTh, xTl)]
                        last = product(proj_bank[:, :], ws, xs, c == 0, c == KC - 1)
                    last.then_inc(t_qk, 1)

                def project_v():
                    if nxt:
                        pe.wait_ge(a_qk, 2 * nxt[2] + 2)
                    b, h, u, p = prev
                    if not nxt:
                        pe.wait_ge(d_vl, u)
                    for t in range(TPB):
                        for c in range(KC):
                            xs = [a[:, c, b * S + t * P:b * S + (t + 1) * P] for a in (xTh, xTl)]
                            ws = [a[2][:, bass.ds(h * DK + c * HD, DK)] for a in (wh, wl)]
                            last = product(proj_bank[:, t * P:(t + 1) * P], xs, ws, c == 0, c == KC - 1)
                    last.then_inc(t_v, 1)

                def turn(q):
                    b, h, u, p = prev
                    pe.wait_ge(d_prob, 4 * u + (q + 1))
                    if q >= 2 or not first(u):
                        pe.wait_ge(d_Tl, 4 * u + (q - 1))
                    for k in range(q + 1):
                        last = pe.transpose(T_bank[q % 2][:, k * P:(k + 1) * P], prob[:, p, q, k * P:(k + 1) * P],
                                            identf[:, :])
                    last.then_inc(t_T, 1)

                def weigh():
                    b, h, u, p = prev2
                    pe.wait_ge(d_Tl, 4 * u + 4)
                    pe.wait_ge(d_vl, u + 1)
                    if not first(u):
                        pe.wait_ge(d_ol, u)
                    for k in range(TPB):
                        vs = [a[:, k * P:(k + 1) * P] for a in (vh, vl)]
                        ps = [a[:, k, k * P:S] for a in (pTh, pTl)]
                        last = product(o_bank[:, k * P:S], vs, ps, k == 0, k == TPB - 1)
                    last.then_inc(t_pv, 1)

                def out_project():
                    b, h, u, p = prev2
                    pe.wait_ge(d_ol, u + 1)
                    for t in range(TPB):
                        os_ = [a[:, t * P:(t + 1) * P] for a in (oh, ol)]
                        ws = [a[3][:, bass.ds(h * D, D)] for a in (wh, wl)]
                        last = product(acc_bank[t // 2][:, t % 2 * D:t % 2 * D + D], os_, ws, False, False, skip=True)
                    last.then_inc(t_op, 1)

                if nxt:
                    project(0)
                if cur:
                    scores(0)
                    scores(1)
                if prev2:
                    weigh()
                if nxt:
                    project(1)
                if prev:
                    turn(0)
                    turn(1)
                if cur:
                    scores(2)
                if prev:
                    turn(2)
                if cur:
                    scores(3)
                if prev:
                    project_v()
                    turn(3)
                if prev2:
                    out_project()

            def open_sums():
                for a in acc_bank:
                    pe.matmul(a[:, :], identb[:, :], zerob[:, :], start=True, stop=False, skip_group_check=True)

            def finish_batch(b):
                if b + 1 < B:
                    pe.wait_ge(d_acc, b + 1)
                    open_sums()

            open_sums()
            pipeline(pe, step, finish_batch)
            if STAGES < 2:
                return

            def turn_norm(phase, b, cols):
                pe.wait_ge(d_nrm, phase * B + b + 1)
                for c in range(KC):
                    n = (phase * B + b) * KC + c
                    if n >= 2:
                        pe.wait_ge(d_xTl, n - 1)
                    for t in range(TPB):
                        last = pe.transpose(T_bank[n % 2][:, t * P:(t + 1) * P], nrm[:, b * TPB + t, cols(c)], identf[:, :])
                    last.then_inc(t_xT, 1)
                pe.wait_ge(d_xTl, (phase * B + b + 1) * KC)

            def x_parts(b, c):
                return [a[:, c, b * S:(b + 1) * S] for a in (xTh, xTl)]

            def hidden(n, b, gate, up, rows=P):
                if n >= 2:
                    pe.wait_ge(a_gelu, n - 1)
                for c in range(KC):
                    last = product(G_bank[n % 2][0:rows, :], gate(c), x_parts(b, c), c == 0, c == KC - 1)
                last.then_inc(t_gate, 1)
                if n >= 2:
                    pe.wait_ge(d_inter, n - 1)
                for c in range(KC):
                    last = product(U_bank[n % 2][0:rows, :], up(c), x_parts(b, c), c == 0, c == KC - 1)
                last.then_inc(t_up, 1)

            def down(n, parts, rows=P):
                pe.wait_ge(g_il, n + 1)
                for t in range(TPB):
                    hs = [a[n % 2][0:rows, t * P:(t + 1) * P] for a in (ih, il)]
                    last = product(acc_bank[t // 2][:, t % 2 * D:t % 2 * D + D], hs, parts, False, False, skip=True)
                last.then_inc(t_down, 1)

            def even_odd(c):
                return slice(c, D, NIBBLES)

            def halves(c):
                return slice(c * P, (c + 1) * P)

            pe.wait_ge(d_fl, NIBBLES * Q_PIECES)
            for b in range(B):
                turn_norm(1, b, even_odd)
                pe.wait_ge(d_acc, B + b)
                open_sums()
                for m in range(M_TILES + 1):
                    n = b * M_TILES + m
                    if m < M_TILES:
                        hidden(n, b, lambda c: [f[0][:, c, m * P:(m + 1) * P] for f in (fh, fl)],
                               lambda c: [f[1][:, c, m * P:(m + 1) * P] for f in (fh, fl)])
                    if m:
                        j, c = (m - 1) // NIBBLES, (m - 1) % NIBBLES
                        down(n - 1, [f[2][:, c, j * D:(j + 1) * D] for f in (fh, fl)])
            if STAGES < 3:
                return
            for b in range(B):
                turn_norm(2, b, halves)
                for f in range(FT):
                    n = b * FT + f
                    if n >= 2:
                        pe.wait_ge(d_kv, n - 1)
                    for w in range(3):
                        for c in range(KC):
                            o = (w * FT + f) * P
                            last = product(qkv_bank[n % 2][w][:, :], [a[:, c, o:o + P] for a in (w1h, w1l)], x_parts(b, c),
                                           c == 0, c == KC - 1)
                        last.then_inc(t_qkv, 1)
                pe.wait_ge(d_acc, 2 * B + b)
                pe.wait_ge(g_attl, FT * (b + 1))
                for t in range(TPB):
                    for f in range(FT):
                        parts = [a[f][:, t * P:(t + 1) * P] for a in (atth, attl)]
                        ws = [a[:, f, 3 * D:4 * D] for a in (w1h, w1l)]
                        last = product(acc_bank[t // 2][:, t % 2 * D:t % 2 * D + D], parts, ws, f == 0, f == FT - 1)
                last.then_inc(t_out1, 1)
            if STAGES < 4:
                return
            pe.wait_ge(g_w2l, L_PIECES)
            for b in range(B):
                turn_norm(3, b, halves)
                pe.wait_ge(d_acc, 3 * B + b)
                open_sums()
                for m in range(I_TILES + 1):
                    n = B * M_TILES + b * I_TILES + m
                    if m < I_TILES:
                        r = i_rows(m)

                        def cols(c, w):
                            o = (c * 2 + w) * INTER + m * P
                            return [a[:, o:o + r] for a in (wh[3], wl[3])]
                        hidden(n, b, lambda c: cols(c, 0), lambda c: cols(c, 1), r)
                    if m:
                        r = i_rows(m - 1)
                        down(n - 1, [a[0:r, (m - 1) * D:m * D] for a in (w2dh, w2dl)], r)


def kernel(**inputs):
    import numpy as np
    import concourse.bacc as bacc
    from concourse.bass_utils import run_bass_kernel_spmd

    a = {k: np.asarray(v) for k, v in inputs.items()}
    f32 = np.float32
    theta = f32(1.0) / np.power(f32(10000.0), np.arange(0, DK, 2, dtype=f32) / f32(DK))
    angle = (np.arange(S, dtype=np.float32)[None, :] * np.concatenate([theta, theta])[:, None]).astype(np.float64)
    turned = np.where(np.arange(DK)[:, None] < DK // 2, 1.0, -1.0) * np.sin(angle)
    scale = 1.0 / np.sqrt(DK)
    ropes = np.stack([np.cos(angle) * scale, turned * scale, np.cos(angle), turned]).astype(np.float32)


    def by_hidden(w):
        rows = w.shape[0]
        return w.reshape(rows, MLP // (NIBBLES * P), P, NIBBLES).transpose(0, 1, 3, 2).reshape(rows, MLP)

    def by_row(w, rows):
        return w.reshape(-1, rows, w.shape[1]).transpose(1, 0, 2).reshape(rows, -1)

    gate_up = np.concatenate([a["L1_ffn_gate_idx"].T, a["L1_ffn_up_idx"].T], axis=1)
    down = np.concatenate([a["L1_ffn_down_idx"].T, np.zeros((I_TILES * P - INTER, D), a["L1_ffn_down_idx"].dtype)])
    arrays = {
        "x": a["L0_attn_h"],
        "wqT": a["L0_attn_wq"].T, "wkT": a["L0_attn_wk"].T, "wvT": a["L0_attn_wv"].T, "woT": a["L0_attn_wo"].T,
        "bqT": a["L0_attn_bq"].reshape(HEADS, DK).T, "bkT": a["L0_attn_bk"].reshape(HEADS, DK).T,
        "bvT": a["L0_attn_bv"].reshape(HEADS, DK).T, "bo": a["L0_attn_bo"],
        "gT": a["L0_attn_ln_g"].reshape(KC, P).T, "bT": a["L0_attn_ln_b"].reshape(KC, P).T,
        "ropes": ropes,
        "w1T": np.concatenate([a["L1_attn_W_qkv"].T, a["L1_attn_W_out"].T], axis=1),
        "packed": np.stack([by_hidden(a["L0_ffn_gate_W_packed"].T), by_hidden(a["L0_ffn_up_W_packed"].T),
                            by_row(a["L0_ffn_down_W_packed"].T, P)]),
        "scales": np.stack([by_hidden(a["L0_ffn_gate_scales"].T), by_hidden(a["L0_ffn_up_scales"].T),
                            by_row(a["L0_ffn_down_scales"].T, P // Q_ROWS)]),
        "codes": np.concatenate([by_row(gate_up, P), by_row(down, P)], axis=1),
        "lut": a["L1_ffn_lut"],
    }
    arrays = {f"in_{k}": np.ascontiguousarray(v) for k, v in arrays.items()}
    nc = bacc.Bacc("TRN2", target_bir_lowering=False, num_devices=1)
    args = [nc.dram_tensor(k, v.shape, mybir.dt.from_np(v.dtype), kind="ExternalInput").ap() for k, v in arrays.items()]
    args.append(nc.dram_tensor("out", (B, S, D), F32, kind="ExternalOutput").ap())
    sandwich(nc, *args)
    return run_bass_kernel_spmd(nc, [arrays], core_ids=[0]).results[0]["out"]
```

```python
from contextlib import ExitStack

import concourse.bass as bass
from concourse import mybir

ALU = mybir.AluOpType
ACT = mybir.ActivationFunctionType
AX_X = mybir.AxisListType.X
F32 = mybir.dt.float32
F16 = mybir.dt.float16
BF16 = mybir.dt.bfloat16
FP8 = mybir.dt.float8e4
I32 = mybir.dt.int32

P = 128
B, S, D = 2, 512, 256
TPB = S // P
KC = D // P
HEADS, DK = 16, 128
HD = HEADS * DK
LN_EPS = 1e-5
MASKED = -1e30

X_SCALE = 16.0
W_SCALE = 256.0
P_SCALE = 64.0
UNITS = B * HEADS
W_COLS = 1024
W_PIECES = 4 * HD * KC // W_COLS + 2
W_ORDER = (tuple((w, c * HD) for w in range(3) for c in range(KC)) + ((3, 0), (3, W_COLS))
           + tuple((w, c * HD + W_COLS) for w in range(3) for c in range(KC)) + ((3, 2 * W_COLS), (3, 3 * W_COLS))
           + ((4, 0), (4, W_COLS)))
QK_W = 2 * KC
FIRST_W = 3 * KC
PEELED = 5
DVE_W = ((6, 7), (8,), (10,), (12,), (14,), (15,), (), ())
POOL_W = ((), (9,), (11,), (13,), (), (), (16,), (17,))
ALL_POOL_W = sum(POOL_W, tuple(range(FIRST_W)))
MLP = 2048
M_TILES = MLP // P
NIBBLES = 2
Q_BLOCK = 32
Q_ROWS = Q_BLOCK // NIBBLES
Q_COLS = 512
Q_PIECES = 3 * MLP // Q_COLS
FP4_AS_FP8 = 64.0
DW = 1024
FT = D // P
ATT_SCALE = 16.0
CUM_EPS = 1e-9
OUT1_SCALE = (D // 16) ** -0.5
INTER = 688
I_TILES = -(-INTER // P)
LUT = 16
GU_COLS = KC * 2 * INTER
DOWN_COLS = I_TILES * D
HALF = P // 2
CHUNKS = tuple((c, min(512, GU_COLS - c)) for c in range(0, GU_COLS, 512)) + tuple(
    (GU_COLS + c, 512) for c in range(0, DOWN_COLS, 512))
LOOKUPS = 2 * len(CHUNKS)
LATE_SLOT = 11
EARLY_LOOKUPS = 8
SUMS = ((0, 0), (0, 1), (1, 0), (2, 0), (1, 1), (3, 0), (2, 1), (3, 1))
NORMS = ((0, 0), (0, 1), (1, 0), (2, 0), (1, 1), (2, 1), (3, 0), (3, 1))
TURNS = ((0, 0), (0, 1), (1, 0), (1, 1), (2, 0), (3, 0), (2, 1), (3, 1))


def sandwich(nc, x_in, wqT, wkT, wvT, woT, bqT, bkT, bvT, bo, gT, bT, ropes, w1T, packed, scales, codes, lut, out):
    with ExitStack() as ctx:
        def sb(name, shape, dt):
            return ctx.enter_context(nc.sbuf_tensor(name, shape, dt))

        def sem(name):
            return ctx.enter_context(nc.semaphore(name))

        bank = [ctx.enter_context(nc.psum_tensor(f"bank{i}", [P, 512], F32)) for i in range(8)]
        acc_bank, S_bank, T_bank, proj_bank, o_bank = bank[0:2], bank[2:4], bank[4:6], bank[6], bank[7]

        x = sb("x", [P, B * TPB, D], F32)
        xa = sb("xa", [P, B * TPB, D], F32)
        nrm = sb("nrm", [P, B * TPB, D], F32)
        y = sb("y", [P, TPB, D], F32)
        stats = sb("stats", [P, TPB, 6], F32)
        mv = sb("mv", [P, TPB, 2], F32)
        std = sb("std", [P, TPB], F32)
        rstd = sb("rstd", [P, TPB], F32)
        eps_ln = sb("eps_ln", [P, 1], F32)
        xT = sb("xT", [P, 2, S], F32)
        stage = sb("stage", [P, 4, W_COLS], F32)
        xTh = sb("xTh", [P, KC, B * S], F16)
        xTl = sb("xTl", [P, KC, B * S], F16)
        identf = sb("identf", [P, P], F32)
        identb = sb("identb", [P, P], BF16)
        maskb = sb("maskb", [P, P], BF16)
        zerob = sb("zerob", [P, 512], BF16)
        wh = [sb(f"w{n}h", [P, 4096], F16) for n in "qkvo"]
        wl = [sb(f"w{n}l", [P, 4096], F16) for n in "qkvo"]
        bias_q = sb("bias_q", [P, HEADS], F32)
        bias_k = sb("bias_k", [P, HEADS], F32)
        bias_v = sb("bias_v", [P, HEADS], F32)
        bo_row = sb("bo_row", [P, D], F32)
        ln_g = sb("ln_g", [P, KC], F32)
        ln_b = sb("ln_b", [P, KC], F32)
        rope = sb("rope", [P, 4, S], F32)
        w1h = sb("w1h", [P, KC, DW], F16)
        w1l = sb("w1l", [P, KC, DW], F16)
        raw = stage[:, 0:2, :].rearrange("p i n -> p (i n)").bitcast(I32).rearrange("p (i n) -> p i n", n=Q_COLS)
        scl = stage[:, 2:4, :].rearrange("p i n -> p (i n)").rearrange("p (i n) -> p i n", n=Q_COLS)
        sign = xT[:, 0, :].bitcast(I32)
        lut_row = sb("lut_row", [P, LUT], F32)
        w2dh = sb("w2dh", [P, DOWN_COLS], F16)
        w2dl = sb("w2dl", [P, DOWN_COLS], F16)
        lut_own = sb("lut_own", [P, LUT // 2], F32)
        lut_h = sb("lut_h", [P, LUT // 2], F16)
        lut_l = sb("lut_l", [P, LUT // 2], F16)
        entry = sb("entry", [P, LUT // 2], F32)
        twice = sb("twice", [P, HALF], F32)
        spread = sb("spread", [P, LUT // 2, P], F16)
        qf = sb("qf", [P, 2, S], F32)
        rc = sb("rc", [P, 2, S], F32)
        rs = sb("rs", [P, 2, S], F32)
        rr = sb("rr", [P, 2, S], F32)
        qkh = sb("qkh", [P, 2, 2, S], F16)
        qkl = sb("qkl", [P, 2, 2, S], F16)
        vh = sb("vh", [P, S], F16)
        vl = sb("vl", [P, S], F16)
        prob = sb("prob", [P, 2, TPB, S], F32)
        nmax = sb("nmax", [P, 2, TPB], F32)
        psum_row = sb("psum_row", [P, 2, TPB], F32)
        rinv = sb("rinv", [P, 2, TPB], F32)
        pTh = sb("pTh", [P, TPB, S], F16)
        pTl = sb("pTl", [P, TPB, S], F16)
        oh = sb("oh", [P, S], F16)
        ol = sb("ol", [P, S], F16)
        gel = qf
        inter = rc
        ih = [qkh[:, i, 0, :] for i in range(2)]
        il = [qkl[:, i, 0, :] for i in range(2)]
        G_bank, U_bank = S_bank, T_bank
        side_bank = bank[6:8]
        w32 = [rr, rs]
        bits = [prob[:, 0, 2 * i:2 * i + 2, :].bitcast(I32) for i in range(NIBBLES)]
        idx = xa[:, :, :].rearrange("p t n -> p (t n)").bitcast(I32).rearrange("p (i n) -> p i n", n=512)
        idx16 = xT[:, 1, :].bitcast(F16).rearrange("p (i n) -> p i n", n=512)
        rope16 = rope[:, :, :].rearrange("p f s -> p (f s)").bitcast(F16).rearrange("p (e n) -> p e n", n=512)
        r16 = [a[:, :, :].rearrange("p w s -> p (w s)").bitcast(F16).rearrange("p (e n) -> p e n", n=512) for a in (rr, rs)]
        hot = [[rope16[:, e, :] for e in range(LUT // 2)], [r16[e // 4][:, e % 4, :] for e in range(LUT // 2)]]
        neg, expo, pos, phi = ([a] * (B * FT - 1) + [z] for a, z in (
            (prob[:, 0, 0:2, :], rope[:, 0:2, :]), (prob[:, 0, 2:4, :], rope[:, 2:4, :]),
            (prob[:, 1, 0:2, :], rr), (prob[:, 1, 2:4, :], rs)))
        kv, kv_sum, k_sum, num, den, att, ones = [stage[:, i // 2, i % 2 * 512:(i % 2 + 1) * 512] for i in range(7)]
        atth = [pTh[:, i, :] for i in range(FT)]
        attl = [pTl[:, i, :] for i in range(FT)]
        fh = [w[:, :].rearrange("p (c n) -> p c n", c=NIBBLES) for w in wh[0:3]]
        fl = [w[:, :].rearrange("p (c n) -> p c n", c=NIBBLES) for w in wl[0:3]]

        s_x = [sem("s_x0"), sem("s_x1")]
        s_small = sem("s_small")
        s_rope = sem("s_rope")
        s_bo = sem("s_bo")
        g_wl = sem("g_wl")
        s_w = [sem(f"s_w{i}") for i in range(4)]
        s_out = sem("s_out")
        s_raw = [sem(f"s_raw{i}") for i in range(4)]
        s_idx = [sem(f"s_idx{i}") for i in range(4)]
        s_lut = sem("s_lut")
        d_bits = sem("d_bits")
        a_fh = sem("a_fh")
        d_fl = sem("d_fl")
        g_w32 = sem("g_w32")
        d_lut = sem("d_lut")
        d_idx16 = sem("d_idx16")
        d_hot = sem("d_hot")
        t_lut = sem("t_lut")
        a_w2 = sem("a_w2")
        g_twice = sem("g_twice")
        d_entry = sem("d_entry")
        t_gate = sem("t_gate")
        t_up = sem("t_up")
        t_down = sem("t_down")
        a_gelu = sem("a_gelu")
        d_inter = sem("d_inter")
        a_ih = sem("a_ih")
        g_il = sem("g_il")
        t_qkv = sem("t_qkv")
        d_neg = sem("d_neg")
        a_pos = sem("a_pos")
        a_expo = sem("a_expo")
        g_phi = sem("g_phi")
        d_kv = sem("d_kv")
        d_cum = sem("d_cum")
        g_num = sem("g_num")
        d_den = sem("d_den")
        d_att = sem("d_att")
        a_atth = sem("a_atth")
        g_attl = sem("g_attl")
        t_out1 = sem("t_out1")
        g_const = sem("g_const")
        g_ident = sem("g_ident")
        d_bn = sem("d_bn")
        d_var = sem("d_var")
        a_std = sem("a_std")
        d_rstd = sem("d_rstd")
        d_z = sem("d_z")
        d_nrm = sem("d_nrm")
        d_vec = sem("d_vec")
        g_res = sem("g_res")
        t_xT = sem("t_xT")
        d_xT = sem("d_xT")
        a_xTh = sem("a_xTh")
        d_xTl = sem("d_xTl")
        a_wh = sem("a_wh")
        d_wl = sem("d_wl")
        t_qk = sem("t_qk")
        t_v = sem("t_v")
        t_S = sem("t_S")
        t_T = sem("t_T")
        t_pv = sem("t_pv")
        t_op = sem("t_op")
        a_qk = sem("a_qk")
        a_exp = sem("a_exp")
        a_Th = sem("a_Th")
        a_qkh = sem("a_qkh")
        a_vh = sem("a_vh")
        a_oh = sem("a_oh")
        d_max = sem("d_max")
        d_sin = sem("d_sin")
        d_Tl = sem("d_Tl")
        d_vl = sem("d_vl")
        d_rinv = sem("d_rinv")
        d_ol = sem("d_ol")
        d_acc = sem("d_acc")
        d_y = sem("d_y")
        d_x = sem("d_x")
        d_prob = sem("d_prob")
        g_cos = sem("g_cos")
        g_rot = sem("g_rot")
        g_qkl = sem("g_qkl")

        x_tok = x_in.rearrange("b (t p) d -> p (b t) d", p=P)
        out_tok = out.rearrange("b (t p) d -> p (b t) d", p=P)
        w1_dram = w1T.rearrange("(c p) n -> p c n", p=P)
        w_dram = [w.rearrange("(c p) n -> p c n", p=P) for w in (wqT, wkT, wvT, woT)]

        def w_piece(j):
            return W_ORDER[j]

        def w_high(j):
            w, c0 = w_piece(j)
            return wh[w][:, c0:c0 + W_COLS] if w < 4 else w1h[:, c0 // DW, :]

        def w_low(j):
            w, c0 = w_piece(j)
            return wl[w][:, c0:c0 + W_COLS] if w < 4 else w1l[:, c0 // DW, :]

        def lows_before(j):
            g = sum(i in ALL_POOL_W for i in range(j))
            return j - g, g

        def q_piece(j):
            c0 = j // 3 * Q_COLS
            return j % 3, slice(c0, c0 + Q_COLS)

        def lookup(s):
            c0, n = CHUNKS[s // 2]
            rows = slice(s % 2 * HALF, (s % 2 + 1) * HALF)
            if c0 < GU_COLS:
                return c0, n, rows, wh[3][rows, c0:c0 + n], wl[3][rows, c0:c0 + n]
            return c0, n, rows, w2dh[rows, c0 - GU_COLS:c0 - GU_COLS + n], w2dl[rows, c0 - GU_COLS:c0 - GU_COLS + n]

        def lookups_beside(m):
            if m < EARLY_LOOKUPS // 2:
                return 2 * m, 2 * m + 1
            s = EARLY_LOOKUPS + 2 * (m - LATE_SLOT)
            return (s, s + 1) if m >= LATE_SLOT else ()

        def unpack_beside(m):
            j = 3 * (m // 4 + 1) + m % 4
            return j if m % 4 < 3 and j < Q_PIECES else None

        def y_event(phase, b):
            k = NORMS.index((phase, b))
            return 2 * B + 2 * k - (b if phase == 3 else 0)

        def turn_bank(phase, b, c):
            return (proj_bank, S_bank[0])[c] if (phase, b) == (1, 0) else side_bank[c]

        def qkv_bank(n, w):
            return side_bank[(3 * (n % FT) + w) % 2]

        def i_rows(m):
            return min(P, INTER - m * P)

        def preparation(cur):
            if cur is None:
                return None
            n = cur[2]
            return {**{h: h + 1 for h in range(PEELED)}, HEADS: PEELED + 1, HEADS + 1: PEELED + 2}.get(n) if isinstance(n, int) else None

        def first(n):
            return isinstance(n, int) and n == 0

        block = ctx.enter_context(nc.Block())


        def pipeline(eng, step, after):
            def unit(n):
                return (n // HEADS, n % HEADS, n, n % 2) if 0 <= n < UNITS else None

            def around(n):
                return unit(n), unit(n + 1), unit(n - 1), unit(n - 2), unit(n - 3)

            step(*around(-1))
            for b in range(B):
                for h in range(PEELED):
                    step(*around(b * HEADS + h))
                    after(b * HEADS + h)
                with eng.Fori(PEELED, HEADS - 2, 2) as i:
                    for j in range(2):
                        step(*((b, i + k, i + (b * HEADS + k), (k + 1) % 2) for k in (j, j + 1, j - 1, j - 2, j - 3)))
                step(*around((b + 1) * HEADS - 1))
                after((b + 1) * HEADS - 1)
            for n in range(UNITS, UNITS + 3):
                step(*around(n))
                after(n)

        @block.sync
        def _(sp):
            for b in range(B):
                sp.dma_start(x[:, b * TPB:(b + 1) * TPB, :], x_tok[:, b * TPB:(b + 1) * TPB, :]).then_inc(s_x[b], 16)
            for dst, src in ((ln_g, gT), (ln_b, bT), (bias_q, bqT), (bias_k, bkT), (bias_v, bvT)):
                sp.dma_start(dst[:, :], src).then_inc(s_small, 16)
            for j in range(W_PIECES):
                w, c0 = w_piece(j)
                if j >= 4:
                    by_dve, by_pool = lows_before(j - 3)
                    if j - 4 in ALL_POOL_W:
                        sp.wait_ge(g_wl, by_pool)
                    else:
                        sp.wait_ge(d_wl, by_dve)
                if w == 4:
                    src = w1_dram[:, c0 // DW, :]
                    dst = stage[:, j % 4, :]
                elif w < 3:
                    src = w_dram[w][:, c0 // HD, c0 % HD:c0 % HD + W_COLS]
                    dst = stage[:, j % 4, :]
                else:
                    src = w_dram[w][:, c0 // D:(c0 + W_COLS) // D, :]
                    dst = stage[:, j % 4, :].rearrange("p (h n) -> p h n", n=D)
                sp.dma_start(dst, src).then_inc(s_w[j % 4], 16)
                if j == 3:
                    sp.dma_start(rope[:, :, :], ropes.rearrange("f p s -> p f s")).then_inc(s_rope, 16)
                    sp.dma_start(bo_row[:, :], bo.partition_broadcast(P)).then_inc(s_bo, 16)
            sp.dma_start(lut_row[:, :], lut.partition_broadcast(P)).then_inc(s_lut, 16)
            by_dve, by_pool = lows_before(W_PIECES)
            sp.wait_ge(d_wl, by_dve)
            sp.wait_ge(g_wl, by_pool)
            for j in range(Q_PIECES):
                w, cols = q_piece(j)
                if j >= 4:
                    sp.wait_ge(g_w32, NIBBLES * (j - 3))
                sp.dma_start(raw[:, j % 4, :], packed[w, :, cols]).then_inc(s_raw[j % 4], 16)
                for g in range(P // Q_ROWS):
                    sp.dma_start(scl[g * Q_ROWS:(g + 1) * Q_ROWS, j % 4, :],
                                 scales[w, g, cols].partition_broadcast(Q_ROWS)).then_inc(s_raw[j % 4], 16)
            sp.wait_ge(d_acc, B)
            for s in range(LOOKUPS):
                if s >= 4:
                    sp.wait_ge(d_idx16, s - 3)
                c0, n, rows, _, _ = lookup(s)
                for h in range(2):
                    sp.dma_start(idx[h * HALF:(h + 1) * HALF, s % 4, 0:n], codes[rows, c0:c0 + n]).then_inc(s_idx[s % 4], 16)
            for b in range(B):
                sp.wait_ge(d_x, NORMS.index((3, b)) + 1)
                sp.dma_start(out_tok[:, b * TPB:(b + 1) * TPB, :], x[:, b * TPB:(b + 1) * TPB, :]).then_inc(s_out, 16)
            sp.wait_ge(s_out, 16 * B)

        @block.gpsimd
        def _(pool):
            pool.memset(identf[:, :], 0.0).then_inc(g_const, 1)
            pool.memset(identb[:, :], 0.0).then_inc(g_const, 1)
            pool.memset(maskb[:, :], 0.0).then_inc(g_const, 1)
            pool.memset(eps_ln[:, :], LN_EPS).then_inc(g_const, 1)
            pool.memset(zerob[:, :], 0.0).then_inc(g_const, 1)
            pool.wait_ge(g_const, 5)
            for m in (identf, identb):
                pool.affine_select(out=m[:, :], in_=m[:, :], compare_op=ALU.not_equal, fill=1.0, base=0,
                                   pattern=[[-1, P]], channel_multiplier=1).then_inc(g_ident, 1)
            pool.affine_select(out=maskb[:, :], in_=maskb[:, :], compare_op=ALU.is_ge, fill=MASKED, base=0,
                               pattern=[[-1, P]], channel_multiplier=1).then_inc(g_ident, 1)
            pool.wait_ge(g_ident, 3)
            pool.tensor_tensor(twice[:, :], identf[:, 0:HALF], identf[:, HALF:P], ALU.add).then_inc(g_twice, 1)

            def low_w(j):
                pool.wait_ge(a_wh, j + 1)
                pool.tensor_tensor(w_low(j), stage[:, j % 4, :], w_high(j), ALU.subtract).then_inc(g_wl, 1)

            def residual(b):
                pool.wait_ge(s_bo, 16)
                pool.wait_ge(d_nrm, b + 1)
                for t in range(b * TPB, (b + 1) * TPB):
                    last = pool.tensor_tensor(xa[:, t, :], xa[:, t, :], bo_row[:, :], ALU.add)
                last.then_inc(g_res, 1)

            def prepare(k):
                for j in POOL_W[k]:
                    low_w(j)

            for j in range(FIRST_W):
                low_w(j)
            pool.wait_ge(s_rope, 16)

            def step(cur, nxt, prev, prev2, prev3):
                if nxt:
                    b, h, u, p = nxt
                    for w in range(2):
                        pool.wait_ge(a_qk, 2 * u + (w + 1))
                        pool.tensor_tensor(rc[:, w, :], qf[:, w, :], rope[:, 2 * w, :], ALU.mult).then_inc(g_cos, 1)
                        if w == 0 and preparation(cur) is not None:
                            prepare(preparation(cur))
                        pool.wait_ge(g_cos, 2 * u + (w + 1))
                        pool.wait_ge(d_sin, 2 * u + (w + 1))
                        pool.tensor_tensor(rr[:, w, :], rc[:, w, :], rs[:, w, :], ALU.add).then_inc(g_rot, 1)
                    for w in range(2):
                        pool.wait_ge(a_qkh, 2 * u + (w + 1))
                        pool.tensor_tensor(qkl[:, p, w, :], rr[:, w, :], qkh[:, p, w, :], ALU.subtract).then_inc(g_qkl, 1)
                    if not cur and not prev:
                        residual(0)
                        residual(1)

            def scaled(j):
                pool.wait_ge(d_bits, 2 * j + 2)
                if j >= 2:
                    pool.wait_ge(d_fl, NIBBLES * (j - 1))
                for c in range(NIBBLES):
                    code = bits[j % 2][:, c, :].bitcast(FP8).rearrange("p (n e) -> p n e", e=4)[:, :, 0]
                    pool.tensor_tensor(w32[j % 2][:, c, :], code, scl[:, j % 4, :], ALU.mult).then_inc(g_w32, 1)

            def low_inter(n, rows=P):
                pool.wait_ge(a_ih, n + 1)
                pool.tensor_tensor(il[n % 2][0:rows, :], inter[0:rows, n % 2, :], ih[n % 2][0:rows, :],
                                   ALU.subtract).then_inc(g_il, 1)

            def features(n):
                for w in range(2):
                    pool.wait_ge(a_expo, 2 * n + w + 1)
                    pool.tensor_tensor(phi[n][:, w, :], pos[n][:, w, :], expo[n][:, w, :], ALU.add).then_inc(g_phi, 1)

            def numerator(n):
                pool.wait_ge(d_cum, 2 * n + 2)
                pool.tensor_tensor(num, phi[n][:, 0, :], kv_sum, ALU.mult).then_inc(g_num, 1)

            def low_att(n):
                pool.wait_ge(a_atth, n + 1)
                pool.tensor_tensor(attl[n % FT], att, atth[n % FT], ALU.subtract).then_inc(g_attl, 1)

            def after(n):
                if n == UNITS:
                    pool.wait_ge(g_qkl, 2 * UNITS)
                    for j in range(3):
                        scaled(j)

            pipeline(pool, step, after)
            for m in range(M_TILES):
                low_inter(m)
                if unpack_beside(m):
                    scaled(unpack_beside(m))
            for m in range(M_TILES):
                low_inter(M_TILES + m)
                if m == 5:
                    features(0)
                if m == 6:
                    numerator(0)
                if m == 7:
                    low_att(0)
                    features(1)
                if m == 8:
                    numerator(1)
                if m == 9:
                    low_att(1)
            for m in range(I_TILES):
                if m == 3:
                    features(FT)
                if m == 4:
                    features(FT + 1)
                low_inter(B * M_TILES + m, i_rows(m))
                if m == 3:
                    numerator(FT)
                if m == 4:
                    low_att(FT)
            numerator(FT + 1)
            low_att(FT + 1)
            for m in range(I_TILES):
                low_inter(B * M_TILES + I_TILES + m, i_rows(m))

        @block.scalar
        def _(act):
            def std_of(event):
                act.wait_ge(d_var, event + 1)
                act.activation(std[:, :], mv[:, :, 1], ACT.Sqrt, bias=eps_ln[:, 0:1]).then_inc(a_std, 1)

            act.wait_ge(g_const, 5)
            def high_xT0(b):
                for c in range(KC):
                    act.wait_ge(d_xT, b * KC + c + 1)
                    act.activation(xTh[:, c, b * S:(b + 1) * S], xT[:, c, :], ACT.Copy).then_inc(a_xTh, 1)

            def high_w(j):
                act.wait_ge(s_w[j % 4], 16 * (j // 4 + 1))
                last = act.activation(w_high(j), stage[:, j % 4, :], ACT.Copy, scale=W_SCALE)
                if j in ALL_POOL_W:
                    last = act.activation(stage[:, j % 4, :], stage[:, j % 4, :], ACT.Copy, scale=W_SCALE)
                last.then_inc(a_wh, 1)

            def prepare(k):
                for j in sorted(DVE_W[k] + POOL_W[k]):
                    high_w(j)

            std_of(0)
            high_w(0)
            high_w(1)
            std_of(1)
            high_w(2)
            high_w(3)
            high_xT0(0)
            std_of(2)
            for j in range(QK_W, FIRST_W):
                high_w(j)
            std_of(3)

            def step(cur, nxt, prev, prev2, prev3):
                def take(w):
                    b, h, u, p = nxt
                    act.wait_ge(t_qk, 2 * u + (w + 1))
                    if not first(u):
                        act.wait_ge(g_rot, 2 * u + (w - 1))
                    act.activation(qf[:, w, :], proj_bank[:, :], ACT.Identity, scale=1 / (X_SCALE * W_SCALE),
                                   bias=(bias_q, bias_k)[w][:, bass.ds(h, 1)]).then_inc(a_qk, 1)

                def exp(q):
                    b, h, u, p = cur
                    n = (q + 1) * P
                    act.wait_ge(d_max, 4 * u + (q + 1))
                    act.activation(prob[:, p, q, 0:n], S_bank[q % 2][:, 0:n], ACT.Exp, bias=nmax[:, p, q:q + 1],
                                   accum_out=psum_row[:, p, q:q + 1]).then_inc(a_exp, 1)

                def high_T(q):
                    b, h, u, p = prev
                    act.wait_ge(t_T, 4 * u + (q + 1))
                    act.activation(pTh[:, 0:q + 1, q * P:(q + 1) * P],
                                   T_bank[q % 2][:, 0:(q + 1) * P].rearrange("p (k n) -> p k n", n=P),
                                   ACT.Copy).then_inc(a_Th, 1)

                def high_qk(w):
                    b, h, u, p = nxt
                    act.wait_ge(g_rot, 2 * u + (w + 1))
                    act.activation(qkh[:, p, w, :], rr[:, w, :], ACT.Copy).then_inc(a_qkh, 1)

                if nxt:
                    take(0)
                if preparation(cur) is not None:
                    prepare(preparation(cur))
                if cur:
                    exp(0)
                    exp(1)
                if nxt:
                    take(1)
                if prev2:
                    b, h, u, p = prev2
                    act.wait_ge(t_pv, u + 1)
                    act.activation(oh[:, :], o_bank[:, :], ACT.Identity, bias=bias_v[:, bass.ds(h, 1)]).then_inc(a_oh, 1)
                if prev:
                    high_T(0)
                    high_T(1)
                if nxt:
                    high_qk(0)
                if cur:
                    exp(2)
                    exp(3)
                if nxt:
                    high_qk(1)
                if prev:
                    high_T(2)
                    b, h, u, p = prev
                    act.wait_ge(t_v, u + 1)
                    act.activation(vh[:, :], o_bank[:, :], ACT.Copy, scale=1 / (X_SCALE * W_SCALE)).then_inc(a_vh, 1)
                    high_T(3)
                if not cur and not prev and nxt:
                    high_xT0(1)
                    prepare(0)

            def high_fp4(j):
                w, cols = q_piece(j)
                for c in range(NIBBLES):
                    act.wait_ge(g_w32, NIBBLES * j + c + 1)
                    act.activation(fh[w][:, c, cols], w32[j % 2][:, c, :], ACT.Copy, scale=W_SCALE * FP4_AS_FP8).then_inc(a_fh, 1)

            def high_xT(phase, b):
                for c in range(KC):
                    act.wait_ge(t_xT, TURNS.index((phase, b)) * KC + c + 1)
                    act.activation(xTh[:, c, b * S:(b + 1) * S], turn_bank(phase, b, c)[:, :], ACT.Copy, scale=X_SCALE).then_inc(a_xTh, 1)

            def looked_up(s):
                c0, n, rows, w_h, w_l = lookup(s)
                act.wait_ge(t_lut, s + 1)
                act.activation(w_h, side_bank[1 - s % 2][0:HALF, 0:n], ACT.Copy)
                act.activation(w_l, side_bank[1 - s % 2][HALF:P, 0:n], ACT.Copy).then_inc(a_w2, 1)

            def gated(n, func, rows=P, between=lambda: None):
                act.wait_ge(t_gate, n + 1)
                if n >= 2:
                    act.wait_ge(d_inter, n - 1)
                act.activation(gel[0:rows, n % 2, :], G_bank[n % 2][0:rows, :], func,
                               scale=1 / (X_SCALE * W_SCALE)).then_inc(a_gelu, 1)
                between()
                act.wait_ge(d_inter, n + 1)
                if n >= 2:
                    act.wait_ge(t_down, n - 1)
                act.activation(ih[n % 2][0:rows, :], inter[0:rows, n % 2, :], ACT.Copy).then_inc(a_ih, 1)

            def exponents(n):
                for w in range(2):
                    act.wait_ge(t_qkv, 3 * n + w + 1)
                    if n:
                        act.wait_ge(g_phi, 2 * (n - 1) + w + 1)
                    act.activation(pos[n][:, w, :], qkv_bank(n, w)[:, :], ACT.Relu, scale=1 / (X_SCALE * W_SCALE)).then_inc(a_pos, 1)
                for w in range(2):
                    act.wait_ge(d_neg, 2 * n + w + 1)
                    act.activation(expo[n][:, w, :], neg[n][:, w, :], ACT.Exp, scale=1 / (X_SCALE * W_SCALE)).then_inc(a_expo, 1)

            def high_att(n):
                act.wait_ge(d_att, n + 1)
                if n >= FT:
                    act.wait_ge(t_out1, n // FT)
                act.activation(atth[n % FT], att, ACT.Copy).then_inc(a_atth, 1)

            def std_y(phase, b):
                std_of(y_event(phase, b))

            def std_x(phase, b):
                std_of(y_event(phase, b) + 1)

            def after(n):
                if n == HEADS + 3:
                    std_y(0, 0)
                if n == HEADS + 4:
                    std_x(0, 0)
                if n == UNITS + 1:
                    act.wait_ge(t_qk, 2 * UNITS)
                    act.wait_ge(t_v, UNITS)
                    high_fp4(0)
                    high_xT(1, 0)
                    high_fp4(1)
                if n == UNITS + 2:
                    std_y(0, 1)
                    high_fp4(2)

            act.wait_ge(d_vec, 3)
            pipeline(act, step, after)

            for m in range(M_TILES):
                gated(m, ACT.Gelu_apprx_tanh)
                if m == 4:
                    std_x(0, 1)
                if m and unpack_beside(m - 1):
                    high_fp4(unpack_beside(m - 1))
                if m == 10:
                    high_xT(1, 1)
            def beside_second(m):
                if m == 0:
                    std_y(1, 0)
                if m == 1:
                    std_x(1, 0)
                if m == 11:
                    std_y(2, 0)
                if m == 12:
                    std_x(2, 0)

            def beside_third(m):
                if m == 0:
                    std_y(1, 1)
                if m == 1:
                    std_x(1, 1)
                if m == 2:
                    high_xT(2, 1)
                if m == 3:
                    exponents(FT)
                if m == 4:
                    exponents(FT + 1)

            def beside_fourth(m):
                if m == 1:
                    std_y(3, 0)

            for m in range(M_TILES):
                gated(M_TILES + m, ACT.Gelu_apprx_tanh, P, lambda: beside_second(m))
                if m == 4:
                    high_xT(2, 0)
                if m == 5:
                    exponents(0)
                if m == 7:
                    high_att(0)
                    exponents(1)
                if m == 9:
                    high_att(1)
                for s in lookups_beside(m):
                    looked_up(s)
            high_xT(3, 0)
            for m in range(I_TILES):
                gated(B * M_TILES + m, ACT.Silu, i_rows(m), lambda: beside_third(m))
                if m == 4:
                    high_att(FT)
            high_att(FT + 1)
            std_y(2, 1)
            std_x(2, 1)
            high_xT(3, 1)
            for m in range(I_TILES):
                gated(B * M_TILES + I_TILES + m, ACT.Silu, i_rows(m), lambda: beside_fourth(m))
            std_y(3, 1)

        @block.vector
        def _(dve):
            for e in range(LUT // 2):
                for h in range(2):
                    dve.memset(entry[h * HALF:(h + 1) * HALF, e:e + 1], float(2 * e + h)).then_inc(d_entry, 1)
            dve.wait_ge(d_entry, LUT)

            def spread_of(event, src):
                for t in range(TPB):
                    last = dve.bn_stats(stats[:, t, :], src[:, t, :])
                last.then_inc(d_bn, 1)
                dve.wait_ge(d_bn, event + 1)
                for t in range(TPB):
                    last = dve.bn_aggr(mv[:, t, :], stats[:, t, :])
                last.then_inc(d_var, 1)

            def rstd_of(event):
                dve.wait_ge(a_std, event + 1)
                dve.reciprocal(rstd[:, :], std[:, :]).then_inc(d_rstd, 1)
                dve.wait_ge(d_rstd, event + 1)

            def normalised(dst, src):
                for t in range(TPB):
                    last = dve.tensor_scalar(dst[:, t, :], src[:, t, :], mv[:, t, 0:1], rstd[:, t:t + 1],
                                             ALU.subtract, ALU.mult)
                return last

            def first_norm(b):
                rows = slice(b * TPB, (b + 1) * TPB)
                dve.wait_ge(s_x[b], 16)
                spread_of(2 * b, x[:, rows, :])
                rstd_of(2 * b)
                normalised(xa[:, rows, :], x[:, rows, :]).then_inc(d_z, 1)

            def second_norm(b):
                rows = slice(b * TPB, (b + 1) * TPB)
                dve.wait_ge(d_z, b + 1)
                spread_of(2 * b + 1, xa[:, rows, :])
                rstd_of(2 * b + 1)
                normalised(nrm[:, rows, :], xa[:, rows, :]).then_inc(d_nrm, 1)

            def both_xT0(b):
                for c in range(KC):
                    n = b * KC + c
                    dve.wait_ge(t_xT, n + 1)
                    dve.tensor_scalar(xT[:, c, :], T_bank[c][:, :], ln_g[:, c:c + 1], ln_b[:, c:c + 1],
                                      ALU.mult, ALU.add).then_inc(d_xT, 1)
                for c in range(KC):
                    dve.wait_ge(a_xTh, b * KC + c + 1)
                    dve.tensor_tensor(xTl[:, c, b * S:(b + 1) * S], xT[:, c, :], xTh[:, c, b * S:(b + 1) * S],
                                      ALU.subtract).then_inc(d_xTl, 1)

            def prepare(k):
                for j in DVE_W[k]:
                    dve.wait_ge(a_wh, j + 1)
                    dve.scalar_tensor_tensor(out=w_low(j), in0=stage[:, j % 4, :], scalar=W_SCALE, in1=w_high(j),
                                             op0=ALU.mult, op1=ALU.subtract).then_inc(d_wl, 1)

            first_norm(0)
            second_norm(0)
            dve.wait_ge(s_small, 16 * 5)
            for v, scale in ((ln_g, X_SCALE), (ln_b, X_SCALE), (bias_v, P_SCALE)):
                dve.tensor_scalar(v[:, :], v[:, :], scale, None, ALU.mult).then_inc(d_vec, 1)
            dve.wait_ge(d_vec, 3)
            both_xT0(0)
            first_norm(1)
            second_norm(1)
            dve.wait_ge(s_rope, 16)

            def step(cur, nxt, prev, prev2, prev3):
                def top(q):
                    b, h, u, p = cur
                    dve.wait_ge(t_S, 4 * u + (q + 1))
                    dve.tensor_reduce(nmax[:, p, q:q + 1], S_bank[q % 2][:, 0:(q + 1) * P], AX_X, ALU.max,
                                      negate=True).then_inc(d_max, 1)

                def rotate(w):
                    b, h, u, p = nxt
                    dve.wait_ge(a_qk, 2 * u + (w + 1))
                    if not first(u):
                        dve.wait_ge(g_rot, 2 * u + (w - 1))
                    half = DK // 2
                    dve.tensor_tensor(rs[0:half, w, :], qf[half:DK, w, :], rope[half:DK, 2 * w + 1, :], ALU.mult)
                    dve.tensor_tensor(rs[half:DK, w, :], qf[0:half, w, :], rope[0:half, 2 * w + 1, :],
                                      ALU.mult).then_inc(d_sin, 1)

                def low_T(q):
                    b, h, u, p = prev
                    dve.wait_ge(a_Th, 4 * u + (q + 1))
                    dve.tensor_tensor(pTl[:, 0:q + 1, q * P:(q + 1) * P],
                                      T_bank[q % 2][:, 0:(q + 1) * P].rearrange("p (k n) -> p k n", n=P),
                                      pTh[:, 0:q + 1, q * P:(q + 1) * P], ALU.subtract).then_inc(d_Tl, 1)

                if cur:
                    top(0)
                    top(1)
                if nxt:
                    rotate(0)
                    rotate(1)
                if prev:
                    low_T(0)
                if prev2:
                    b, h, u, p = prev2
                    dve.wait_ge(a_oh, u + 1)
                    dve.scalar_tensor_tensor(out=ol[:, :], in0=o_bank[:, :], scalar=bias_v[:, bass.ds(h, 1)],
                                             in1=oh[:, :], op0=ALU.add, op1=ALU.subtract).then_inc(d_ol, 1)
                if prev:
                    low_T(1)
                if cur:
                    top(2)
                    top(3)
                if preparation(cur) is not None:
                    prepare(preparation(cur))
                if prev:
                    low_T(2)
                    b, h, u, p = prev
                    dve.wait_ge(a_vh, u + 1)
                    dve.scalar_tensor_tensor(out=vl[:, :], in0=o_bank[:, :], scalar=1 / (X_SCALE * W_SCALE),
                                             in1=vh[:, :], op0=ALU.mult, op1=ALU.subtract).then_inc(d_vl, 1)
                    low_T(3)
                if not cur and not prev and nxt:
                    both_xT0(1)
                    prepare(0)
                if cur:
                    b, h, u, p = cur
                    dve.wait_ge(a_exp, 4 * u + 4)
                    dve.reciprocal(rinv[:, p, :], psum_row[:, p, :]).then_inc(d_rinv, 1)
                    dve.wait_ge(d_rinv, u + 1)
                    for q in range(TPB):
                        row = prob[:, p, q, 0:(q + 1) * P]
                        dve.tensor_scalar(row, row, rinv[:, p, q:q + 1], P_SCALE, ALU.mult, ALU.mult).then_inc(d_prob, 1)

            def row_tile(banks, t):
                return banks[t // 2][:, t % 2 * D:t % 2 * D + D]

            def block_out(phase, b):
                return nrm[:, 0:TPB, :] if (phase, b) == (3, 0) else y[:, :, :]

            def take_sums(phase, b, banks, scale):
                dst = block_out(phase, b)
                for t in range(TPB):
                    if phase:
                        last = dve.tensor_scalar(dst[:, t, :], row_tile(banks, t), scale, None, ALU.mult)
                    else:
                        last = dve.scalar_tensor_tensor(out=dst[:, t, :], in0=row_tile(banks, t), scalar=scale,
                                                        in1=xa[:, b * TPB + t, :], op0=ALU.mult, op1=ALU.add)
                last.then_inc(d_acc, 1)
                dve.wait_ge(d_acc, SUMS.index((phase, b)) + 1)

            def add(phase, b):
                k, src = NORMS.index((phase, b)), block_out(phase, b)
                rstd_of(y_event(phase, b))
                normalised(src, src).then_inc(d_y, 1)
                dve.wait_ge(d_y, k + 1)
                for t in range(TPB):
                    last = dve.tensor_tensor(x[:, b * TPB + t, :], x[:, b * TPB + t, :], src[:, t, :], ALU.add)
                last.then_inc(d_x, 1)
                if phase < 3:
                    dve.wait_ge(d_x, k + 1)
                    spread_of(y_event(phase, b) + 1, x[:, b * TPB:(b + 1) * TPB, :])

            def norm(phase, b):
                rows = slice(b * TPB, (b + 1) * TPB)
                rstd_of(y_event(phase, b) + 1)
                normalised(nrm[:, rows, :], x[:, rows, :]).then_inc(d_nrm, 1)

            def attention_sums(b):
                dve.wait_ge(t_op, HEADS * (b + 1))
                dve.wait_ge(g_res, b + 1)
                take_sums(0, b, acc_bank, 1 / (P_SCALE * W_SCALE))
                spread_of(y_event(0, b), y[:, :, :])

            def unpacked(j):
                r, (low, high) = raw[:, j % 4, :], (bits[j % 2][:, c, :] for c in range(NIBBLES))
                dve.wait_ge(s_raw[j % 4], 16 * (1 + P // Q_ROWS) * (j // 4 + 1))
                if j >= 2:
                    dve.wait_ge(g_w32, NIBBLES * (j - 1))
                if j:
                    dve.wait_ge(d_bits, 2 * j)
                dve.tensor_scalar(low, r, 2, 0x1C, ALU.logical_shift_left, ALU.bitwise_and)
                dve.tensor_scalar(high, r, 2, 0x1C, ALU.logical_shift_right, ALU.bitwise_and)
                dve.tensor_scalar(sign, r, 4, 0x80, ALU.logical_shift_left, ALU.bitwise_and).then_inc(d_bits, 1)
                dve.wait_ge(d_bits, 2 * j + 1)
                dve.tensor_tensor(low, low, sign, ALU.bitwise_or)
                dve.scalar_tensor_tensor(out=high, in0=r, scalar=0x80, in1=high,
                                         op0=ALU.bitwise_and, op1=ALU.bitwise_or).then_inc(d_bits, 1)

            def low_fp4(j):
                w, cols = q_piece(j)
                for c in range(NIBBLES):
                    dve.wait_ge(a_fh, NIBBLES * j + c + 1)
                    dve.scalar_tensor_tensor(out=fl[w][:, c, cols], in0=w32[j % 2][:, c, :], scalar=W_SCALE * FP4_AS_FP8,
                                             in1=fh[w][:, c, cols], op0=ALU.mult, op1=ALU.subtract).then_inc(d_fl, 1)

            def low_xT(phase, b):
                for c in range(KC):
                    dve.wait_ge(a_xTh, TURNS.index((phase, b)) * KC + c + 1)
                    dve.scalar_tensor_tensor(out=xTl[:, c, b * S:(b + 1) * S], in0=turn_bank(phase, b, c)[:, :], scalar=X_SCALE,
                                             in1=xTh[:, c, b * S:(b + 1) * S],
                                             op0=ALU.mult, op1=ALU.subtract).then_inc(d_xTl, 1)

            def lut_spread():
                dve.wait_ge(s_lut, 16)
                dve.wait_ge(g_twice, 1)
                for h in range(2):
                    rows = slice(h * HALF, (h + 1) * HALF)
                    last = dve.tensor_scalar(lut_own[rows, :], lut_row[rows, h:LUT:2], W_SCALE, None, ALU.mult)
                last.then_inc(d_lut, 1)
                dve.wait_ge(d_lut, 1)
                dve.tensor_copy(lut_h[:, :], lut_own[:, :]).then_inc(d_lut, 1)
                dve.wait_ge(d_lut, 2)
                dve.tensor_tensor(lut_l[:, :], lut_own[:, :], lut_h[:, :], ALU.subtract).then_inc(d_lut, 1)
                dve.wait_ge(d_lut, 3)
                for e in range(LUT // 2):
                    dve.tensor_scalar(spread[:, e, 0:HALF], twice[:, :], lut_h[:, e:e + 1], None, ALU.mult)
                    last = dve.tensor_scalar(spread[:, e, HALF:P], twice[:, :], lut_l[:, e:e + 1], None, ALU.mult)
                last.then_inc(d_lut, 1)

            def entries_hit(s):
                n = CHUNKS[s // 2][1]
                dve.wait_ge(s_idx[s % 4], 32 * (s // 4 + 1))
                if s >= 2:
                    dve.wait_ge(d_hot, s - 1)
                dve.tensor_copy(idx16[:, s % 2, 0:n], idx[:, s % 4, 0:n]).then_inc(d_idx16, 1)
                dve.wait_ge(d_idx16, s + 1)
                if s >= 2:
                    dve.wait_ge(t_lut, s - 1)
                for e in range(LUT // 2):
                    last = dve.tensor_scalar(hot[s % 2][e][:, 0:n], idx16[:, s % 2, 0:n], entry[:, e:e + 1], None, ALU.is_equal)
                last.then_inc(d_hot, 1)

            def product_of(n, rows=P):
                dve.wait_ge(a_gelu, n + 1)
                dve.wait_ge(t_up, n + 1)
                if n >= 2:
                    dve.wait_ge(g_il, n - 1)
                dve.scalar_tensor_tensor(out=inter[0:rows, n % 2, :], in0=U_bank[n % 2][0:rows, :],
                                         scalar=1 / (X_SCALE * W_SCALE), in1=gel[0:rows, n % 2, :],
                                         op0=ALU.mult, op1=ALU.mult).then_inc(d_inter, 1)

            def negatives(n):
                for w in range(2):
                    dve.wait_ge(a_pos, 2 * n + w + 1)
                    dve.tensor_scalar(neg[n][:, w, :], qkv_bank(n, w)[:, :], 0.0, None, ALU.min).then_inc(d_neg, 1)

            def attend(n):
                dve.wait_ge(t_qkv, 3 * n + 3)
                dve.wait_ge(g_phi, 2 * n + 2)
                dve.scalar_tensor_tensor(out=kv, in0=qkv_bank(n, 2)[:, :], scalar=ATT_SCALE / (X_SCALE * W_SCALE),
                                         in1=phi[n][:, 1, :], op0=ALU.mult, op1=ALU.mult).then_inc(d_kv, 1)
                dve.wait_ge(d_kv, n + 1)
                dve.tensor_tensor_scan(kv_sum, ones, kv, 0.0, ALU.mult, ALU.add).then_inc(d_cum, 1)
                dve.tensor_tensor_scan(k_sum, ones, phi[n][:, 1, :], 0.0, ALU.mult, ALU.add).then_inc(d_cum, 1)
                dve.wait_ge(d_cum, 2 * n + 2)
                dve.tensor_tensor(den, phi[n][:, 0, :], k_sum, ALU.mult).then_inc(d_den, 1)
                dve.wait_ge(d_den, 3 * n + 1)
                dve.tensor_scalar(den, den, CUM_EPS, None, ALU.add).then_inc(d_den, 1)
                dve.wait_ge(d_den, 3 * n + 2)
                dve.reciprocal(den, den).then_inc(d_den, 1)
                dve.wait_ge(d_den, 3 * n + 3)
                dve.wait_ge(g_num, n + 1)
                if n:
                    dve.wait_ge(g_attl, n)
                dve.tensor_tensor(att, num, den, ALU.mult).then_inc(d_att, 1)

            def after(n):
                if n == HEADS + 2:
                    attention_sums(0)
                if n == HEADS + 3:
                    add(0, 0)
                if n == HEADS + 4:
                    norm(0, 0)
                if n == UNITS:
                    unpacked(0)
                    unpacked(1)
                if n == UNITS + 1:
                    unpacked(2)
                    low_fp4(0)
                    low_xT(1, 0)
                    low_fp4(1)
                if n == UNITS + 2:
                    attention_sums(1)
                    low_fp4(2)

            pipeline(dve, step, after)

            for m in range(M_TILES):
                product_of(m)
                if m == 3:
                    add(0, 1)
                if m == 7:
                    norm(0, 1)
                if unpack_beside(m):
                    unpacked(unpack_beside(m))
                if m and unpack_beside(m - 1):
                    low_fp4(unpack_beside(m - 1))
                if m == 10:
                    low_xT(1, 1)
                if m == 13:
                    lut_spread()
                    dve.memset(ones, 1.0)
                if m == M_TILES - 1:
                    for s in lookups_beside(0):
                        entries_hit(s)
            dve.wait_ge(t_down, M_TILES)
            take_sums(1, 0, acc_bank, 1 / W_SCALE)
            spread_of(y_event(1, 0), y[:, :, :])
            for m in range(M_TILES):
                product_of(M_TILES + m)
                if m + 1 < M_TILES:
                    for s in lookups_beside(m + 1):
                        entries_hit(s)
                if m == 0:
                    add(1, 0)
                if m == 1:
                    norm(1, 0)
                if m == 4:
                    low_xT(2, 0)
                if m == 5:
                    negatives(0)
                if m == 6:
                    attend(0)
                if m == 7:
                    negatives(1)
                if m == 8:
                    attend(1)
                if m == 10:
                    dve.wait_ge(t_out1, 1)
                    take_sums(2, 0, side_bank, OUT1_SCALE / (ATT_SCALE * W_SCALE))
                    spread_of(y_event(2, 0), y[:, :, :])
                if m == 11:
                    add(2, 0)
                if m == 12:
                    norm(2, 0)
            low_xT(3, 0)
            dve.wait_ge(t_down, B * M_TILES)
            take_sums(1, 1, acc_bank, 1 / W_SCALE)
            spread_of(y_event(1, 1), y[:, :, :])
            for m in range(I_TILES):
                if m == 2:
                    low_xT(2, 1)
                if m == 3:
                    negatives(FT)
                if m == 4:
                    negatives(FT + 1)
                product_of(B * M_TILES + m, i_rows(m))
                if m == 0:
                    add(1, 1)
                    norm(1, 1)
                if m == 3:
                    attend(FT)
            attend(FT + 1)
            dve.wait_ge(t_down, B * M_TILES + I_TILES)
            take_sums(3, 0, acc_bank, 1 / W_SCALE)
            dve.wait_ge(t_out1, B)
            take_sums(2, 1, side_bank, OUT1_SCALE / (ATT_SCALE * W_SCALE))
            spread_of(y_event(2, 1), y[:, :, :])
            add(2, 1)
            norm(2, 1)
            low_xT(3, 1)
            for m in range(I_TILES):
                product_of(B * M_TILES + I_TILES + m, i_rows(m))
                if m == 0:
                    spread_of(y_event(3, 0), block_out(3, 0))
                if m == 1:
                    add(3, 0)
            dve.wait_ge(t_down, B * M_TILES + B * I_TILES)
            take_sums(3, 1, acc_bank, 1 / W_SCALE)
            spread_of(y_event(3, 1), y[:, :, :])
            add(3, 1)

        @block.tensor
        def _(pe):
            def product(dst, lhs, rhs, start, stop, skip=False):
                terms = ((lhs[0], rhs[0]), (lhs[0], rhs[1]), (lhs[1], rhs[0]))
                for i, (l, r) in enumerate(terms):
                    last = pe.matmul(dst, l, r, start=start and i == 0, stop=stop and i == 2, skip_group_check=skip)
                return last

            pe.wait_ge(g_ident, 3)

            def turn_norm0(b):
                pe.wait_ge(d_nrm, b + 1)
                for c in range(KC):
                    for t in range(TPB):
                        last = pe.transpose(T_bank[c][:, t * P:(t + 1) * P], nrm[:, b * TPB + t, c * P:(c + 1) * P],
                                            identf[:, :])
                    last.then_inc(t_xT, 1)

            def prepare(k):
                if k == 1:
                    pe.wait_ge(g_wl, FIRST_W)
                if k == 0:
                    turn_norm0(1)
                    pe.wait_ge(d_xT, B * KC)
                if k == PEELED:
                    pe.wait_ge(d_xTl, B * KC)
                    by_dve, by_pool = lows_before(W_PIECES - KC)
                    pe.wait_ge(d_wl, by_dve)
                    pe.wait_ge(g_wl, by_pool)

            turn_norm0(0)
            pe.wait_ge(d_xTl, KC)
            pe.wait_ge(g_wl, QK_W)

            def step(cur, nxt, prev, prev2, prev3):
                def scores(q):
                    b, h, u, p = cur
                    if q == 0:
                        pe.wait_ge(a_qkh, 2 * u + 2)
                        pe.wait_ge(g_qkl, 2 * u + 2)
                    if q >= 2 or not first(u):
                        pe.wait_ge(a_exp, 4 * u + (q - 1))
                    n = (q + 1) * P
                    qs = [a[:, p, 0, q * P:(q + 1) * P] for a in (qkh, qkl)]
                    ks = [a[:, p, 1, 0:n] for a in (qkh, qkl)]
                    product(S_bank[q % 2][:, 0:n], qs, ks, True, False)
                    pe.matmul(S_bank[q % 2][:, q * P:n], identb[:, :], maskb[:, :], start=False, stop=True).then_inc(t_S, 1)

                def project(w):
                    b, h, u, p = nxt
                    if w:
                        pe.wait_ge(a_qk, 2 * u + 1)
                    elif not first(u):
                        pe.wait_ge(a_qk, 2 * u)
                    for c in range(KC):
                        ws = [a[w][:, bass.ds(h * DK + c * HD, DK)] for a in (wh, wl)]
                        xs = [a[:, c, b * S:(b + 1) * S] for a in (xTh, xTl)]
                        last = product(proj_bank[:, :], ws, xs, c == 0, c == KC - 1)
                    last.then_inc(t_qk, 1)

                def project_v():
                    b, h, u, p = prev
                    if not first(u):
                        pe.wait_ge(d_ol, u)
                    for t in range(TPB):
                        for c in range(KC):
                            xs = [a[:, c, b * S + t * P:b * S + (t + 1) * P] for a in (xTh, xTl)]
                            ws = [a[2][:, bass.ds(h * DK + c * HD, DK)] for a in (wh, wl)]
                            last = product(o_bank[:, t * P:(t + 1) * P], xs, ws, c == 0, c == KC - 1)
                    last.then_inc(t_v, 1)

                def turn(q):
                    b, h, u, p = prev
                    pe.wait_ge(d_prob, 4 * u + (q + 1))
                    if q >= 2 or not first(u):
                        pe.wait_ge(d_Tl, 4 * u + (q - 1))
                    for k in range(q + 1):
                        last = pe.transpose(T_bank[q % 2][:, k * P:(k + 1) * P], prob[:, p, q, k * P:(k + 1) * P],
                                            identf[:, :])
                    last.then_inc(t_T, 1)

                def weigh():
                    b, h, u, p = prev2
                    pe.wait_ge(d_Tl, 4 * u + 4)
                    pe.wait_ge(d_vl, u + 1)
                    for k in range(TPB):
                        vs = [a[:, k * P:(k + 1) * P] for a in (vh, vl)]
                        ps = [a[:, k, k * P:S] for a in (pTh, pTl)]
                        last = product(o_bank[:, k * P:S], vs, ps, k == 0, k == TPB - 1)
                    last.then_inc(t_pv, 1)

                def out_project():
                    b, h, u, p = prev3
                    pe.wait_ge(d_ol, u + 1)
                    for t in range(TPB):
                        os_ = [a[:, t * P:(t + 1) * P] for a in (oh, ol)]
                        ws = [a[3][:, bass.ds(h * D, D)] for a in (wh, wl)]
                        last = product(acc_bank[t // 2][:, t % 2 * D:t % 2 * D + D], os_, ws, False, False, skip=True)
                    last.then_inc(t_op, 1)

                if nxt:
                    project(0)
                if prev3:
                    out_project()
                if cur:
                    scores(0)
                    scores(1)
                if nxt:
                    project(1)
                if prev2:
                    weigh()
                if prev:
                    turn(0)
                    turn(1)
                if cur:
                    scores(2)
                    scores(3)
                if prev:
                    turn(2)
                    project_v()
                    turn(3)
                if not cur and not prev and nxt:
                    prepare(0)
                if preparation(cur) is not None:
                    prepare(preparation(cur))

            def open_sums():
                for a in acc_bank:
                    pe.matmul(a[:, :], identb[:, :], zerob[:, :], start=True, stop=False, skip_group_check=True)

            def turn_norm(phase, b, cols):
                pe.wait_ge(d_nrm, B + NORMS.index((phase - 1, b)) + 1)
                k = TURNS.index((phase, b))
                for c in range(KC):
                    if k > B + 1 or (k == B + 1 and c == 0):
                        pe.wait_ge(d_xTl, (k - 1) * KC + c + 1)
                    for t in range(TPB):
                        last = pe.transpose(turn_bank(phase, b, c)[:, t * P:(t + 1) * P], nrm[:, b * TPB + t, cols(c)], identf[:, :])
                    last.then_inc(t_xT, 1)

            def x_parts(b, c):
                return [a[:, c, b * S:(b + 1) * S] for a in (xTh, xTl)]

            def even_odd(c):
                return slice(c, D, NIBBLES)

            def halves(c):
                return slice(c * P, (c + 1) * P)

            def look_up(s):
                pe.wait_ge(d_hot, s + 1)
                pe.wait_ge(d_lut, 4)
                if s >= 2:
                    pe.wait_ge(a_w2, s - 1)
                if s in (EARLY_LOOKUPS, EARLY_LOOKUPS + 1):
                    pe.wait_ge(d_acc, SUMS.index((2, 0)) + 1)
                n = CHUNKS[s // 2][1]
                for e in range(LUT // 2):
                    last = pe.matmul(side_bank[1 - s % 2][:, 0:n], spread[:, e, :], hot[s % 2][e][:, 0:n],
                                     start=e == 0, stop=e == LUT // 2 - 1)
                last.then_inc(t_lut, 1)

            def project1(b, i):
                f, w = i // 3, i % 3
                if i < 2:
                    pe.wait_ge(d_xTl, (TURNS.index((2, b)) + 1) * KC)
                else:
                    n, before = b * FT + (i - 2) // 3, (i - 2) % 3
                    if before == 2:
                        pe.wait_ge(d_kv, n + 1)
                    else:
                        pe.wait_ge(a_expo, 2 * n + before + 1)
                o = (w * FT + f) * P
                for c in range(KC):
                    last = product(side_bank[i % 2][:, :], [a[:, c, o:o + P] for a in (w1h, w1l)], x_parts(b, c),
                                   c == 0, c == KC - 1)
                last.then_inc(t_qkv, 1)

            def out_project1(b):
                pe.wait_ge(g_attl, FT * (b + 1))
                for t in range(TPB):
                    for f in range(FT):
                        parts = [a[f][:, t * P:(t + 1) * P] for a in (atth, attl)]
                        ws = [a[:, f, 3 * D:4 * D] for a in (w1h, w1l)]
                        last = product(side_bank[t // 2][:, t % 2 * D:t % 2 * D + D], parts, ws, f == 0, f == FT - 1)
                last.then_inc(t_out1, 1)

            def feed_forward(first_tile, tiles, b, before, weights, rows, beside):
                for m in range(tiles + 1):
                    n = first_tile + m
                    if m < tiles:
                        r = rows(m)
                        if n >= 2:
                            pe.wait_ge(a_gelu, n - 1)
                        for c in range(KC):
                            last = product(G_bank[n % 2][0:r, :], weights(0, m, c), x_parts(b, c), c == 0, c == KC - 1)
                        last.then_inc(t_gate, 1)
                        beside(2 * m)
                        if n >= 2:
                            pe.wait_ge(d_inter, n - 1)
                        for c in range(KC):
                            last = product(U_bank[n % 2][0:r, :], weights(1, m, c), x_parts(b, c), c == 0, c == KC - 1)
                        last.then_inc(t_up, 1)
                        beside(2 * m + 1)
                    else:
                        beside(2 * m)
                    if m:
                        r = rows(m - 1)
                        if m == 1:
                            pe.wait_ge(d_acc, SUMS.index(before) + 1)
                            open_sums()
                        pe.wait_ge(g_il, n)
                        ws = weights(2, m - 1, 0)
                        for t in range(TPB):
                            hs = [a[(n - 1) % 2][0:r, t * P:(t + 1) * P] for a in (ih, il)]
                            last = product(row_tile(t), hs, ws, False, False, skip=True)
                        last.then_inc(t_down, 1)

            def row_tile(t):
                return acc_bank[t // 2][:, t % 2 * D:t % 2 * D + D]

            def fp4_weights(b):
                def weights(w, m, c):
                    if b == 0 and m % 4 == 0 and c == 0:
                        pe.wait_ge(d_fl, NIBBLES * (m // 4 * 3 + w + 1))
                    if w < 2:
                        return [f[w][:, c, m * P:(m + 1) * P] for f in (fh, fl)]
                    return [f[2][:, m % NIBBLES, m // NIBBLES * D:(m // NIBBLES + 1) * D] for f in (fh, fl)]
                return weights

            def table_weights(w, m, c):
                if w < 2:
                    o = (c * 2 + w) * INTER + m * P
                    return [a[:, o:o + i_rows(m)] for a in (wh[3], wl[3])]
                return [a[0:i_rows(m), m * D:(m + 1) * D] for a in (w2dh, w2dl)]

            def beside_first(k):
                if k == 20:
                    turn_norm(1, 1, even_odd)

            def beside_second(k):
                if k == 9:
                    pe.wait_ge(a_w2, EARLY_LOOKUPS)
                    turn_norm(2, 0, halves)
                if k in (10, 11, 13, 14, 15, 17):
                    project1(0, (10, 11, 13, 14, 15, 17).index(k))
                if k == 21:
                    out_project1(0)
                if k < 2 * M_TILES and lookups_beside(k // 2):
                    look_up(lookups_beside(k // 2)[k % 2])
                if k == 2 * M_TILES:
                    pe.wait_ge(a_w2, LOOKUPS)
                    turn_norm(3, 0, halves)

            def beside_third(k):
                if k == 4:
                    turn_norm(2, 1, halves)
                for i, slot in enumerate((5, 5, 7, 7, 8, 10)):
                    if k == slot:
                        project1(1, i)

            def after(n):
                if n == HEADS + 2:
                    pe.wait_ge(d_acc, 1)
                    open_sums()
                if n == UNITS:
                    pe.wait_ge(a_qk, 2 * UNITS)
                    pe.wait_ge(a_exp, TPB * UNITS)
                    turn_norm(1, 0, even_odd)

            open_sums()
            pipeline(pe, step, after)

            pe.wait_ge(d_ol, UNITS)
            pe.wait_ge(d_xTl, (TURNS.index((1, 0)) + 1) * KC)
            feed_forward(0, M_TILES, 0, (0, 1), fp4_weights(0), lambda m: P, beside_first)
            pe.wait_ge(d_xTl, (TURNS.index((1, 1)) + 1) * KC)
            pe.wait_ge(g_wl, len(ALL_POOL_W))
            feed_forward(M_TILES, M_TILES, 1, (1, 0), fp4_weights(1), lambda m: P, beside_second)
            pe.wait_ge(d_xTl, (TURNS.index((3, 0)) + 1) * KC)
            feed_forward(B * M_TILES, I_TILES, 0, (1, 1), table_weights, i_rows, beside_third)
            out_project1(1)
            pe.wait_ge(d_acc, SUMS.index((2, 1)) + 1)
            turn_norm(3, 1, halves)
            pe.wait_ge(d_xTl, (TURNS.index((3, 1)) + 1) * KC)
            feed_forward(B * M_TILES + I_TILES, I_TILES, 1, (3, 0), table_weights, i_rows, lambda k: None)


def kernel(**inputs):
    import numpy as np
    import concourse.bacc as bacc
    from concourse.bass_utils import run_bass_kernel_spmd

    a = {k: np.asarray(v) for k, v in inputs.items()}
    f32 = np.float32
    theta = f32(1.0) / np.power(f32(10000.0), np.arange(0, DK, 2, dtype=f32) / f32(DK))
    angle = (np.arange(S, dtype=np.float32)[None, :] * np.concatenate([theta, theta])[:, None]).astype(np.float64)
    turned = np.where(np.arange(DK)[:, None] < DK // 2, 1.0, -1.0) * np.sin(angle)
    scale = 1.0 / np.sqrt(DK)
    ropes = np.stack([np.cos(angle) * scale, turned * scale, np.cos(angle), turned]).astype(np.float32)


    def by_hidden(w):
        rows = w.shape[0]
        return w.reshape(rows, MLP // (NIBBLES * P), P, NIBBLES).transpose(0, 1, 3, 2).reshape(rows, MLP)

    def by_row(w, rows):
        return w.reshape(-1, rows, w.shape[1]).transpose(1, 0, 2).reshape(rows, -1)

    gate_up = np.concatenate([a["L1_ffn_gate_idx"].T, a["L1_ffn_up_idx"].T], axis=1)
    down = np.concatenate([a["L1_ffn_down_idx"].T, np.zeros((I_TILES * P - INTER, D), a["L1_ffn_down_idx"].dtype)])
    arrays = {
        "x": a["L0_attn_h"],
        "wqT": a["L0_attn_wq"].T, "wkT": a["L0_attn_wk"].T, "wvT": a["L0_attn_wv"].T, "woT": a["L0_attn_wo"].T,
        "bqT": a["L0_attn_bq"].reshape(HEADS, DK).T, "bkT": a["L0_attn_bk"].reshape(HEADS, DK).T,
        "bvT": a["L0_attn_bv"].reshape(HEADS, DK).T, "bo": a["L0_attn_bo"],
        "gT": a["L0_attn_ln_g"].reshape(KC, P).T, "bT": a["L0_attn_ln_b"].reshape(KC, P).T,
        "ropes": ropes,
        "w1T": np.concatenate([a["L1_attn_W_qkv"].T, a["L1_attn_W_out"].T], axis=1),
        "packed": np.stack([by_hidden(a["L0_ffn_gate_W_packed"].T), by_hidden(a["L0_ffn_up_W_packed"].T),
                            by_row(a["L0_ffn_down_W_packed"].T, P)]),
        "scales": np.stack([by_hidden(a["L0_ffn_gate_scales"].T), by_hidden(a["L0_ffn_up_scales"].T),
                            by_row(a["L0_ffn_down_scales"].T, P // Q_ROWS)]),
        "codes": np.concatenate([by_row(gate_up, P), by_row(down, P)], axis=1),
        "lut": a["L1_ffn_lut"],
    }
    arrays = {f"in_{k}": np.ascontiguousarray(v) for k, v in arrays.items()}
    nc = bacc.Bacc("TRN2", target_bir_lowering=False, num_devices=1)
    args = [nc.dram_tensor(k, v.shape, mybir.dt.from_np(v.dtype), kind="ExternalInput").ap() for k, v in arrays.items()]
    args.append(nc.dram_tensor("out", (B, S, D), F32, kind="ExternalOutput").ap())
    sandwich(nc, *args)
    return run_bass_kernel_spmd(nc, [arrays], core_ids=[0]).results[0]["out"]
```

```python
from contextlib import ExitStack

import concourse.bass as bass
from concourse import mybir

ALU = mybir.AluOpType
ACT = mybir.ActivationFunctionType
AX_X = mybir.AxisListType.X
F32 = mybir.dt.float32
F16 = mybir.dt.float16
BF16 = mybir.dt.bfloat16
FP8 = mybir.dt.float8e4
I32 = mybir.dt.int32

P = 128
B, S, D = 2, 512, 256
TPB = S // P
PEELED = 7
KC = D // P
HEADS, DK = 16, 128
HD = HEADS * DK
LN_EPS = 1e-5
MASKED = -1e30

X_SCALE = 16.0
W_SCALE = 256.0
P_SCALE = 64.0
UNITS = B * HEADS
W_COLS = 1024
W_PIECES = 4 * HD * KC // W_COLS + 2
W_ORDER = (tuple((w, c * HD) for w in range(3) for c in range(KC)) + ((3, 0), (3, W_COLS))
           + tuple((w, c * HD + W_COLS) for w in range(3) for c in range(KC)) + ((3, 2 * W_COLS), (3, 3 * W_COLS))
           + ((4, 0), (4, W_COLS)))
QK_W = 2 * KC
FIRST_W = 3 * KC
DVE_W = ((), (6, 7), (9,), (10,), (12,), (14,), (15,), (), (), ())
POOL_W = ((), (), (8,), (), (11,), (13,), (), (), (16,), (17,))
RESIDUAL_STEPS = {3: 0, 7: 1}
ALL_POOL_W = sum(POOL_W, tuple(range(FIRST_W)))
MLP = 2048
M_TILES = MLP // P
NIBBLES = 2
Q_BLOCK = 32
Q_ROWS = Q_BLOCK // NIBBLES
Q_COLS = 512
Q_PIECES = 3 * MLP // Q_COLS
FP4_AS_FP8 = 64.0
DW = 1024
FT = D // P
ATT_SCALE = 16.0
CUM_EPS = 1e-9
OUT1_SCALE = (D // 16) ** -0.5
FFN_SCALE = 1 / W_SCALE
ATT1_SCALE = OUT1_SCALE / (ATT_SCALE * W_SCALE)
INTER = 688
I_TILES = -(-INTER // P)
LUT = 16
GU_COLS = KC * 2 * INTER
DOWN_COLS = I_TILES * D
HALF = P // 2
CHUNKS = tuple((c, min(512, GU_COLS - c)) for c in range(0, GU_COLS, 512)) + tuple(
    (GU_COLS + c, 512) for c in range(0, DOWN_COLS, 512))
LOOKUPS = 2 * len(CHUNKS)
LOOKUP_SLOTS = ((range(0, 4), 0), (range(9, 11), 8), (range(13, 16), 12))
SUMS = ((0, 0), (0, 1), (1, 0), (2, 0), (1, 1), (2, 1), (3, 0), (3, 1))
COPIED = ((0, 0), (0, 1), (2, 0), (3, 0))
NORMS = ((0, 0), (0, 1), (1, 0), (2, 0), (1, 1), (2, 1), (3, 0), (3, 1))
TURNS = ((0, 0), (0, 1), (1, 0), (1, 1), (2, 0), (3, 0), (2, 1), (3, 1))


def sandwich(nc, x_in, wqT, wkT, wvT, woT, bqT, bkT, bvT, bo, gT, bT, ropes, w1T, packed, scales, codes, lut, out):
    with ExitStack() as ctx:
        def sb(name, shape, dt):
            return ctx.enter_context(nc.sbuf_tensor(name, shape, dt))

        def sem(name):
            return ctx.enter_context(nc.semaphore(name))

        bank = [ctx.enter_context(nc.psum_tensor(f"bank{i}", [P, 512], F32)) for i in range(8)]
        acc_bank, S_bank, T_bank, proj_bank, o_bank = bank[0:2], bank[2:4], bank[4:6], bank[6], bank[7]

        x = sb("x", [P, B * TPB, D], F32)
        xa = sb("xa", [P, B * TPB, D], F32)
        nrm = sb("nrm", [P, B * TPB, D], F32)
        y = sb("y", [P, TPB, D], F32)
        stats = sb("stats", [P, TPB, 6], F32)
        mv = sb("mv", [P, TPB, 2], F32)
        std = sb("std", [P, TPB], F32)
        rstd = sb("rstd", [P, TPB], F32)
        eps_ln = sb("eps_ln", [P, 1], F32)
        eps_ffn = sb("eps_ffn", [P, 1], F32)
        eps_out1 = sb("eps_out1", [P, 1], F32)
        unread = sb("unread", [P, 1], F32)
        xT = sb("xT", [P, 2, S], F32)
        stage = sb("stage", [P, 4, W_COLS], F32)
        xTh = sb("xTh", [P, KC, B * S], F16)
        xTl = sb("xTl", [P, KC, B * S], F16)
        identf = sb("identf", [P, P], F32)
        identb = sb("identb", [P, P], BF16)
        maskb = sb("maskb", [P, P], BF16)
        zerob = sb("zerob", [P, 512], BF16)
        wh = [sb(f"w{n}h", [P, 4096], F16) for n in "qkvo"]
        wl = [sb(f"w{n}l", [P, 4096], F16) for n in "qkvo"]
        bias_q = sb("bias_q", [P, HEADS], F32)
        bias_k = sb("bias_k", [P, HEADS], F32)
        bias_v = sb("bias_v", [P, HEADS], F32)
        bo_row = sb("bo_row", [P, D], F32)
        ln_g = sb("ln_g", [P, KC], F32)
        ln_b = sb("ln_b", [P, KC], F32)
        rope = sb("rope", [P, 4, S], F32)
        w1h = sb("w1h", [P, KC, DW], F16)
        w1l = sb("w1l", [P, KC, DW], F16)
        raw = stage[:, 0:2, :].rearrange("p i n -> p (i n)").bitcast(I32).rearrange("p (i n) -> p i n", n=Q_COLS)
        scl = stage[:, 2:4, :].rearrange("p i n -> p (i n)").rearrange("p (i n) -> p i n", n=Q_COLS)
        sign = xT[:, 0, :].bitcast(I32)
        lut_row = sb("lut_row", [P, LUT], F32)
        w2dh = sb("w2dh", [P, DOWN_COLS], F16)
        w2dl = sb("w2dl", [P, DOWN_COLS], F16)
        lut_own = sb("lut_own", [P, LUT // 2], F32)
        lut_h = sb("lut_h", [P, LUT // 2], F16)
        lut_l = sb("lut_l", [P, LUT // 2], F16)
        entry = sb("entry", [P, LUT // 2], F32)
        twice = sb("twice", [P, HALF], F32)
        spread = sb("spread", [P, LUT // 2, P], F16)
        qf = sb("qf", [P, 2, S], F32)
        rc = sb("rc", [P, 2, S], F32)
        rs = sb("rs", [P, 2, S], F32)
        rr = sb("rr", [P, 2, S], F32)
        qkh = sb("qkh", [P, 2, 2, S], F16)
        qkl = sb("qkl", [P, 2, 2, S], F16)
        vh = sb("vh", [P, S], F16)
        vl = sb("vl", [P, S], F16)
        prob = sb("prob", [P, 2, TPB, S], F32)
        nmax = sb("nmax", [P, 2, TPB], F32)
        psum_row = sb("psum_row", [P, 2, TPB], F32)
        rinv = sb("rinv", [P, 2, TPB], F32)
        pTh = sb("pTh", [P, TPB, S], F16)
        pTl = sb("pTl", [P, TPB, S], F16)
        oh = sb("oh", [P, 2, S], F16)
        ol = sb("ol", [P, 2, S], F16)
        gel = qf
        inter = rc
        ih = [qkh[:, i, 0, :] for i in range(2)]
        il = [qkl[:, i, 0, :] for i in range(2)]
        G_bank, U_bank = S_bank, T_bank
        side_bank = bank[6:8]
        w32 = [rr, rs]
        bits = [prob[:, 0, 2 * i:2 * i + 2, :].bitcast(I32) for i in range(NIBBLES)]
        idx = xa[:, :, :].rearrange("p t n -> p (t n)").bitcast(I32).rearrange("p (i n) -> p i n", n=512)
        idx16 = xT[:, 1, :].bitcast(F16).rearrange("p (i n) -> p i n", n=512)
        rope16 = rope[:, :, :].rearrange("p f s -> p (f s)").bitcast(F16).rearrange("p (e n) -> p e n", n=512)
        r16 = [a[:, :, :].rearrange("p w s -> p (w s)").bitcast(F16).rearrange("p (e n) -> p e n", n=512) for a in (rr, rs)]
        hot = [[rope16[:, e, :] for e in range(LUT // 2)], [r16[e // 4][:, e % 4, :] for e in range(LUT // 2)]]
        neg, expo, pos, phi = ([a] * (B * FT - 1) + [z] for a, z in (
            (prob[:, 0, 0:2, :], rope[:, 0:2, :]), (prob[:, 0, 2:4, :], rope[:, 2:4, :]),
            (prob[:, 1, 0:2, :], rr), (prob[:, 1, 2:4, :], rs)))
        kv, kv_sum, k_sum, num, den, att, ones = [stage[:, i // 2, i % 2 * 512:(i % 2 + 1) * 512] for i in range(7)]
        atth = [pTh[:, i, :] for i in range(FT)]
        attl = [pTl[:, i, :] for i in range(FT)]
        fh = [w[:, :].rearrange("p (c n) -> p c n", c=NIBBLES) for w in wh[0:3]]
        fl = [w[:, :].rearrange("p (c n) -> p c n", c=NIBBLES) for w in wl[0:3]]

        s_x = [sem("s_x0"), sem("s_x1")]
        s_small = sem("s_small")
        s_rope = sem("s_rope")
        s_bo = sem("s_bo")
        g_wl = sem("g_wl")
        s_w = [sem(f"s_w{i}") for i in range(4)]
        s_out = sem("s_out")
        s_raw = [sem(f"s_raw{i}") for i in range(4)]
        s_idx = [sem(f"s_idx{i}") for i in range(4)]
        s_lut = sem("s_lut")
        d_bits = sem("d_bits")
        a_fh = sem("a_fh")
        d_fl = sem("d_fl")
        g_w32 = sem("g_w32")
        d_lut = sem("d_lut")
        d_idx16 = sem("d_idx16")
        d_hot = sem("d_hot")
        t_lut = sem("t_lut")
        a_w2 = sem("a_w2")
        g_twice = sem("g_twice")
        d_entry = sem("d_entry")
        t_gate = sem("t_gate")
        t_up = sem("t_up")
        t_down = sem("t_down")
        a_gelu = sem("a_gelu")
        d_inter = sem("d_inter")
        a_ih = sem("a_ih")
        g_il = sem("g_il")
        t_qkv = sem("t_qkv")
        d_neg = sem("d_neg")
        a_pos = sem("a_pos")
        a_expo = sem("a_expo")
        g_phi = sem("g_phi")
        d_kv = sem("d_kv")
        d_cum = sem("d_cum")
        g_num = sem("g_num")
        d_den = sem("d_den")
        d_att = sem("d_att")
        a_atth = sem("a_atth")
        g_attl = sem("g_attl")
        t_out1 = sem("t_out1")
        g_const = sem("g_const")
        g_ident = sem("g_ident")
        d_bn = sem("d_bn")
        d_var = sem("d_var")
        a_std = sem("a_std")
        d_rstd = sem("d_rstd")
        d_z = sem("d_z")
        d_nrm = sem("d_nrm")
        d_vec = sem("d_vec")
        g_res = sem("g_res")
        t_xT = sem("t_xT")
        d_xT = sem("d_xT")
        a_xTh = sem("a_xTh")
        d_xTl = sem("d_xTl")
        a_wh = sem("a_wh")
        d_wl = sem("d_wl")
        t_qk = sem("t_qk")
        t_v = sem("t_v")
        t_S = sem("t_S")
        t_T = sem("t_T")
        t_pv = sem("t_pv")
        t_op = sem("t_op")
        a_qk = sem("a_qk")
        a_exp = sem("a_exp")
        a_Th = sem("a_Th")
        a_qkh = sem("a_qkh")
        a_vh = sem("a_vh")
        a_oh = sem("a_oh")
        d_max = sem("d_max")
        d_sin = sem("d_sin")
        d_Tl = sem("d_Tl")
        d_vl = sem("d_vl")
        d_rinv = sem("d_rinv")
        d_ol = sem("d_ol")
        d_acc = sem("d_acc")
        d_y = sem("d_y")
        d_x = sem("d_x")
        d_prob = sem("d_prob")
        g_cos = sem("g_cos")
        g_rot = sem("g_rot")
        g_qkl = sem("g_qkl")

        x_tok = x_in.rearrange("b (t p) d -> p (b t) d", p=P)
        out_tok = out.rearrange("b (t p) d -> p (b t) d", p=P)
        w1_dram = w1T.rearrange("(c p) n -> p c n", p=P)
        w_dram = [w.rearrange("(c p) n -> p c n", p=P) for w in (wqT, wkT, wvT, woT)]

        def w_piece(j):
            return W_ORDER[j]

        def w_high(j):
            w, c0 = w_piece(j)
            return wh[w][:, c0:c0 + W_COLS] if w < 4 else w1h[:, c0 // DW, :]

        def w_low(j):
            w, c0 = w_piece(j)
            return wl[w][:, c0:c0 + W_COLS] if w < 4 else w1l[:, c0 // DW, :]

        def lows_before(j):
            g = sum(i in ALL_POOL_W for i in range(j))
            return j - g, g

        def q_piece(j):
            c0 = j // 3 * Q_COLS
            return j % 3, slice(c0, c0 + Q_COLS)

        def lookup(s):
            c0, n = CHUNKS[s // 2]
            rows = slice(s % 2 * HALF, (s % 2 + 1) * HALF)
            if c0 < GU_COLS:
                return c0, n, rows, wh[3][rows, c0:c0 + n], wl[3][rows, c0:c0 + n]
            return c0, n, rows, w2dh[rows, c0 - GU_COLS:c0 - GU_COLS + n], w2dl[rows, c0 - GU_COLS:c0 - GU_COLS + n]

        def lookups_beside(m):
            for slots, first_lookup in LOOKUP_SLOTS:
                if m in slots:
                    s = first_lookup + 2 * (m - slots[0])
                    return s, s + 1
            return ()

        def unpack_beside(m):
            j = 3 * (m // 4 + 1) + m % 4
            return j if m % 4 < 3 and j < Q_PIECES else None

        def y_event(phase, b):
            k = NORMS.index((phase, b))
            return 2 * B + 2 * k - (b if phase == 3 else 0)

        def turn_bank(phase, b, c):
            return (proj_bank, S_bank[0])[c] if (phase, b) == (1, 0) else side_bank[c]

        def qkv_bank(n, w):
            return side_bank[(3 * (n % FT) + w) % 2]

        def i_rows(m):
            return min(P, INTER - m * P)

        def straight(cur, n):
            return cur is not None and isinstance(cur[2], int) and cur[2] == n

        def preparation(cur):
            if cur is None:
                return None
            n = cur[2]
            steps = {**{h: h + 1 for h in range(PEELED)}, HEADS: PEELED + 1, HEADS + 1: PEELED + 2}
            return steps.get(n) if isinstance(n, int) else None

        def early(n):
            return isinstance(n, int) and n < 2

        def first(n):
            return isinstance(n, int) and n == 0

        block = ctx.enter_context(nc.Block())

        def pipeline(eng, step, after):
            def unit(n):
                return (n // HEADS, n % HEADS, n, n % 2) if 0 <= n < UNITS else None

            def around(n):
                return unit(n), unit(n + 1), unit(n - 1), unit(n - 2), unit(n - 3)

            step(*around(-1))
            for b in range(B):
                for h in range(PEELED):
                    step(*around(b * HEADS + h))
                    after(b * HEADS + h)
                with eng.Fori(PEELED, HEADS - 2, 2) as i:
                    for j in range(2):
                        step(*((b, i + k, i + (b * HEADS + k), (k + 1) % 2) for k in (j, j + 1, j - 1, j - 2, j - 3)))
                step(*around((b + 1) * HEADS - 1))
                after((b + 1) * HEADS - 1)
            for n in range(UNITS, UNITS + 3):
                step(*around(n))
                after(n)

        @block.sync
        def _(sp):
            for b in range(B):
                sp.dma_start(x[:, b * TPB:(b + 1) * TPB, :], x_tok[:, b * TPB:(b + 1) * TPB, :]).then_inc(s_x[b], 16)
            for dst, src in ((ln_g, gT), (ln_b, bT), (bias_q, bqT), (bias_k, bkT), (bias_v, bvT)):
                sp.dma_start(dst[:, :], src).then_inc(s_small, 16)
            for j in range(W_PIECES):
                w, c0 = w_piece(j)
                if j >= 4:
                    by_dve, by_pool = lows_before(j - 3)
                    if j - 4 in ALL_POOL_W:
                        sp.wait_ge(g_wl, by_pool)
                    else:
                        sp.wait_ge(d_wl, by_dve)
                if w == 4:
                    src = w1_dram[:, c0 // DW, :]
                    dst = stage[:, j % 4, :]
                elif w < 3:
                    src = w_dram[w][:, c0 // HD, c0 % HD:c0 % HD + W_COLS]
                    dst = stage[:, j % 4, :]
                else:
                    src = w_dram[w][:, c0 // D:(c0 + W_COLS) // D, :]
                    dst = stage[:, j % 4, :].rearrange("p (h n) -> p h n", n=D)
                sp.dma_start(dst, src).then_inc(s_w[j % 4], 16)
                if j == 3:
                    sp.dma_start(rope[:, :, :], ropes.rearrange("f p s -> p f s")).then_inc(s_rope, 16)
                    sp.dma_start(bo_row[:, :], bo.partition_broadcast(P)).then_inc(s_bo, 16)
            sp.dma_start(lut_row[:, :], lut.partition_broadcast(P)).then_inc(s_lut, 16)
            by_dve, by_pool = lows_before(W_PIECES)
            sp.wait_ge(d_wl, by_dve)
            sp.wait_ge(g_wl, by_pool)
            for j in range(Q_PIECES):
                w, cols = q_piece(j)
                if j >= 4:
                    sp.wait_ge(g_w32, NIBBLES * (j - 3))
                sp.dma_start(raw[:, j % 4, :], packed[w, :, cols]).then_inc(s_raw[j % 4], 16)
                for g in range(P // Q_ROWS):
                    sp.dma_start(scl[g * Q_ROWS:(g + 1) * Q_ROWS, j % 4, :],
                                 scales[w, g, cols].partition_broadcast(Q_ROWS)).then_inc(s_raw[j % 4], 16)
            sp.wait_ge(d_acc, B)
            for s in range(LOOKUPS):
                if s >= 4:
                    sp.wait_ge(d_idx16, s - 3)
                c0, n, rows, _, _ = lookup(s)
                for h in range(2):
                    sp.dma_start(idx[h * HALF:(h + 1) * HALF, s % 4, 0:n], codes[rows, c0:c0 + n]).then_inc(s_idx[s % 4], 16)
            for b in range(B):
                sp.wait_ge(d_x, NORMS.index((3, b)) + 1)
                sp.dma_start(out_tok[:, b * TPB:(b + 1) * TPB, :], x[:, b * TPB:(b + 1) * TPB, :]).then_inc(s_out, 16)
            sp.wait_ge(s_out, 16 * B)

        @block.gpsimd
        def _(pool):
            pool.memset(identf[:, :], 0.0).then_inc(g_const, 1)
            pool.memset(identb[:, :], 0.0).then_inc(g_const, 1)
            pool.memset(maskb[:, :], 0.0).then_inc(g_const, 1)
            pool.memset(eps_ln[:, :], LN_EPS).then_inc(g_const, 1)
            pool.memset(eps_ffn[:, :], LN_EPS / FFN_SCALE ** 2).then_inc(g_const, 1)
            pool.memset(eps_out1[:, :], LN_EPS / ATT1_SCALE ** 2).then_inc(g_const, 1)
            pool.memset(zerob[:, :], 0.0).then_inc(g_const, 1)
            pool.wait_ge(g_const, 7)
            for m in (identf, identb):
                pool.affine_select(out=m[:, :], in_=m[:, :], compare_op=ALU.not_equal, fill=1.0, base=0,
                                   pattern=[[-1, P]], channel_multiplier=1).then_inc(g_ident, 1)
            pool.affine_select(out=maskb[:, :], in_=maskb[:, :], compare_op=ALU.is_ge, fill=MASKED, base=0,
                               pattern=[[-1, P]], channel_multiplier=1).then_inc(g_ident, 1)
            pool.wait_ge(g_ident, 3)
            pool.tensor_tensor(twice[:, :], identf[:, 0:HALF], identf[:, HALF:P], ALU.add).then_inc(g_twice, 1)

            def low_w(j):
                pool.wait_ge(a_wh, j + 1)
                pool.tensor_tensor(w_low(j), stage[:, j % 4, :], w_high(j), ALU.subtract).then_inc(g_wl, 1)

            def residual(b):
                pool.wait_ge(s_bo, 16)
                pool.wait_ge(d_nrm, b + 1)
                for t in range(b * TPB, (b + 1) * TPB):
                    last = pool.tensor_tensor(xa[:, t, :], xa[:, t, :], bo_row[:, :], ALU.add)
                last.then_inc(g_res, 1)

            def prepare(k):
                for j in POOL_W[k]:
                    low_w(j)
                if k in RESIDUAL_STEPS:
                    residual(RESIDUAL_STEPS[k])

            for j in range(FIRST_W):
                low_w(j)
            pool.wait_ge(s_rope, 16)

            def step(cur, nxt, prev, prev2, prev3):
                if nxt:
                    b, h, u, p = nxt
                    for w in range(2):
                        pool.wait_ge(a_qk, 2 * u + (w + 1))
                        pool.tensor_tensor(rc[:, w, :], qf[:, w, :], rope[:, 2 * w, :], ALU.mult).then_inc(g_cos, 1)
                        pool.wait_ge(g_cos, 2 * u + (w + 1))
                        pool.wait_ge(d_sin, 2 * u + (w + 1))
                        pool.tensor_tensor(rr[:, w, :], rc[:, w, :], rs[:, w, :], ALU.add).then_inc(g_rot, 1)
                    for w in range(2):
                        pool.wait_ge(a_qkh, 2 * u + (w + 1))
                        pool.tensor_tensor(qkl[:, p, w, :], rr[:, w, :], qkh[:, p, w, :], ALU.subtract).then_inc(g_qkl, 1)
                    if preparation(cur) is not None:
                        prepare(preparation(cur))

            def scaled(j):
                pool.wait_ge(d_bits, 2 * j + 2)
                if j >= 2:
                    pool.wait_ge(d_fl, NIBBLES * (j - 1))
                for c in range(NIBBLES):
                    code = bits[j % 2][:, c, :].bitcast(FP8).rearrange("p (n e) -> p n e", e=4)[:, :, 0]
                    pool.tensor_tensor(w32[j % 2][:, c, :], code, scl[:, j % 4, :], ALU.mult).then_inc(g_w32, 1)

            def low_inter(n, rows=P):
                pool.wait_ge(a_ih, n + 1)
                pool.tensor_tensor(il[n % 2][0:rows, :], inter[0:rows, n % 2, :], ih[n % 2][0:rows, :],
                                   ALU.subtract).then_inc(g_il, 1)

            def features(n):
                for w in range(2):
                    pool.wait_ge(a_expo, 2 * n + w + 1)
                    pool.tensor_tensor(phi[n][:, w, :], pos[n][:, w, :], expo[n][:, w, :], ALU.add).then_inc(g_phi, 1)

            def numerator(n):
                pool.wait_ge(d_cum, n + 1)
                pool.tensor_tensor(num, phi[n][:, 0, :], kv_sum, ALU.mult).then_inc(g_num, 1)

            def low_att(n):
                pool.wait_ge(a_atth, n + 1)
                pool.tensor_tensor(attl[n % FT], att, atth[n % FT], ALU.subtract).then_inc(g_attl, 1)

            def after(n):
                if n == UNITS:
                    pool.wait_ge(g_qkl, 2 * UNITS)
                    for j in range(3):
                        scaled(j)

            pipeline(pool, step, after)
            for m in range(M_TILES):
                low_inter(m)
                if unpack_beside(m):
                    scaled(unpack_beside(m))
            for m in range(M_TILES):
                low_inter(M_TILES + m)
                if m == 5:
                    features(0)
                if m == 6:
                    numerator(0)
                if m == 7:
                    low_att(0)
                    features(1)
                if m == 8:
                    numerator(1)
                if m == 9:
                    low_att(1)
            for m in range(I_TILES):
                if m == 2:
                    features(FT)
                if m == 4:
                    low_att(FT)
                if m == 5:
                    numerator(FT + 1)
                    low_att(FT + 1)
                low_inter(B * M_TILES + m, i_rows(m))
                if m == 3:
                    numerator(FT)
                    features(FT + 1)
            for m in range(I_TILES):
                low_inter(B * M_TILES + I_TILES + m, i_rows(m))

        @block.scalar
        def _(act):
            def std_of(event, eps=eps_ln):
                act.wait_ge(d_var, event + 1)
                act.activation(std[:, :], mv[:, :, 1], ACT.Sqrt, bias=eps[:, 0:1]).then_inc(a_std, 1)

            def std_y(phase, b):
                std_of(y_event(phase, b), eps_ln if (phase, b) in COPIED else eps_out1 if phase == 2 else eps_ffn)

            def std_x(phase, b):
                std_of(y_event(phase, b) + 1)

            act.wait_ge(g_const, 7)
            def high_xT0(b):
                for c in range(KC):
                    act.wait_ge(d_xT, b * KC + c + 1)
                    act.activation(xTh[:, c, b * S:(b + 1) * S], xT[:, c, :], ACT.Copy).then_inc(a_xTh, 1)

            def high_w(j):
                act.wait_ge(s_w[j % 4], 16 * (j // 4 + 1))
                last = act.activation(w_high(j), stage[:, j % 4, :], ACT.Copy, scale=W_SCALE)
                if j in ALL_POOL_W:
                    last = act.activation(stage[:, j % 4, :], stage[:, j % 4, :], ACT.Copy, scale=W_SCALE)
                last.then_inc(a_wh, 1)

            def prepare(k):
                for j in sorted(DVE_W[k] + POOL_W[k]):
                    high_w(j)

            def table(func):
                act.activation(unread[:, :], eps_ln[:, :], func)

            table(ACT.Sqrt)
            std_of(0)
            high_w(0)
            high_w(1)
            std_of(1)
            high_w(2)
            high_w(3)
            high_xT0(0)
            for j in range(QK_W, FIRST_W):
                high_w(j)
            std_of(2)

            def step(cur, nxt, prev, prev2, prev3):
                def take(w):
                    b, h, u, p = nxt
                    act.wait_ge(t_qk, 2 * u + (w + 1))
                    if not first(u):
                        act.wait_ge(g_rot, 2 * u + (w - 1))
                    act.activation(qf[:, w, :], proj_bank[:, :], ACT.Identity, scale=1 / (X_SCALE * W_SCALE),
                                   bias=(bias_q, bias_k)[w][:, bass.ds(h, 1)]).then_inc(a_qk, 1)

                def exp(q):
                    b, h, u, p = cur
                    n = (q + 1) * P
                    act.wait_ge(d_max, 4 * u + (q + 1))
                    act.activation(prob[:, p, q, 0:n], S_bank[q % 2][:, 0:n], ACT.Exp, bias=nmax[:, p, q:q + 1],
                                   accum_out=psum_row[:, p, q:q + 1]).then_inc(a_exp, 1)

                def high_T(q):
                    b, h, u, p = prev
                    act.wait_ge(t_T, 4 * u + (q + 1))
                    act.activation(pTh[:, 0:q + 1, q * P:(q + 1) * P],
                                   T_bank[q % 2][:, 0:(q + 1) * P].rearrange("p (k n) -> p k n", n=P),
                                   ACT.Copy).then_inc(a_Th, 1)

                def high_qk(w):
                    b, h, u, p = nxt
                    act.wait_ge(g_rot, 2 * u + (w + 1))
                    act.activation(qkh[:, p, w, :], rr[:, w, :], ACT.Copy).then_inc(a_qkh, 1)

                if nxt:
                    take(0)
                if preparation(cur) not in (None, 1):
                    prepare(preparation(cur))
                if straight(cur, HEADS + 4):
                    std_y(0, 0)
                if straight(cur, HEADS + 6):
                    std_x(0, 0)
                if nxt:
                    take(1)
                if cur:
                    exp(0)
                    exp(1)
                if not cur and not prev and nxt:
                    std_of(3)
                    table(ACT.Exp)
                if prev2:
                    b, h, u, p = prev2
                    act.wait_ge(t_pv, u + 1)
                    if not early(u):
                        act.wait_ge(t_op, 2 * u - 2)
                    act.activation(oh[:, p, :], o_bank[:, :], ACT.Identity, bias=bias_v[:, bass.ds(h, 1)]).then_inc(a_oh, 1)
                if prev:
                    high_T(0)
                    high_T(1)
                if nxt:
                    high_qk(0)
                    high_qk(1)
                if cur:
                    exp(2)
                    exp(3)
                if preparation(cur) == 1:
                    prepare(1)
                if prev:
                    high_T(2)
                    b, h, u, p = prev
                    act.wait_ge(t_v, u + 1)
                    act.activation(vh[:, :], o_bank[:, :], ACT.Copy, scale=1 / (X_SCALE * W_SCALE)).then_inc(a_vh, 1)
                    high_T(3)
                if not cur and not prev and nxt:
                    high_xT0(1)
                    prepare(0)

            def high_fp4(j):
                w, cols = q_piece(j)
                for c in range(NIBBLES):
                    act.wait_ge(g_w32, NIBBLES * j + c + 1)
                    act.activation(fh[w][:, c, cols], w32[j % 2][:, c, :], ACT.Copy, scale=W_SCALE * FP4_AS_FP8).then_inc(a_fh, 1)

            def high_xT(phase, b):
                for c in range(KC):
                    act.wait_ge(t_xT, TURNS.index((phase, b)) * KC + c + 1)
                    act.activation(xTh[:, c, b * S:(b + 1) * S], turn_bank(phase, b, c)[:, :], ACT.Copy, scale=X_SCALE).then_inc(a_xTh, 1)

            def looked_up(s):
                c0, n, rows, w_h, w_l = lookup(s)
                act.wait_ge(t_lut, s + 1)
                act.activation(w_h, side_bank[1 - s % 2][0:HALF, 0:n], ACT.Copy)
                act.activation(w_l, side_bank[1 - s % 2][HALF:P, 0:n], ACT.Copy).then_inc(a_w2, 1)

            def gated(n, func, rows=P, between=lambda: None):
                act.wait_ge(t_gate, n + 1)
                if n >= 2:
                    act.wait_ge(d_inter, n - 1)
                act.activation(gel[0:rows, n % 2, :], G_bank[n % 2][0:rows, :], func,
                               scale=1 / (X_SCALE * W_SCALE)).then_inc(a_gelu, 1)
                between()
                act.wait_ge(d_inter, n + 1)
                if n >= 2:
                    act.wait_ge(t_down, n - 1)
                act.activation(ih[n % 2][0:rows, :], inter[0:rows, n % 2, :], ACT.Copy).then_inc(a_ih, 1)

            def exponents(n):
                for w in range(2):
                    act.wait_ge(t_qkv, 3 * n + w + 1)
                    if n:
                        act.wait_ge(g_phi, 2 * (n - 1) + w + 1)
                    act.activation(pos[n][:, w, :], qkv_bank(n, w)[:, :], ACT.Relu, scale=1 / (X_SCALE * W_SCALE)).then_inc(a_pos, 1)
                for w in range(2):
                    act.wait_ge(d_neg, 2 * n + w + 1)
                    act.activation(expo[n][:, w, :], neg[n][:, w, :], ACT.Exp, scale=1 / (X_SCALE * W_SCALE)).then_inc(a_expo, 1)

            def high_att(n):
                act.wait_ge(d_att, n + 1)
                if n >= FT:
                    act.wait_ge(t_out1, n // FT)
                act.activation(atth[n % FT], att, ACT.Copy).then_inc(a_atth, 1)

            def after(n):
                if n == UNITS + 1:
                    act.wait_ge(t_qk, 2 * UNITS)
                    act.wait_ge(t_v, UNITS)
                    high_fp4(0)
                    high_xT(1, 0)
                    high_fp4(1)

            act.wait_ge(d_vec, 3)
            pipeline(act, step, after)

            def beside_first(m):
                if m == 0:
                    high_fp4(2)
                if m == 2:
                    std_y(0, 1)
                if m == 9:
                    std_x(0, 1)

            def beside_second(m):
                if m == 1:
                    std_x(1, 0)
                if m == 12:
                    std_y(2, 0)
                if m == 13:
                    std_x(2, 0)

            def beside_third(m):
                if m == 0:
                    std_y(1, 1)
                if m == 1:
                    std_x(1, 1)
                if m == 2:
                    high_xT(2, 1)
                    exponents(FT)
                if m == 4:
                    high_att(FT)
                if m == 5:
                    high_att(FT + 1)

            def beside_fourth(m):
                if m == 1:
                    std_y(3, 0)

            for m in range(M_TILES):
                gated(m, ACT.Gelu_apprx_tanh, P, lambda: beside_first(m))
                if m and unpack_beside(m - 1):
                    high_fp4(unpack_beside(m - 1))
                if m == 13:
                    high_xT(1, 1)
            for m in range(M_TILES):
                gated(M_TILES + m, ACT.Gelu_apprx_tanh, P, lambda: beside_second(m))
                if m == 0:
                    std_y(1, 0)
                if m == 4:
                    high_xT(2, 0)
                if m == 5:
                    exponents(0)
                if m == 7:
                    high_att(0)
                    exponents(1)
                if m == 9:
                    high_att(1)
                for s in lookups_beside(m):
                    looked_up(s)
                if m == M_TILES - 1:
                    high_xT(3, 0)
            for m in range(I_TILES):
                gated(B * M_TILES + m, ACT.Silu, i_rows(m), lambda: beside_third(m))
                if m == 3:
                    exponents(FT + 1)
            std_y(2, 1)
            std_x(2, 1)
            high_xT(3, 1)
            for m in range(I_TILES):
                gated(B * M_TILES + I_TILES + m, ACT.Silu, i_rows(m), lambda: beside_fourth(m))
            std_y(3, 1)

        @block.vector
        def _(dve):
            for e in range(LUT // 2):
                for h in range(2):
                    dve.memset(entry[h * HALF:(h + 1) * HALF, e:e + 1], float(2 * e + h)).then_inc(d_entry, 1)
            dve.wait_ge(d_entry, LUT)

            def spread_of(event, src):
                for t in range(TPB):
                    last = dve.bn_stats(stats[:, t, :], src[t])
                last.then_inc(d_bn, 1)
                dve.wait_ge(d_bn, event + 1)
                for t in range(TPB):
                    last = dve.bn_aggr(mv[:, t, :], stats[:, t, :])
                last.then_inc(d_var, 1)

            def rstd_of(event):
                dve.wait_ge(a_std, event + 1)
                dve.reciprocal(rstd[:, :], std[:, :]).then_inc(d_rstd, 1)
                dve.wait_ge(d_rstd, event + 1)

            def normalised(dst, src):
                for t in range(TPB):
                    last = dve.tensor_scalar(dst[t], src[t], mv[:, t, 0:1], rstd[:, t:t + 1], ALU.subtract, ALU.mult)
                return last

            def row_tiles(a, b):
                return [a[:, b * TPB + t, :] for t in range(TPB)]

            def first_norm(b):
                dve.wait_ge(s_x[b], 16)
                spread_of(2 * b, row_tiles(x, b))
                rstd_of(2 * b)
                normalised(row_tiles(xa, b), row_tiles(x, b)).then_inc(d_z, 1)

            def second_spread(b):
                dve.wait_ge(d_z, b + 1)
                spread_of(2 * b + 1, row_tiles(xa, b))

            def second_norm(b):
                rstd_of(2 * b + 1)
                normalised(row_tiles(nrm, b), row_tiles(xa, b)).then_inc(d_nrm, 1)

            def both_xT0(b):
                for c in range(KC):
                    n = b * KC + c
                    dve.wait_ge(t_xT, n + 1)
                    dve.tensor_scalar(xT[:, c, :], T_bank[c][:, :], ln_g[:, c:c + 1], ln_b[:, c:c + 1],
                                      ALU.mult, ALU.add).then_inc(d_xT, 1)
                for c in range(KC):
                    dve.wait_ge(a_xTh, b * KC + c + 1)
                    dve.tensor_tensor(xTl[:, c, b * S:(b + 1) * S], xT[:, c, :], xTh[:, c, b * S:(b + 1) * S],
                                      ALU.subtract).then_inc(d_xTl, 1)

            def prepare(k):
                for j in DVE_W[k]:
                    dve.wait_ge(a_wh, j + 1)
                    dve.scalar_tensor_tensor(out=w_low(j), in0=stage[:, j % 4, :], scalar=W_SCALE, in1=w_high(j),
                                             op0=ALU.mult, op1=ALU.subtract).then_inc(d_wl, 1)

            first_norm(0)
            second_spread(0)
            second_norm(0)
            dve.wait_ge(s_small, 16 * 5)
            for v, scale in ((ln_g, X_SCALE), (ln_b, X_SCALE), (bias_v, P_SCALE)):
                dve.tensor_scalar(v[:, :], v[:, :], scale, None, ALU.mult).then_inc(d_vec, 1)
            dve.wait_ge(d_vec, 3)
            both_xT0(0)
            first_norm(1)
            dve.wait_ge(s_rope, 16)

            def unpacked(j):
                r, (low, high) = raw[:, j % 4, :], (bits[j % 2][:, c, :] for c in range(NIBBLES))
                dve.wait_ge(s_raw[j % 4], 16 * (1 + P // Q_ROWS) * (j // 4 + 1))
                if j >= 2:
                    dve.wait_ge(g_w32, NIBBLES * (j - 1))
                if j:
                    dve.wait_ge(d_bits, 2 * j)
                dve.tensor_scalar(low, r, 2, 0x1C, ALU.logical_shift_left, ALU.bitwise_and)
                dve.tensor_scalar(high, r, 2, 0x1C, ALU.logical_shift_right, ALU.bitwise_and)
                dve.tensor_scalar(sign, r, 4, 0x80, ALU.logical_shift_left, ALU.bitwise_and).then_inc(d_bits, 1)

            def signed(j):
                r, (low, high) = raw[:, j % 4, :], (bits[j % 2][:, c, :] for c in range(NIBBLES))
                dve.wait_ge(d_bits, 2 * j + 1)
                dve.tensor_tensor(low, low, sign, ALU.bitwise_or)
                dve.scalar_tensor_tensor(out=high, in0=r, scalar=0x80, in1=high,
                                         op0=ALU.bitwise_and, op1=ALU.bitwise_or).then_inc(d_bits, 1)

            def step(cur, nxt, prev, prev2, prev3):
                def top(q):
                    b, h, u, p = cur
                    dve.wait_ge(t_S, 4 * u + (q + 1))
                    dve.tensor_reduce(nmax[:, p, q:q + 1], S_bank[q % 2][:, 0:(q + 1) * P], AX_X, ALU.max,
                                      negate=True).then_inc(d_max, 1)

                def rotate(w):
                    b, h, u, p = nxt
                    dve.wait_ge(a_qk, 2 * u + (w + 1))
                    if not first(u):
                        dve.wait_ge(g_rot, 2 * u + (w - 1))
                    half = DK // 2
                    dve.tensor_tensor(rs[0:half, w, :], qf[half:DK, w, :], rope[half:DK, 2 * w + 1, :], ALU.mult)
                    dve.tensor_tensor(rs[half:DK, w, :], qf[0:half, w, :], rope[0:half, 2 * w + 1, :],
                                      ALU.mult).then_inc(d_sin, 1)

                def low_T(q):
                    b, h, u, p = prev
                    dve.wait_ge(a_Th, 4 * u + (q + 1))
                    dve.tensor_tensor(pTl[:, 0:q + 1, q * P:(q + 1) * P],
                                      T_bank[q % 2][:, 0:(q + 1) * P].rearrange("p (k n) -> p k n", n=P),
                                      pTh[:, 0:q + 1, q * P:(q + 1) * P], ALU.subtract).then_inc(d_Tl, 1)

                if nxt:
                    rotate(0)
                    if not cur and not prev:
                        second_spread(1)
                if prev:
                    b, h, u, p = prev
                    dve.wait_ge(a_exp, 4 * u + 4)
                    dve.reciprocal(rinv[:, p, :], psum_row[:, p, :]).then_inc(d_rinv, 1)
                    dve.wait_ge(d_rinv, u + 1)
                    for q in range(TPB):
                        row = prob[:, p, q, 0:(q + 1) * P]
                        dve.tensor_scalar(row, row, rinv[:, p, q:q + 1], P_SCALE, ALU.mult, ALU.mult).then_inc(d_prob, 1)
                if cur:
                    top(0)
                    top(1)
                if nxt:
                    rotate(1)
                    if not cur and not prev:
                        second_norm(1)
                if straight(prev, UNITS - 1):
                    unpacked(0)
                if prev:
                    low_T(0)
                if prev2:
                    b, h, u, p = prev2
                    dve.wait_ge(a_oh, u + 1)
                    dve.scalar_tensor_tensor(out=ol[:, p, :], in0=o_bank[:, :], scalar=bias_v[:, bass.ds(h, 1)],
                                             in1=oh[:, p, :], op0=ALU.add, op1=ALU.subtract).then_inc(d_ol, 1)
                if prev:
                    low_T(1)
                if cur:
                    top(2)
                    top(3)
                if preparation(cur) is not None:
                    prepare(preparation(cur))
                if straight(cur, HEADS + 2):
                    attention_sums(0)
                if straight(cur, HEADS + 3):
                    spread_of(y_event(0, 0), block_out(0, 0))
                if straight(cur, HEADS + 4):
                    add(0, 0)
                if straight(cur, HEADS + 5):
                    spread_of_x(0, 0)
                if straight(cur, HEADS + 6):
                    norm(0, 0)
                if prev:
                    low_T(2)
                    if straight(prev, UNITS - 1):
                        signed(0)
                    b, h, u, p = prev
                    dve.wait_ge(a_vh, u + 1)
                    dve.scalar_tensor_tensor(out=vl[:, :], in0=o_bank[:, :], scalar=1 / (X_SCALE * W_SCALE),
                                             in1=vh[:, :], op0=ALU.mult, op1=ALU.subtract).then_inc(d_vl, 1)
                    low_T(3)
                if not cur and not prev and nxt:
                    both_xT0(1)
                    prepare(0)

            def row_tile(banks, t):
                return banks[t // 2][:, t % 2 * D:t % 2 * D + D]

            def block_out(phase, b):
                if (phase, b) not in COPIED:
                    return [row_tile(side_bank if phase == 2 else acc_bank, t) for t in range(TPB)]
                src = nrm if (phase, b) == (3, 0) else y
                return [src[:, t, :] for t in range(TPB)]

            def take_sums(phase, b, banks, scale):
                for t, dst in enumerate(block_out(phase, b)):
                    if phase:
                        last = dve.tensor_scalar(dst, row_tile(banks, t), scale, None, ALU.mult)
                    else:
                        last = dve.scalar_tensor_tensor(out=dst, in0=row_tile(banks, t), scalar=scale,
                                                        in1=xa[:, b * TPB + t, :], op0=ALU.mult, op1=ALU.add)
                last.then_inc(d_acc, 1)
                dve.wait_ge(d_acc, SUMS.index((phase, b)) + 1)

            def add(phase, b):
                k = NORMS.index((phase, b))
                rstd_of(y_event(phase, b))
                last = normalised([y[:, t, :] for t in range(TPB)], block_out(phase, b))
                if (phase, b) in COPIED:
                    last.then_inc(d_y, 1)
                    dve.wait_ge(d_y, COPIED.index((phase, b)) + 1)
                else:
                    last.then_inc(d_acc, 1)
                    dve.wait_ge(d_acc, SUMS.index((phase, b)) + 1)
                rows = x[:, b * TPB:(b + 1) * TPB, :]
                dve.tensor_tensor(rows, rows, y[:, :, :], ALU.add).then_inc(d_x, 1)

            def spread_of_x(phase, b):
                dve.wait_ge(d_x, NORMS.index((phase, b)) + 1)
                spread_of(y_event(phase, b) + 1, row_tiles(x, b))

            def norm(phase, b):
                rstd_of(y_event(phase, b) + 1)
                normalised(row_tiles(nrm, b), row_tiles(x, b)).then_inc(d_nrm, 1)

            def attention_sums(b):
                dve.wait_ge(t_op, 2 * HEADS * (b + 1))
                dve.wait_ge(g_res, b + 1)
                take_sums(0, b, acc_bank, 1 / (P_SCALE * W_SCALE))

            def low_fp4(j):
                w, cols = q_piece(j)
                for c in range(NIBBLES):
                    dve.wait_ge(a_fh, NIBBLES * j + c + 1)
                    dve.scalar_tensor_tensor(out=fl[w][:, c, cols], in0=w32[j % 2][:, c, :], scalar=W_SCALE * FP4_AS_FP8,
                                             in1=fh[w][:, c, cols], op0=ALU.mult, op1=ALU.subtract).then_inc(d_fl, 1)

            def low_xT(phase, b):
                for c in range(KC):
                    dve.wait_ge(a_xTh, TURNS.index((phase, b)) * KC + c + 1)
                    dve.scalar_tensor_tensor(out=xTl[:, c, b * S:(b + 1) * S], in0=turn_bank(phase, b, c)[:, :], scalar=X_SCALE,
                                             in1=xTh[:, c, b * S:(b + 1) * S],
                                             op0=ALU.mult, op1=ALU.subtract).then_inc(d_xTl, 1)

            def lut_spread():
                dve.wait_ge(s_lut, 16)
                dve.wait_ge(g_twice, 1)
                for h in range(2):
                    rows = slice(h * HALF, (h + 1) * HALF)
                    last = dve.tensor_scalar(lut_own[rows, :], lut_row[rows, h:LUT:2], W_SCALE, None, ALU.mult)
                last.then_inc(d_lut, 1)
                dve.wait_ge(d_lut, 1)
                dve.tensor_copy(lut_h[:, :], lut_own[:, :]).then_inc(d_lut, 1)
                dve.wait_ge(d_lut, 2)
                dve.tensor_tensor(lut_l[:, :], lut_own[:, :], lut_h[:, :], ALU.subtract).then_inc(d_lut, 1)
                dve.wait_ge(d_lut, 3)
                for e in range(LUT // 2):
                    dve.tensor_scalar(spread[:, e, 0:HALF], twice[:, :], lut_h[:, e:e + 1], None, ALU.mult)
                    last = dve.tensor_scalar(spread[:, e, HALF:P], twice[:, :], lut_l[:, e:e + 1], None, ALU.mult)
                last.then_inc(d_lut, 1)

            def entries_hit(s):
                n = CHUNKS[s // 2][1]
                dve.wait_ge(s_idx[s % 4], 32 * (s // 4 + 1))
                if s >= 2:
                    dve.wait_ge(d_hot, s - 1)
                dve.tensor_copy(idx16[:, s % 2, 0:n], idx[:, s % 4, 0:n]).then_inc(d_idx16, 1)
                dve.wait_ge(d_idx16, s + 1)
                if s >= 2:
                    dve.wait_ge(t_lut, s - 1)
                for e in range(LUT // 2):
                    last = dve.tensor_scalar(hot[s % 2][e][:, 0:n], idx16[:, s % 2, 0:n], entry[:, e:e + 1], None, ALU.is_equal)
                last.then_inc(d_hot, 1)

            def product_of(n, rows=P):
                dve.wait_ge(a_gelu, n + 1)
                dve.wait_ge(t_up, n + 1)
                if n >= 2:
                    dve.wait_ge(g_il, n - 1)
                dve.scalar_tensor_tensor(out=inter[0:rows, n % 2, :], in0=U_bank[n % 2][0:rows, :],
                                         scalar=1 / (X_SCALE * W_SCALE), in1=gel[0:rows, n % 2, :],
                                         op0=ALU.mult, op1=ALU.mult).then_inc(d_inter, 1)

            def negatives(n):
                for w in range(2):
                    dve.wait_ge(a_pos, 2 * n + w + 1)
                    dve.tensor_scalar(neg[n][:, w, :], qkv_bank(n, w)[:, :], 0.0, None, ALU.min).then_inc(d_neg, 1)

            def denominator(n):
                dve.wait_ge(g_phi, 2 * n + 2)
                dve.tensor_tensor_scan(k_sum, ones, phi[n][:, 1, :], 0.0, ALU.mult, ALU.add).then_inc(d_den, 1)
                dve.wait_ge(d_den, 4 * n + 1)
                if n:
                    dve.wait_ge(d_att, n)
                dve.tensor_tensor(den, phi[n][:, 0, :], k_sum, ALU.mult).then_inc(d_den, 1)
                dve.wait_ge(d_den, 4 * n + 2)
                dve.tensor_scalar(den, den, CUM_EPS, None, ALU.add).then_inc(d_den, 1)
                dve.wait_ge(d_den, 4 * n + 3)
                dve.reciprocal(den, den).then_inc(d_den, 1)

            def weighted(n):
                dve.wait_ge(t_qkv, 3 * n + 3)
                dve.wait_ge(g_phi, 2 * n + 2)
                dve.scalar_tensor_tensor(out=kv, in0=qkv_bank(n, 2)[:, :], scalar=ATT_SCALE / (X_SCALE * W_SCALE),
                                         in1=phi[n][:, 1, :], op0=ALU.mult, op1=ALU.mult).then_inc(d_kv, 1)
                dve.wait_ge(d_kv, n + 1)
                if n:
                    dve.wait_ge(g_num, n)
                dve.tensor_tensor_scan(kv_sum, ones, kv, 0.0, ALU.mult, ALU.add).then_inc(d_cum, 1)

            def attend(n):
                dve.wait_ge(d_den, 4 * n + 4)
                dve.wait_ge(g_num, n + 1)
                if n:
                    dve.wait_ge(g_attl, n)
                dve.tensor_tensor(att, num, den, ALU.mult).then_inc(d_att, 1)

            def after(n):
                if n == UNITS:
                    unpacked(1)
                    signed(1)
                if n == UNITS + 1:
                    low_fp4(0)
                    low_xT(1, 0)
                    low_fp4(1)
                    unpacked(2)
                    signed(2)
                if n == UNITS + 2:
                    attention_sums(1)
                    spread_of(y_event(0, 1), block_out(0, 1))

            pipeline(dve, step, after)

            for m in range(M_TILES):
                product_of(m)
                if m == 0:
                    low_fp4(2)
                if m == 3:
                    add(0, 1)
                if m == 7:
                    spread_of_x(0, 1)
                if m == 11:
                    norm(0, 1)
                if unpack_beside(m):
                    unpacked(unpack_beside(m))
                    signed(unpack_beside(m))
                if m and unpack_beside(m - 1):
                    low_fp4(unpack_beside(m - 1))
                if m == 12:
                    lut_spread()
                    dve.memset(ones, 1.0)
                if m == 13:
                    low_xT(1, 1)
                if m >= M_TILES - 2:
                    entries_hit(m - (M_TILES - 2))
            for m in range(M_TILES):
                product_of(M_TILES + m)
                if m == 8:
                    weighted(1)
                for s in lookups_beside(m + 1):
                    entries_hit(s)
                if m == 0:
                    dve.wait_ge(t_down, M_TILES)
                    spread_of(y_event(1, 0), block_out(1, 0))
                    add(1, 0)
                    spread_of_x(1, 0)
                if m == 1:
                    norm(1, 0)
                if m == 4:
                    low_xT(2, 0)
                if m == 5:
                    negatives(0)
                if m == 6:
                    weighted(0)
                    denominator(0)
                    attend(0)
                if m == 7:
                    negatives(1)
                if m == 8:
                    denominator(1)
                    attend(1)
                if m == 11:
                    dve.wait_ge(t_out1, 1)
                    take_sums(2, 0, side_bank, ATT1_SCALE)
                    spread_of(y_event(2, 0), block_out(2, 0))
                if m == 12:
                    add(2, 0)
                    spread_of_x(2, 0)
                if m == 13:
                    norm(2, 0)
                if m == 15:
                    low_xT(3, 0)
            dve.wait_ge(t_down, B * M_TILES)
            spread_of(y_event(1, 1), block_out(1, 1))
            for m in range(I_TILES):
                if m == 2:
                    low_xT(2, 1)
                if m == 5:
                    denominator(FT + 1)
                    attend(FT + 1)
                product_of(B * M_TILES + m, i_rows(m))
                if m == 0:
                    add(1, 1)
                    spread_of_x(1, 1)
                    norm(1, 1)
                if m == 2:
                    negatives(FT)
                if m == 3:
                    weighted(FT)
                    negatives(FT + 1)
                    denominator(FT)
                    attend(FT)
                if m == 4:
                    weighted(FT + 1)
            dve.wait_ge(t_out1, B)
            spread_of(y_event(2, 1), block_out(2, 1))
            add(2, 1)
            spread_of_x(2, 1)
            norm(2, 1)
            dve.wait_ge(t_down, B * M_TILES + I_TILES)
            take_sums(3, 0, acc_bank, FFN_SCALE)
            low_xT(3, 1)
            for m in range(I_TILES):
                product_of(B * M_TILES + I_TILES + m, i_rows(m))
                if m == 0:
                    spread_of(y_event(3, 0), block_out(3, 0))
                if m == 1:
                    add(3, 0)
            dve.wait_ge(t_down, B * M_TILES + B * I_TILES)
            spread_of(y_event(3, 1), block_out(3, 1))
            add(3, 1)

        @block.tensor
        def _(pe):
            def product(dst, lhs, rhs, start, stop, skip=False):
                terms = ((lhs[0], rhs[0]), (lhs[0], rhs[1]), (lhs[1], rhs[0]))
                for i, (l, r) in enumerate(terms):
                    last = pe.matmul(dst, l, r, start=start and i == 0, stop=stop and i == 2, skip_group_check=skip)
                return last

            pe.wait_ge(g_ident, 3)

            def turn_norm0(b):
                pe.wait_ge(d_nrm, b + 1)
                for c in range(KC):
                    for t in range(TPB):
                        last = pe.transpose(T_bank[c][:, t * P:(t + 1) * P], nrm[:, b * TPB + t, c * P:(c + 1) * P],
                                            identf[:, :])
                    last.then_inc(t_xT, 1)

            def prepare(k):
                if k:
                    pe.wait_ge(g_wl, FIRST_W + len(sum(POOL_W[:k], ())))
                if len(sum(DVE_W[:k], ())):
                    pe.wait_ge(d_wl, len(sum(DVE_W[:k], ())))
                if k == 0:
                    keep_warm(4)
                    turn_norm0(1)
                    pe.wait_ge(d_xT, B * KC)
                if k == PEELED:
                    pe.wait_ge(d_xTl, B * KC)

            def keep_warm(n):
                with pe.Fori(0, n):
                    for _ in range(4):
                        pe.matmul(S_bank[1][:, :], identb[:, :], zerob[:, :], start=True, stop=True)

            keep_warm(7)
            turn_norm0(0)
            keep_warm(2)
            pe.wait_ge(d_xTl, KC)
            pe.wait_ge(g_wl, QK_W)

            def step(cur, nxt, prev, prev2, prev3):
                def scores(q):
                    b, h, u, p = cur
                    if q == 0:
                        pe.wait_ge(a_qkh, 2 * u + 2)
                        pe.wait_ge(g_qkl, 2 * u + 2)
                    if q >= 2 or not first(u):
                        pe.wait_ge(a_exp, 4 * u + (q - 1))
                    n = (q + 1) * P
                    qs = [a[:, p, 0, q * P:(q + 1) * P] for a in (qkh, qkl)]
                    ks = [a[:, p, 1, 0:n] for a in (qkh, qkl)]
                    product(S_bank[q % 2][:, 0:n], qs, ks, True, False)
                    pe.matmul(S_bank[q % 2][:, q * P:n], identb[:, :], maskb[:, :], start=False, stop=True).then_inc(t_S, 1)

                def project(w):
                    b, h, u, p = nxt
                    if w:
                        pe.wait_ge(a_qk, 2 * u + 1)
                    elif not first(u):
                        pe.wait_ge(a_qk, 2 * u)
                    for c in range(KC):
                        ws = [a[w][:, bass.ds(h * DK + c * HD, DK)] for a in (wh, wl)]
                        xs = [a[:, c, b * S:(b + 1) * S] for a in (xTh, xTl)]
                        last = product(proj_bank[:, :], ws, xs, c == 0, c == KC - 1)
                    last.then_inc(t_qk, 1)

                def project_v():
                    b, h, u, p = prev
                    if not first(u):
                        pe.wait_ge(d_ol, u)
                    for t in range(TPB):
                        for c in range(KC):
                            xs = [a[:, c, b * S + t * P:b * S + (t + 1) * P] for a in (xTh, xTl)]
                            ws = [a[2][:, bass.ds(h * DK + c * HD, DK)] for a in (wh, wl)]
                            last = product(o_bank[:, t * P:(t + 1) * P], xs, ws, c == 0, c == KC - 1)
                    last.then_inc(t_v, 1)

                def turn(q):
                    b, h, u, p = prev
                    pe.wait_ge(d_prob, 4 * u + (q + 1))
                    if q >= 2 or not first(u):
                        pe.wait_ge(d_Tl, 4 * u + (q - 1))
                    for k in range(q + 1):
                        last = pe.transpose(T_bank[q % 2][:, k * P:(k + 1) * P], prob[:, p, q, k * P:(k + 1) * P],
                                            identf[:, :])
                    last.then_inc(t_T, 1)

                def weigh():
                    b, h, u, p = prev2
                    pe.wait_ge(d_Tl, 4 * u + 4)
                    pe.wait_ge(d_vl, u + 1)
                    for k in range(TPB):
                        vs = [a[:, k * P:(k + 1) * P] for a in (vh, vl)]
                        ps = [a[:, k, k * P:S] for a in (pTh, pTl)]
                        last = product(o_bank[:, k * P:S], vs, ps, k == 0, k == TPB - 1)
                    last.then_inc(t_pv, 1)

                def out_project(tiles):
                    b, h, u, p = prev3
                    pe.wait_ge(d_ol, u + 1)
                    for t in tiles:
                        os_ = [a[:, p, t * P:(t + 1) * P] for a in (oh, ol)]
                        ws = [a[3][:, bass.ds(h * D, D)] for a in (wh, wl)]
                        last = product(acc_bank[t // 2][:, t % 2 * D:t % 2 * D + D], os_, ws, False, False, skip=True)
                    last.then_inc(t_op, 1)

                if nxt:
                    project(0)
                if straight(prev3, HEADS):
                    pe.wait_ge(d_acc, 1)
                    open_sums()
                if prev3:
                    out_project(range(2))
                if cur:
                    scores(0)
                    scores(1)
                if nxt:
                    project(1)
                if prev2:
                    weigh()
                if prev:
                    turn(0)
                    turn(1)
                if cur:
                    scores(2)
                if prev3:
                    out_project(range(2, TPB))
                if cur:
                    scores(3)
                if prev:
                    turn(2)
                    project_v()
                    turn(3)
                if not cur and not prev and nxt:
                    prepare(0)
                if preparation(cur) is not None:
                    prepare(preparation(cur))

            def open_sums():
                for a in acc_bank:
                    pe.matmul(a[:, :], identb[:, :], zerob[:, :], start=True, stop=False, skip_group_check=True)

            def turn_norm(phase, b, cols):
                pe.wait_ge(d_nrm, B + NORMS.index((phase - 1, b)) + 1)
                k = TURNS.index((phase, b))
                for c in range(KC):
                    if k > B + 1 or (k == B + 1 and c == 0):
                        pe.wait_ge(d_xTl, (k - 1) * KC + c + 1)
                    for t in range(TPB):
                        last = pe.transpose(turn_bank(phase, b, c)[:, t * P:(t + 1) * P], nrm[:, b * TPB + t, cols(c)], identf[:, :])
                    last.then_inc(t_xT, 1)

            def x_parts(b, c):
                return [a[:, c, b * S:(b + 1) * S] for a in (xTh, xTl)]

            def even_odd(c):
                return slice(c, D, NIBBLES)

            def halves(c):
                return slice(c * P, (c + 1) * P)

            def look_up(s):
                pe.wait_ge(d_hot, s + 1)
                pe.wait_ge(d_lut, 4)
                if s >= 2:
                    pe.wait_ge(a_w2, s - 1)
                if s in (8, 9):
                    pe.wait_ge(d_kv, FT)
                    pe.wait_ge(a_expo, 2 * FT)
                if s in (12, 13):
                    pe.wait_ge(d_acc, SUMS.index((2, 0)) + 1)
                n = CHUNKS[s // 2][1]
                for e in range(LUT // 2):
                    last = pe.matmul(side_bank[1 - s % 2][:, 0:n], spread[:, e, :], hot[s % 2][e][:, 0:n],
                                     start=e == 0, stop=e == LUT // 2 - 1)
                last.then_inc(t_lut, 1)

            def project1(b, i):
                f, w = i // 3, i % 3
                if i < 2:
                    pe.wait_ge(d_xTl, (TURNS.index((2, b)) + 1) * KC)
                else:
                    n, before = b * FT + (i - 2) // 3, (i - 2) % 3
                    if before == 2:
                        pe.wait_ge(d_kv, n + 1)
                    else:
                        pe.wait_ge(a_expo, 2 * n + before + 1)
                o = (w * FT + f) * P
                for c in range(KC):
                    last = product(side_bank[i % 2][:, :], [a[:, c, o:o + P] for a in (w1h, w1l)], x_parts(b, c),
                                   c == 0, c == KC - 1)
                last.then_inc(t_qkv, 1)

            def out_project1(b):
                pe.wait_ge(g_attl, FT * (b + 1))
                for t in range(TPB):
                    for f in range(FT):
                        parts = [a[f][:, t * P:(t + 1) * P] for a in (atth, attl)]
                        ws = [a[:, f, 3 * D:4 * D] for a in (w1h, w1l)]
                        last = product(side_bank[t // 2][:, t % 2 * D:t % 2 * D + D], parts, ws, f == 0, f == FT - 1)
                last.then_inc(t_out1, 1)

            def gate_up(n, m, b, weights, rows, beside):
                r = rows(m)
                if n >= 2:
                    pe.wait_ge(a_gelu, n - 1)
                for c in range(KC):
                    last = product(G_bank[n % 2][0:r, :], weights(0, m, c), x_parts(b, c), c == 0, c == KC - 1)
                last.then_inc(t_gate, 1)
                beside(2 * m)
                if n >= 2:
                    pe.wait_ge(d_inter, n - 1)
                for c in range(KC):
                    last = product(U_bank[n % 2][0:r, :], weights(1, m, c), x_parts(b, c), c == 0, c == KC - 1)
                last.then_inc(t_up, 1)
                beside(2 * m + 1)

            def down(n, m, before, weights, rows):
                r = rows(m)
                if m == 0:
                    pe.wait_ge(d_acc, SUMS.index(before) + 1)
                    open_sums()
                pe.wait_ge(g_il, n + 1)
                ws = weights(2, m, 0)
                for t in range(TPB):
                    hs = [a[n % 2][0:r, t * P:(t + 1) * P] for a in (ih, il)]
                    last = product(row_tile(t), hs, ws, False, False, skip=True)
                last.then_inc(t_down, 1)

            def row_tile(t):
                return acc_bank[t // 2][:, t % 2 * D:t % 2 * D + D]

            def fp4_weights(b):
                def weights(w, m, c):
                    if b == 0 and m % 4 == 0 and c == 0:
                        pe.wait_ge(d_fl, NIBBLES * (m // 4 * 3 + w + 1))
                    if w < 2:
                        return [f[w][:, c, m * P:(m + 1) * P] for f in (fh, fl)]
                    return [f[2][:, m % NIBBLES, m // NIBBLES * D:(m // NIBBLES + 1) * D] for f in (fh, fl)]
                return weights

            def table_weights(w, m, c):
                if w < 2:
                    o = (c * 2 + w) * INTER + m * P
                    return [a[:, o:o + i_rows(m)] for a in (wh[3], wl[3])]
                return [a[0:i_rows(m), m * D:(m + 1) * D] for a in (w2dh, w2dl)]

            def beside_first(k):
                if k == 26:
                    turn_norm(1, 1, even_odd)

            def beside_second(k):
                if k == 9:
                    pe.wait_ge(a_w2, 8)
                    turn_norm(2, 0, halves)
                if k in (10, 11, 13, 14, 15, 17):
                    project1(0, (10, 11, 13, 14, 15, 17).index(k))
                if k == 23:
                    pe.wait_ge(a_w2, 12)
                    out_project1(0)
                if k < 2 * M_TILES and lookups_beside(k // 2):
                    look_up(lookups_beside(k // 2)[k % 2])
                if k == 2 * M_TILES - 1:
                    pe.wait_ge(a_w2, LOOKUPS)
                    turn_norm(3, 0, halves)

            def beside_third(k):
                if k == 4:
                    turn_norm(2, 1, halves)
                for i, slot in enumerate((5, 5, 7, 7, 7, 9)):
                    if k == slot:
                        project1(1, i)

            def after(n):
                if n == UNITS:
                    pe.wait_ge(a_qk, 2 * UNITS)
                    pe.wait_ge(a_exp, TPB * UNITS)
                    turn_norm(1, 0, even_odd)

            open_sums()
            pipeline(pe, step, after)

            pe.wait_ge(d_ol, UNITS)
            pe.wait_ge(d_xTl, (TURNS.index((1, 0)) + 1) * KC)
            run1, run2, run3, run4 = 0, M_TILES, B * M_TILES, B * M_TILES + I_TILES
            all_rows = lambda m: P
            for m in range(M_TILES):
                gate_up(run1 + m, m, 0, fp4_weights(0), all_rows, beside_first)
                if m:
                    down(run1 + m - 1, m - 1, (0, 1), fp4_weights(0), all_rows)
            pe.wait_ge(d_xTl, (TURNS.index((1, 1)) + 1) * KC)
            pe.wait_ge(g_wl, len(ALL_POOL_W))
            for m in range(M_TILES):
                gate_up(run2 + m, m, 1, fp4_weights(1), all_rows, beside_second)
                if m:
                    down(run2 + m - 1, m - 1, (1, 0), fp4_weights(1), all_rows)
                else:
                    down(run2 - 1, M_TILES - 1, None, fp4_weights(0), all_rows)
            pe.wait_ge(d_xTl, (TURNS.index((3, 0)) + 1) * KC)
            for m in range(I_TILES):
                gate_up(run3 + m, m, 0, table_weights, i_rows, beside_third)
                if m:
                    down(run3 + m - 1, m - 1, (1, 1), table_weights, i_rows)
                else:
                    down(run3 - 1, M_TILES - 1, None, fp4_weights(1), all_rows)
            out_project1(1)
            down(run4 - 1, I_TILES - 1, None, table_weights, i_rows)
            pe.wait_ge(d_acc, SUMS.index((2, 1)) + 1)
            turn_norm(3, 1, halves)
            pe.wait_ge(d_xTl, (TURNS.index((3, 1)) + 1) * KC)
            for m in range(I_TILES):
                gate_up(run4 + m, m, 1, table_weights, i_rows, lambda k: None)
                if m:
                    down(run4 + m - 1, m - 1, (3, 0), table_weights, i_rows)
            down(run4 + I_TILES - 1, I_TILES - 1, None, table_weights, i_rows)


def kernel(**inputs):
    import numpy as np
    import concourse.bacc as bacc
    from concourse.bass_utils import run_bass_kernel_spmd

    a = {k: np.asarray(v) for k, v in inputs.items()}
    f32 = np.float32
    theta = f32(1.0) / np.power(f32(10000.0), np.arange(0, DK, 2, dtype=f32) / f32(DK))
    angle = (np.arange(S, dtype=np.float32)[None, :] * np.concatenate([theta, theta])[:, None]).astype(np.float64)
    turned = np.where(np.arange(DK)[:, None] < DK // 2, 1.0, -1.0) * np.sin(angle)
    scale = 1.0 / np.sqrt(DK)
    ropes = np.stack([np.cos(angle) * scale, turned * scale, np.cos(angle), turned]).astype(np.float32)

    def by_hidden(w):
        rows = w.shape[0]
        return w.reshape(rows, MLP // (NIBBLES * P), P, NIBBLES).transpose(0, 1, 3, 2).reshape(rows, MLP)

    def by_row(w, rows):
        return w.reshape(-1, rows, w.shape[1]).transpose(1, 0, 2).reshape(rows, -1)

    gate_up = np.concatenate([a["L1_ffn_gate_idx"].T, a["L1_ffn_up_idx"].T], axis=1)
    down = np.concatenate([a["L1_ffn_down_idx"].T, np.zeros((I_TILES * P - INTER, D), a["L1_ffn_down_idx"].dtype)])
    arrays = {
        "x": a["L0_attn_h"],
        "wqT": a["L0_attn_wq"].T, "wkT": a["L0_attn_wk"].T, "wvT": a["L0_attn_wv"].T, "woT": a["L0_attn_wo"].T,
        "bqT": a["L0_attn_bq"].reshape(HEADS, DK).T, "bkT": a["L0_attn_bk"].reshape(HEADS, DK).T,
        "bvT": a["L0_attn_bv"].reshape(HEADS, DK).T, "bo": a["L0_attn_bo"],
        "gT": a["L0_attn_ln_g"].reshape(KC, P).T, "bT": a["L0_attn_ln_b"].reshape(KC, P).T,
        "ropes": ropes,
        "w1T": np.concatenate([a["L1_attn_W_qkv"].T, a["L1_attn_W_out"].T], axis=1),
        "packed": np.stack([by_hidden(a["L0_ffn_gate_W_packed"].T), by_hidden(a["L0_ffn_up_W_packed"].T),
                            by_row(a["L0_ffn_down_W_packed"].T, P)]),
        "scales": np.stack([by_hidden(a["L0_ffn_gate_scales"].T), by_hidden(a["L0_ffn_up_scales"].T),
                            by_row(a["L0_ffn_down_scales"].T, P // Q_ROWS)]),
        "codes": np.concatenate([by_row(gate_up, P), by_row(down, P)], axis=1),
        "lut": a["L1_ffn_lut"],
    }
    arrays = {f"in_{k}": np.ascontiguousarray(v) for k, v in arrays.items()}
    nc = bacc.Bacc("TRN2", target_bir_lowering=False, num_devices=1)
    args = [nc.dram_tensor(k, v.shape, mybir.dt.from_np(v.dtype), kind="ExternalInput").ap() for k, v in arrays.items()]
    args.append(nc.dram_tensor("out", (B, S, D), F32, kind="ExternalOutput").ap())
    sandwich(nc, *args)
    return run_bass_kernel_spmd(nc, [arrays], core_ids=[0]).results[0]["out"]
```
